# Optimizing a Trainium2 kernel written in Bass

```python
import numpy as np
import jax
import jax.numpy as jnp

def _softmax(x, axis=-1):
    return jax.nn.softmax(x, axis=axis)

def _gelu(x):
    return jax.nn.gelu(x, approximate=True)

def _silu(x):
    return jax.nn.silu(x)

def _sigmoid(x):
    return jax.nn.sigmoid(x)

def _layernorm(x, axis=-1, eps=1e-05):
    m = jnp.mean(x, axis=axis, keepdims=True)
    v = jnp.var(x, axis=axis, keepdims=True)
    return (x - m) / jnp.sqrt(v + eps)

def _scatter_add(tgt, idx, src, axis=0):
    return tgt.at[idx].add(src)

def _segment_sum(src, seg, n):
    return jax.ops.segment_sum(src, seg, n)
kernel_name = 'mk_recurrent_d1_jaxref_r2_b87559'

def setup_inputs(seed: int=0):
    np.random.seed(seed)
    _w = jnp.asarray

    def _L0_attn_setup():
        import jax, jax.numpy as jnp
        import numpy as np
        import math
        HIDDEN = 512
        HEADS = 16
        HEAD_DIM = HIDDEN // HEADS
        NUM_FEATURES = 64
        B, N = (4, 2048)

        def _feature_map(x, rf):
            proj = jnp.einsum('bhnd,fd->bhnf', x, rf) / jnp.sqrt(jnp.float32(NUM_FEATURES))
            norm = jnp.linalg.norm(x, axis=-1, keepdims=True)
            return jnp.exp(proj - norm)
        key = jax.random.key(seed)
        ks = jax.random.split(key, 5)
        x = jax.random.normal(ks[0], (B, N, HIDDEN), dtype=jnp.float32)
        w_qkv = jax.random.normal(ks[1], (3 * HIDDEN, HIDDEN), dtype=jnp.float32) / math.sqrt(HIDDEN)
        w_out = jax.random.normal(ks[2], (HIDDEN, HIDDEN), dtype=jnp.float32) / math.sqrt(HIDDEN)
        b_out = jnp.zeros((HIDDEN,), dtype=jnp.float32)
        random_features = jax.random.normal(ks[3], (NUM_FEATURES, HEAD_DIM), dtype=jnp.float32)
        return {'x': x, 'w_qkv': w_qkv, 'w_out': w_out, 'b_out': b_out, 'random_features': random_features}
    _L0_attn_in = _L0_attn_setup()

    def _L0_ffn_setup():
        import jax, jax.numpy as jnp
        import numpy as np
        EPS = 1e-06
        LN_EPS = 1e-05

        def _absmean_core(W):
            gamma = jnp.mean(jnp.abs(W)) + EPS
            Ws = W / gamma
            Wq = jnp.sign(Ws) * jnp.minimum(jnp.round(jnp.abs(Ws)), 1.0)
            return (Wq, gamma)

        @jax.custom_vjp
        def absmean(W):
            return _absmean_core(W)[0]

        def _absmean_fwd(W):
            Wq, gamma = _absmean_core(W)
            return (Wq, gamma)

        def _absmean_bwd(gamma, g):
            return (g / gamma,)
        absmean.defvjp(_absmean_fwd, _absmean_bwd)

        def layernorm(x, w, b, eps=LN_EPS):
            mu = jnp.mean(x, axis=-1, keepdims=True)
            var = jnp.mean((x - mu) ** 2, axis=-1, keepdims=True)
            return (x - mu) * jax.lax.rsqrt(var + eps) * w + b
        key = jax.random.key(seed)
        k1, k2, k3 = jax.random.split(key, 3)
        d, h = (512, 2048)
        B, T = (8, 1024)
        return {'x': jax.random.normal(k1, (B, T, d), jnp.float32), 'W_fc': jax.random.normal(k2, (h, d), jnp.float32), 'ln_w': jnp.ones((h,), jnp.float32), 'ln_b': jnp.zeros((h,), jnp.float32), 'W_proj': jax.random.normal(k3, (d, h), jnp.float32)}
    _L0_ffn_in = _L0_ffn_setup()
    _d = {'L0_attn_x': _L0_attn_in['x'], 'L0_attn_w_qkv': _L0_attn_in['w_qkv'], 'L0_attn_w_out': _L0_attn_in['w_out'], 'L0_attn_b_out': _L0_attn_in['b_out'], 'L0_attn_random_features': _L0_attn_in['random_features'], 'L0_ffn_W_fc': _L0_ffn_in['W_fc'], 'L0_ffn_ln_w': _L0_ffn_in['ln_w'], 'L0_ffn_ln_b': _L0_ffn_in['ln_b'], 'L0_ffn_W_proj': _L0_ffn_in['W_proj']}
    _x0 = _d['L0_attn_x']
    _d['L0_attn_x'] = jax.random.normal(jax.random.fold_in(jax.random.key(seed), 1), (4, 2048, 512), dtype=_x0.dtype)
    del _x0
    return _d

def reference(L0_attn_x, L0_attn_w_qkv, L0_attn_w_out, L0_attn_b_out, L0_attn_random_features, L0_ffn_W_fc, L0_ffn_ln_w, L0_ffn_ln_b, L0_ffn_W_proj):

    def _L0_attn_ref(x, w_qkv, w_out, b_out, random_features):
        import jax, jax.numpy as jnp
        import numpy as np
        import math
        HIDDEN = 512
        HEADS = 16
        HEAD_DIM = HIDDEN // HEADS
        NUM_FEATURES = 64
        B, N = (4, 2048)

        def _feature_map(x, rf):
            proj = jnp.einsum('bhnd,fd->bhnf', x, rf) / jnp.sqrt(jnp.float32(NUM_FEATURES))
            norm = jnp.linalg.norm(x, axis=-1, keepdims=True)
            return jnp.exp(proj - norm)
        b, n, _ = x.shape
        qkv = jnp.einsum('bnh,oh->bno', x, w_qkv)
        qkv = qkv.reshape(b, n, 3, HEADS, HEAD_DIM)
        qkv = jnp.transpose(qkv, (2, 0, 3, 1, 4))
        q, k, v = (qkv[0], qkv[1], qkv[2])
        q_prime = _feature_map(q, random_features)
        k_prime = _feature_map(k, random_features)
        kv = jnp.einsum('bhnf,bhnd->bhfd', k_prime, v)
        normalizer = jnp.einsum('bhnf,bhf->bhn', q_prime, k_prime.sum(axis=2))
        out = jnp.einsum('bhnf,bhfd->bhnd', q_prime, kv)
        out = out / (normalizer[..., None] + 1e-06)
        out = jnp.transpose(out, (0, 2, 1, 3)).reshape(b, n, HIDDEN)
        return jnp.einsum('bnh,oh->bno', out, w_out) + b_out

    def _L0_ffn_ref(x, W_fc, ln_w, ln_b, W_proj):
        import jax, jax.numpy as jnp
        import numpy as np
        EPS = 1e-06
        LN_EPS = 1e-05

        def _absmean_core(W):
            gamma = jnp.mean(jnp.abs(W)) + EPS
            Ws = W / gamma
            Wq = jnp.sign(Ws) * jnp.minimum(jnp.round(jnp.abs(Ws)), 1.0)
            return (Wq, gamma)

        @jax.custom_vjp
        def absmean(W):
            return _absmean_core(W)[0]

        def _absmean_fwd(W):
            Wq, gamma = _absmean_core(W)
            return (Wq, gamma)

        def _absmean_bwd(gamma, g):
            return (g / gamma,)
        absmean.defvjp(_absmean_fwd, _absmean_bwd)

        def layernorm(x, w, b, eps=LN_EPS):
            mu = jnp.mean(x, axis=-1, keepdims=True)
            var = jnp.mean((x - mu) ** 2, axis=-1, keepdims=True)
            return (x - mu) * jax.lax.rsqrt(var + eps) * w + b
        h = jnp.einsum('btd,hd->bth', x, absmean(W_fc))
        h = jax.nn.gelu(h, approximate=False)
        h = layernorm(h, ln_w, ln_b)
        return jnp.einsum('bth,dh->btd', h, absmean(W_proj))
    x = L0_attn_x
    xn = _layernorm(x, axis=-1)
    s = _L0_attn_ref(xn, L0_attn_w_qkv, L0_attn_w_out, L0_attn_b_out, L0_attn_random_features)
    g = _silu(_L0_ffn_ref(xn, L0_ffn_W_fc, L0_ffn_ln_w, L0_ffn_ln_b, L0_ffn_W_proj))
    x = x + s * g
    return x

_drawn_inputs = setup_inputs


def setup_inputs(seed=0):
    import zlib

    import numpy as np

    out = dict(_drawn_inputs(seed))
    spreads = {'L0_attn_b_out': (0.0, 0.1), 'L0_ffn_ln_w': (1.0, 0.2), 'L0_ffn_ln_b': (0.0, 0.1)}
    factors = {}
    for name, (base, spread) in spreads.items():
        noise = np.random.default_rng([zlib.crc32(name.encode()), seed]).standard_normal(out[name].shape)
        drawn = base * np.exp(spread * noise) if base else spread * noise
        out[name] = jnp.asarray(drawn.astype(out[name].dtype))
    for name, factor in factors.items():
        out[name] = (out[name] * factor).astype(out[name].dtype)
    return out
```

```python
from contextlib import ExitStack

import numpy as np

import concourse.bass as bass
from concourse import mybir

F32 = mybir.dt.float32
F16 = mybir.dt.float16
BF16 = mybir.dt.bfloat16
I32 = mybir.dt.int32
ALU = mybir.AluOpType
ACT = mybir.ActivationFunctionType
AX = mybir.AxisListType
ABSMAX = bass.bass_isa.ReduceOp.max

P = 128
D = 512
KD = D // P
HEADS = 16
DH = D // HEADS
NF = 64
HID = 2048
NJ = HID // P
B, SEQ = 4, 2048
TOK = 512
SUB = TOK // P
TB = SEQ // TOK
PAIRS = HEADS // 2
SLOTS = 5
XS = 2 * KD * TOK
LN_EPS = 1e-5
VC = 65
GAMMA_EPS = 1e-6
DEN_EPS = 1e-6

X_UP = 2.0 ** 8
W_UP = 2.0 ** 8
QK_DOWN = 2.0 ** -11
SQ_DOWN = 2.0 ** -13
SQ_LIFT = 2.0 ** 12
G_UP = 2.0 ** 5
SQSUM_DOWN = 2.0 ** -7


def setup_constants():
    ident = np.eye(P, dtype=np.float32)
    sel = np.zeros((P, PAIRS * P), np.float32)
    for part in range(2):
        for h in range(HEADS):
            sel[part * HEADS + h, h * NF:(h + 1) * NF] = 1.0
    heads = np.zeros((P, 2 * KD), np.float32)
    for p in range(P):
        heads[p, p // DH] = 1.0
        heads[p, KD + p // DH] = 1.0 / SQ_LIFT
    pick = np.zeros((6, 2 * P), np.float32)
    pick[0:3, 0:P] = 1.0
    pick[3:6, P:] = 1.0
    return {"c_ident": ident, "c_sel": sel, "c_heads": heads, "c_pick": pick}


def build_program(nc, x, w_qkv, w_out, b_out, rf, w_fc, ln_w, ln_b, w_proj, c_ident, c_sel, c_heads, c_pick, out):
    ds = bass.ds
    x_v = x.rearrange("b (t s p) d -> (b t) p s d", s=SUB, p=P)
    out_v = out.rearrange("b (t s p) d -> (b t) p s d", s=SUB, p=P)

    with ExitStack() as ctx:
        def sb(name, shape, dt):
            return ctx.enter_context(nc.sbuf_tensor(name, shape, dt))

        def sem(name):
            return ctx.enter_context(nc.semaphore(name))

        xT = sb("xT", [P, SLOTS * XS], F16)
        wqkv = sb("wqkv", [P, 2, KD, 3 * D], F16)
        wo = sb("wo", [P, 2, KD, D], F16)
        wfc = sb("wfc", [P, KD, HID], BF16)
        wpj = sb("wpj", [P, NJ, D], BF16)
        S = sb("S", [P, TB * SUB * D], F32)
        A_bc = sb("A_bc", [P, D], F32)
        B_bc = sb("B_bc", [P, D], F32)
        bo_h = sb("bo_h", [P, D], F32)
        rfb = sb("rfb", [P, 2, 4 * NF], F16)
        nsel = sb("nsel", [P, PAIRS, P], BF16)
        heads16 = sb("heads16", [P, 2 * KD], F16)
        ident16 = sb("ident16", [P, P], F16)
        ident32 = sb("ident32", [P, P], F32)
        ones16 = sb("ones16", [P, 2], F16)
        wn = sb("wn", [P, NJ], F32)
        sc = sb("sc", [P, 16], F32)
        S_W, S_O, S_RF, S_E, S_NK, S_NS, S_CO, S_CR = range(8)
        col = lambda i: sc[:, i:i + 1]

        ARENA = 37376
        arena = sb("arena", [P, ARENA // 4], F32)

        def at(off, n, dt=F32):
            size = 4 if dt in (F32, I32) else 2
            v = arena[:, off // 4:(off + n * size) // 4]
            return v if dt == F32 else v.bitcast(dt)

        R = 0
        kp = at(R, 2 * 2 * D * 1).rearrange("p (a n) -> p a n", a=2)
        vv = at(R + 8192, SUB * PAIRS * VC).rearrange("p (s h c) -> p s h c", s=SUB, c=VC)
        qp = at(R, 2 * TOK).rearrange("p (a n) -> p a n", a=2)
        dn = at(R + 4096, 2 * TOK).rearrange("p (a n) -> p a n", a=2)
        dT = at(R + 8192, TOK)
        at32 = at(R + 10240, 2 * TOK).rearrange("p (a n) -> p a n", a=2)
        rT = at(R + 14336, SUB * 4)
        gh = at(R + 8192, 2 * TOK, F16).rearrange("p (a n) -> p a n", a=2)
        gl = at(R + 10240, 2 * TOK, F16).rearrange("p (a n) -> p a n", a=2)
        KVQ = 16640
        qkT = at(KVQ, 2 * KD * TOK, F16).rearrange("p (a g n) -> p a g n", a=2, g=KD)
        sqL = at(KVQ + 8192, 2 * TOK).rearrange("p (a n) -> p a n", a=2)
        sqh = at(KVQ + 12288, KD * TOK, F16).rearrange("p (g n) -> p g n", g=KD)
        sql = at(KVQ + 16384, KD * TOK, F16).rearrange("p (g n) -> p g n", g=KD)
        gbuf = at(KVQ, 2 * TOK).rearrange("p (a n) -> p a n", a=2)
        accg = at(KVQ + 4096, TOK)
        accs = at(KVQ + 6144, TOK)
        gsq = sqL
        accp = sqh
        stage_qkv = at(0, KD * 3 * D).rearrange("p (k n) -> p k n", k=KD)
        stage_wo = at(24576, KD * D).rearrange("p (k n) -> p k n", k=KD)
        neg_pj = at(0, NJ * D, BF16).rearrange("p (j n) -> p j n", j=NJ)
        stage_fc = S[:, :].rearrange("p (k n) -> p k n", k=KD)
        stage_pj = xT[:, XS:].bitcast(F32).rearrange("p (j n) -> p j n", j=NJ)
        neg_fc = wpj[:, :, :].rearrange("p j n -> p (j n)").rearrange("p (k n) -> p k n", k=KD)

        xat = sb("xat", [P, SUB, D], F32)
        attT = xat[:, :, :].bitcast(F16).rearrange("p (a b) n -> p a (b n)", a=2).rearrange(
            "p a (g n) -> p a g n", g=KD)
        yb = xat
        xhl = sb("xhl", [P, 2, 2, D], F16)
        kvs = sb("kvs", [P, PAIRS * P], F32)
        th = kvs[:, 0:D]
        kvb = sb("kvb", [P, PAIRS, P], F32)
        xres = kvb[:, :, :].rearrange("p a b -> p (a b)").rearrange("p (a n) -> p a n", a=2)
        nrm = sb("nrm", [P, SUB, P], F16)
        nrmT = sb("nrmT", [P, TOK], F16)
        ssb = sb("ssb", [P, SUB * HEADS], F32)
        rsb = sb("rsb", [P, SUB * HEADS], F32)
        nk = sb("nk", [P, SUB * HEADS], F32)
        rt_y = sb("rt_y", [P, SUB * HEADS], F32)
        rt_t = sb("rt_t", [P, SUB * HEADS], F32)
        mhalf = sb("mhalf", [P, SUB], F32)
        bst = sb("bst", [P, SUB, 6], F32)
        mv = sb("mv", [P, SUB, 2], F32)
        ve = sb("ve", [P, SUB], F32)
        rstd = sb("rstd", [P, SUB], F32)
        xsc = sb("xsc", [P, SUB], F32)
        xnb = sb("xnb", [P, SUB], F32)
        nm = sb("nm", [P, SUB], F32)
        e2 = sb("e2", [P, SUB], F32)
        mm = sb("mm", [P, SUB], F32)
        fv = sb("fv", [P, SUB], F32)
        frs = sb("frs", [P, SUB], F32)
        fr = sb("fr", [P, SUB], F32)
        mx = sb("mx", [P, 4], F32)
        gm = sb("gm", [P, 4], F32)
        pw = sb("pw", [P, 4], F32)
        ip = sb("ip", [P, 4], F32)
        gpart = xhl[:, 1, 0, 0:4 * NJ].bitcast(F32).rearrange("p (a n) -> p a n", a=2)
        gsum = sb("gsum", [P, 2], F32)
        thr = sb("thr", [P, 2], F32)
        nthr = sb("nthr", [P, 2], F32)
        ones32 = xhl[:, 0, 0, 0:2 * P].bitcast(F32)
        lnwb = yb[:, 0, 0:2 * NJ].rearrange("p (a j) -> p a j", a=2)
        lnr = yb[:, 0, 64:64 + 4 * NJ].rearrange("p (a j) -> p a j", a=4)
        lnp = yb[:, 0, 128:128 + 4 * NJ].bitcast(BF16)[:, 0:6 * NJ].rearrange("p (j c) -> p j c", c=6)
        rfT = yb[:, 0, 256:256 + NF]
        heads32 = yb[:, 0, 384:392]
        junk = yb[:, 1:3, :]
        ab6 = yb[0:6, 3, :]
        pick = xhl[0:6, 1, 1, :].bitcast(F32).rearrange("p (a n) -> p a n", a=2)
        sel32 = kvb

        ps = [ctx.enter_context(nc.psum_tensor(f"bank{i}", [P, 512], F32)) for i in range(8)]
        kvbank = ps[0:2]
        attbank = ps[0:2]
        small = ps[2]
        proj = ps[3:5]
        feat = ps[5:7]
        tbank = ps[7]
        down = [ps[0], ps[1], ps[3], ps[4]]
        t16 = tbank[:, :].bitcast(F16).rearrange("p (a n) -> p a n", n=P)

        ld_qkv, ld_wo, ld_fc, ld_pj = sem("ld_qkv"), sem("ld_wo"), sem("ld_fc"), sem("ld_pj")
        ld_small = sem("ld_small")
        v_set = sem("v_set")
        g_const = sem("g_const")
        v_max, g_max, v_scale = sem("v_max"), sem("g_max"), sem("v_scale")
        a_gpart, v_gsum, pe_gsum, v_thr = sem("a_gpart"), sem("v_gsum"), sem("pe_gsum"), sem("v_thr")
        a_whi, v_neg = sem("a_whi"), sem("v_neg")
        pe_ab, v_ab, pe_abc, v_abc = sem("pe_ab"), sem("v_ab"), sem("pe_abc"), sem("v_abc")
        x_in, ln_st, ln_mv, ln_ve, ln_rstd = sem("x_in"), sem("ln_st"), sem("ln_mv"), sem("ln_ve"), sem("ln_rstd")
        ln_sc, ln_xn, ln_hi, ln_lo = sem("ln_sc"), sem("ln_xn"), sem("ln_hi"), sem("ln_lo")
        pe_t, t_ev = sem("pe_t"), sem("t_ev")
        p_full, p_free = sem("p_full"), sem("p_free")
        a_hi, a_sq, g_sqh, v_sql = sem("a_hi"), sem("a_sq"), sem("g_sqh"), sem("v_sql")
        pe_ssq, v_ssb, v_rt1, v_root, v_nk = sem("pe_ssq"), sem("v_ssb"), sem("v_rt1"), sem("v_root"), sem("v_nk")
        f_full, f_free, a_kp = sem("f_full"), sem("f_free"), sem("a_kp")
        pe_kv, v_kvz, v_kva = sem("pe_kv"), sem("v_kvz"), sem("v_kva")
        v_kvb0 = sem("v_kvb0")
        v_nh, v_nl, pe_nt, v_nt = sem("v_nh"), sem("v_nl"), sem("pe_nt"), sem("v_nt")
        pe_att, a_dn, v_num = sem("pe_att"), sem("a_dn"), sem("v_num")
        v_dt, v_rt, v_rr, g_mul, g_ah, v_al = (sem("v_dt"), sem("v_rt"), sem("v_rr"), sem("g_mul"), sem("g_ah"),
                                               sem("v_al"))
        pe_fc, a_g, g_free, a_gsq = sem("pe_fc"), sem("a_g"), sem("g_free"), sem("a_gsq")
        v_gh, v_gl, v_accs, g_accg = sem("v_gh"), sem("v_gl"), sem("v_accs"), sem("g_accg")
        pe_dn, a_yb, v_aph, v_apl, pe_st = sem("pe_dn"), sem("a_yb"), sem("v_aph"), sem("v_apl"), sem("pe_st")
        v_st, v_s3, v_s4, v_s5, g_rs, v_fr = (sem("v_st"), sem("v_s3"), sem("v_s4"), sem("v_s5"), sem("g_rs"),
                                              sem("v_fr"))
        v_y1, v_y, a_th, v_u, g_us, g_o = sem("v_y1"), sem("v_y"), sem("a_th"), sem("v_u"), sem("g_us"), sem("g_o")
        xr_in, o_out = sem("xr_in"), sem("o_out")
        sp_own, pe_own, a_own, g_own, v_own = sem("sp_own"), sem("pe_own"), sem("a_own"), sem("g_own"), sem("v_own")
        block = ctx.enter_context(nc.Block())

        def settle(engine, own):
            engine.sem_inc(own, 1)

        PU, FU = 64, 66

        ROOT_STEPS = 11

        @block.sync
        def _(sp):
            sp.dma_start(stage_qkv, w_qkv.rearrange("(k p) n -> p k n", p=P)).then_inc(ld_qkv, 16)
            sp.dma_start(stage_wo, w_out.rearrange("(k p) n -> p k n", p=P)).then_inc(ld_wo, 16)
            sp.dma_start(ident32[:, :], c_ident).then_inc(ld_small, 16)
            sp.dma_start(heads32, c_heads).then_inc(ld_small, 16)
            sp.dma_start(sel32[:, :, :], c_sel.rearrange("p (a b) -> p a b", a=PAIRS)).then_inc(ld_small, 16)
            for h in range(4):
                sp.dma_start(rfT[h * DH:(h + 1) * DH, :], rf).then_inc(ld_small, 16)
            sp.dma_start(lnwb[:, 0, :], ln_w).then_inc(ld_small, 16)
            sp.dma_start(lnwb[:, 1, :], ln_b).then_inc(ld_small, 16)
            sp.dma_start(bo_h[:, :], b_out.rearrange("(a d) -> a d", a=1).partition_broadcast(P)).then_inc(ld_small, 16)
            sp.dma_start(pick, c_pick.rearrange("q (a p) -> q a p", a=2)).then_inc(ld_small, 16)
            sp.dma_start(stage_fc, w_fc.rearrange("(k p) n -> p k n", p=P)).then_inc(ld_fc, 16)
            sp.dma_start(stage_pj, w_proj.rearrange("(j p) n -> p j n", p=P)).then_inc(ld_pj, 16)
            sp.wait_ge(v_abc, 2)
            sp.dma_start(xat[:, :, :], x_v[0]).then_inc(x_in, 16)
            with sp.Fori(0, B) as b:
                with sp.Fori(0, TB) as t:
                    n = sp.snap(b * TB + t)
                    src = sp.snap((n + 1) % (B * TB))
                    sp.wait_ge(ln_lo, 4 * n + 4)
                    settle(sp, sp_own)
                    sp.wait_ge(o_out, 256 * b)
                    sp.dma_start(xat[:, :, :], x_v[ds(src, 1)].rearrange("a p s d -> p (a s) d")).then_inc(x_in, 16)
                sp.wait_ge(v_al, 16 * b + 16)
                sp.wait_ge(pe_att, 32 * b + 32 + 2)
                settle(sp, sp_own)
                with sp.Fori(0, TB) as t:
                    n = sp.snap(b * TB + t)
                    for s in range(SUB):
                        sp.wait_ge(g_o, 4 * n + s + 1)
                        settle(sp, sp_own)
                        sp.wait_ge(xr_in, 64 * n + 16 * s)
                        sp.dma_start(xres[:, s % 2, :], x_v[ds(n, 1), :, s, :].rearrange(
                            "a p d -> p (a d)")).then_inc(xr_in, 16)
                        if s:
                            sp.wait_ge(g_o, 4 * n + s + 2)
                            sp.dma_start(out_v[ds(n, 1), :, s - 1, :].rearrange("a p d -> p (a d)"),
                                         yb[:, s - 1, :]).then_inc(o_out, 16)
                    sp.wait_ge(g_o, 4 * n + 4 + 2)
                    sp.dma_start(out_v[ds(n, 1), :, SUB - 1, :].rearrange("a p d -> p (a d)"),
                                 yb[:, SUB - 1, :]).then_inc(o_out, 16)
            sp.wait_ge(o_out, 64 * B * TB)

        @block.tensor
        def _(pe):
            def mm(o, lhsT, rhs, start, stop, **kw):
                return nc.tensor.matmul(o, lhsT, rhs, start=start, stop=stop, skip_group_check=True, **kw)

            pe.wait_ge(g_const, 1)
            pe.wait_ge(v_gsum, 2)
            mm(small[:, 0:2], ones32, gsum[:, :], True, True).then_inc(pe_gsum, 1)
            pe.wait_ge(v_neg, 4)
            for j in range(NJ):
                i = mm(feat[1][0:6, :], lnp[:, j, :], wpj[:, j, :], j == 0, j == NJ - 1)
            i.then_inc(pe_ab, 1)
            pe.wait_ge(v_ab, 1)
            for h in range(2):
                mm(proj[h][:, :], pick[:, h, :], ab6, True, True).then_inc(pe_abc, 1)

            def transpose_x(m, s):
                pe.wait_ge(ln_lo, 4 * m + s + 1)
                pe.wait_ge(t_ev, 4 * m + s)
                for a in range(2):
                    for k in range(KD):
                        i = nc.tensor.transpose(t16[:, a * KD + k, :], xhl[:, s % 2, a, k * P:(k + 1) * P],
                                                ident16[:, :])
                i.then_inc(pe_t, 1)

            for s in range(SUB):
                transpose_x(0, s)

            def xmov(off, a, k):
                return xT[:, ds(off + (a * KD + k) * TOK, TOK)]

            def project_T(u, off, first, groups=range(KD)):
                for g in groups:
                    pe.wait_ge(p_free, u + g + 1)
                    o = proj[g % 2][:, :]
                    for i, (wa, xa) in enumerate(((0, 0), (0, 1), (1, 0))):
                        for k in range(KD):
                            c0 = first + g * P
                            ins = mm(o, wqkv[:, wa, k, c0:c0 + P], xmov(off, xa, k), i == 0 and k == 0,
                                     i == 2 and k == KD - 1)
                    ins.then_inc(p_full, 1)

            def project_v(u, off, s):
                pe.wait_ge(p_free, u + 4 + s + 1)
                o = proj[s % 2][:, :]
                for i, (wa, xa) in enumerate(((0, 0), (1, 0), (0, 1))):
                    for k in range(KD):
                        ins = mm(o, xT[:, ds(off + (xa * KD + k) * TOK + s * P, P)], wqkv[:, wa, k, 2 * D:3 * D],
                                 i == 0 and k == 0, i == 2 and k == KD - 1)
                ins.then_inc(p_full, 1)

            def square_sums(h4, r):
                pe.wait_ge(v_sql, h4 + 4 + 2)
                pe.wait_ge(v_ssb, r)
                for s in range(SUB):
                    for g in range(KD):
                        o = small[:, s * HEADS + g * 4:s * HEADS + g * 4 + 4]
                        mm(o, sqh[:, g, s * P:(s + 1) * P], heads16[:, 0:4], True, False)
                        ins = mm(o, sql[:, g, s * P:(s + 1) * P], heads16[:, 4:8], False, True)
                ins.then_inc(pe_ssq, 1)

            def k_features(f, s, h):
                pe.wait_ge(f_free, f + 2 * s + h + 1)
                for g2 in range(2):
                    g = 2 * h + g2
                    o = feat[h][:, g2 * 4 * NF:(g2 + 1) * 4 * NF]
                    mm(o, qkT[:, 0, g, s * P:(s + 1) * P], rfb[:, 0, :], True, False)
                    mm(o, qkT[:, 1, g, s * P:(s + 1) * P], rfb[:, 0, :], False, False)
                    ins = mm(o, qkT[:, 0, g, s * P:(s + 1) * P], rfb[:, 1, :], False, True)
                ins.then_inc(f_full, 1)

            def kv_sums(n, u, s):
                pe.wait_ge(a_kp, 8 * n + 2 * s + 2)
                pe.wait_ge(p_free, u + 4 + s + 3)
                if s == 0:
                    pe.wait_ge(v_kva, 2 * n)
                for p in range(PAIRS):
                    ins = mm(kvbank[p // 4][0:VC, (p % 4) * P:(p % 4 + 1) * P], vv[:, s, p, :],
                             kp[:, s % 2, p * P:(p + 1) * P], s == 0 and p % 4 == 0, s == SUB - 1)
                ins.then_inc(pe_kv, 1)

            def out_project(u, n, s):
                pe.wait_ge(v_al, 4 * n + 4)
                pe.wait_ge(p_free, u + s + 1)
                for i, (wa, xa) in enumerate(((0, 0), (1, 0), (0, 1))):
                    for g in range(KD):
                        ins = mm(proj[s % 2][:, :], attT[:, xa, g, s * P:(s + 1) * P], wo[:, wa, g, :],
                                 i == 0 and g == 0, i == 2 and g == KD - 1)
                ins.then_inc(p_full, 1)

            def norms_T(n, b):
                pe.wait_ge(v_nl, n + 1)
                pe.wait_ge(t_ev, 16 * b + 20)
                pe.wait_ge(v_nt, n)
                for s in range(SUB):
                    ins = nc.tensor.transpose(t16[:, s, :], nrm[:, s, :], ident16[:, :])
                ins.then_inc(pe_nt, 1)

            def q_feature(f, p):
                pe.wait_ge(f_free, f + p + 1)
                o = feat[p % 2][:, :]
                c0 = (p % 2) * P
                mm(o, rfb[:, 0, c0:c0 + P], qkT[:, 0, p // 2, :], True, False)
                mm(o, rfb[:, 0, c0:c0 + P], qkT[:, 1, p // 2, :], False, False)
                mm(o, rfb[:, 1, c0:c0 + P], qkT[:, 0, p // 2, :], False, False)

            def minus_norm(p):
                mm(feat[p % 2][:, :], nsel[:, p, :], nrmT[:, :], False, True).then_inc(f_full, 1)

            def attend(n, f, p):
                pe.wait_ge(f_free, f + p + 1 + 2)
                pe.wait_ge(v_num, 8 * n + p + 1)
                pe.wait_ge(a_dn, 8 * n + p + 1)
                mm(attbank[p % 2][:, :], kvb[:, p, :], qp[:, p % 2, :], True, True).then_inc(pe_att, 1)

            def q_tile(b, t, n, u, f, off, noff, first):
                if first:
                    project_T(u, off, 0)
                    pe.wait_ge(v_kva, 8 * b + 8)
                    for j in range(2):
                        pe.wait_ge(f_free, f - 2 + j + 1)
                        for p in range(4):
                            c0 = (4 * j + p) * P
                            ins = nc.tensor.transpose(feat[j][:, p * 66:p * 66 + VC], kvs[0:VC, c0:c0 + P],
                                                      ident32[0:VC, 0:VC])
                        ins.then_inc(f_full, 1)
                    project_T(u + 4, noff, 0, (0,))
                else:
                    project_T(u, off, 0, (2, 3))
                    out_project(u + 4, n - 1, 0)
                square_sums(32 * b + 4 * t + 16, 8 * b + t + 4)
                if not first:
                    for s in range(1, SUB):
                        out_project(u + 4, n - 1, s)
                if first:
                    pe.wait_ge(f_free, f + 2)
                q_feature(f, 0)
                q_feature(f, 1)
                norms_T(n, b)
                pe.wait_ge(v_nt, n + 1)
                minus_norm(0)
                minus_norm(1)
                un = u + 4 if first else u + 8
                for p in range(PAIRS):
                    if p == PAIRS - 2 and noff is not None and not first:
                        project_T(un, noff, 0, (0,))
                    if p == PAIRS - 1:
                        if noff is not None:
                            project_T(un, noff, 0, (1,))
                    attend(n, f, p)
                    if p + 2 < PAIRS:
                        q_feature(f, p + 2)
                        minus_norm(p + 2)

            def up(g0, off, j, i):
                pe.wait_ge(a_g, g0 + 1)
                for k in range(KD):
                    for a in range(2):
                        ins = mm(feat[i][:, :], wfc[:, k, ds(j * P, P)], xmov(off, a, k), k == 0 and a == 0,
                                 k == KD - 1 and a == 1)
                ins.then_inc(pe_fc, 1)

            def down_step(g0, n, j, i, first=False, last=False):
                pe.wait_ge(v_gl, g0 + 1 + 2)
                for s in range(SUB):
                    if first:
                        pe.wait_ge(a_yb, 4 * n - 4 + s + 1 + 4)
                    mm(down[s][:, :], gh[:, i, s * P:(s + 1) * P], wpj[:, ds(j, 1), :], first, False)
                    ins = mm(down[s][:, :], gl[:, i, s * P:(s + 1) * P], wpj[:, ds(j, 1), :], False, last)
                ins.then_inc(pe_dn, 1)

            def ffn_sums(n):
                pe.wait_ge(v_apl, 2 * n + 2)
                pe.wait_ge(v_st, 2 * n)
                for s in range(SUB):
                    for q in range(2):
                        o = small[:, 2 * s + q:2 * s + q + 1]
                        mm(o, accp[:, 2 * q, s * P:(s + 1) * P], ones16[:, 0:1], True, False)
                        ins = mm(o, accp[:, 2 * q + 1, s * P:(s + 1) * P], ones16[:, 0:1], False, True)
                ins.then_inc(pe_st, 1)

            def ffn_tile(n, off, noff, first, last):
                g0 = pe.snap(16 * n)
                for i in range(2):
                    if not first:
                        up(g0 + i + 2, off, i + 2, i)
                    down_step(g0 + i, n, i, i, first=i == 0)
                    if i == 0 and not first:
                        ffn_sums(n - 1)
                with pe.Fori(1, NJ // 2 - 1) as jj:
                    j = 2 * jj
                    for i in range(2):
                        up(g0 + j + i + 2, off, j + i + 2, i)
                        down_step(g0 + j + i, n, j + i, i)
                for i in range(2):
                    if not last:
                        up(g0 + NJ + i, noff, i, i)
                    down_step(g0 + NJ - 2 + i, n, NJ - 2 + i, i, last=i == 1)
                if last:
                    ffn_sums(n)

            with pe.Fori(0, B) as b:
                pe.wait_ge(a_yb, 16 * b + 4)
                pe.wait_ge(a_g, 64 * b + 2)
                pe.wait_ge(v_st, 8 * b)
                settle(pe, pe_own)
                with pe.Fori(0, TB) as t:
                    n = pe.snap(b * TB + t)
                    u = pe.snap(b * PU + t * 8)
                    f = pe.snap(b * FU + t * 8)
                    off = pe.snap((n % SLOTS) * XS)
                    pe.wait_ge(t_ev, 4 * n + 4)
                    project_T(u, off, D)
                    project_v(u, off, 0)
                    square_sums(32 * b + 4 * t, 8 * b + t)
                    for s in range(1, SUB):
                        project_v(u, off, s)
                    for s in range(SUB):
                        for h in range(2):
                            k_features(f, s, h)
                        transpose_x(n + 1, s)
                        if s:
                            kv_sums(n, u, s - 1)
                    kv_sums(n, u, SUB - 1)
                n0 = pe.snap(b * TB)
                q_tile(b, 0, n0, pe.snap(b * PU + 32), pe.snap(b * FU + 34), pe.snap((n0 % SLOTS) * XS),
                       pe.snap(((n0 + 1) % SLOTS) * XS), True)
                with pe.Fori(1, TB - 1) as t:
                    n = pe.snap(b * TB + t)
                    q_tile(b, t, n, pe.snap(b * PU + 28 + t * 8), pe.snap(b * FU + 34 + t * 8),
                           pe.snap((n % SLOTS) * XS), pe.snap(((n + 1) % SLOTS) * XS), False)
                n3 = pe.snap(b * TB + TB - 1)
                t = TB - 1
                q_tile(b, t, n3, pe.snap(b * PU + 28 + t * 8), pe.snap(b * FU + 34 + t * 8),
                       pe.snap((n3 % SLOTS) * XS), None, False)
                pe.wait_ge(f_free, FU * b + FU + 2)
                off0 = pe.snap((n0 % SLOTS) * XS)
                for i in range(4):
                    up(16 * n0 + i, off0, i, i % 2)
                for s in range(SUB):
                    out_project(pe.snap(b * PU + 60), n3, s)
                pe.wait_ge(p_free, PU * b + PU + 2)
                pe.wait_ge(v_num, 32 * b + 32 + 2)
                pe.wait_ge(a_dn, 32 * b + 32 + 2)
                ffn_tile(n0, off0, pe.snap(((n0 + 1) % SLOTS) * XS), True, False)
                with pe.Fori(1, TB - 1) as t:
                    n = pe.snap(b * TB + t)
                    ffn_tile(n, pe.snap((n % SLOTS) * XS), pe.snap(((n + 1) % SLOTS) * XS), False, False)
                ffn_tile_last = pe.snap((n3 % SLOTS) * XS)
                ffn_tile(n3, ffn_tile_last, None, False, True)

        @block.scalar
        def _(act):
            def A(o, i, f, **kw):
                return nc.scalar.activation(o, i, f, **kw)

            act.wait_ge(v_scale, 1)
            A(wqkv[:, 0, :, :], stage_qkv, ACT.Copy, scale=col(S_W)).then_inc(a_whi, 1)
            A(wo[:, 0, :, :], stage_wo, ACT.Copy, scale=col(S_O)).then_inc(a_whi, 1)
            for q, (stage, l) in enumerate(((stage_fc, ld_fc), (stage_pj, ld_pj))):
                act.wait_ge(l, 16)
                flat = stage.rearrange("p a n -> p (a n)")
                for c in range(NJ):
                    if NJ * q + c >= 2:
                        act.wait_ge(a_gpart, NJ * q + c - 1)
                    A(junk[:, c % 2, :], flat[:, c * D:(c + 1) * D], ACT.Abs,
                      accum_out=gpart[:, q, c:c + 1]).then_inc(a_gpart, 1)

            def normalise(m, s):
                act.wait_ge(ln_sc, 2 * m + 2)
                A(xat[:, s, :], xat[:, s, :], ACT.Identity, scale=xsc[:, s:s + 1],
                  bias=xnb[:, s:s + 1]).then_inc(ln_xn, 1)

            for s in range(SUB):
                normalise(0, s)

            def split_high(u, h4, g, fwait):
                if g == 0:
                    act.wait_ge(f_full, fwait)
                act.wait_ge(p_full, u + g + 1)
                A(qkT[:, 0, g, :], proj[g % 2][:, :], ACT.Copy, scale=QK_DOWN).then_inc(a_hi, 1)
                act.wait_ge(v_sql, h4 + g + 1)
                A(sqL[:, g % 2, :], proj[g % 2][:, :], ACT.Square, scale=SQ_DOWN).then_inc(a_sq, 1)

            def exp_k(n, f, s, h):
                act.wait_ge(f_free, f + 2 * s + h + 3)
                v = kp[:, s % 2, h * D:(h + 1) * D]
                A(v, v, ACT.Exp, scale=col(S_E)).then_inc(a_kp, 1)

            def exp_q(n, f, p):
                act.wait_ge(f_full, f + p + 1)
                act.wait_ge(pe_att, 8 * n + p + 1)
                A(qp[:, p % 2, :], feat[p % 2][:, :], ACT.Exp, scale=col(S_E)).then_inc(f_free, 1)

            def denominators(n, p):
                act.wait_ge(pe_att, 8 * n + p + 1 + 2)
                if p % 2 == 0:
                    act.wait_ge(g_mul, 4 * n + p // 2 + 1)
                h = 64 * (p % 2)
                A(dn[h:h + 64, (p // 2) % 2, :], attbank[p % 2][64:128, :], ACT.Copy,
                  bias=DEN_EPS).then_inc(a_dn, 1)

            def q_tile(b, t, n, u, f, fwait):
                h4 = 32 * b + 16 + 4 * t
                for g in range(KD):
                    split_high(u, h4, g, fwait)
                exp_q(n, f, 0)
                for p in range(PAIRS):
                    if p + 1 < PAIRS:
                        exp_q(n, f, p + 1)
                    denominators(n, p)

            def gelu_step(g0, i):
                act.wait_ge(pe_fc, g0 + 1)
                act.wait_ge(v_gl, g0 + 1)
                act.wait_ge(g_accg, g0 + 1)
                A(gbuf[:, i, :], feat[i][:, :], ACT.Gelu, scale=1.0 / X_UP).then_inc(a_g, 1)
                act.wait_ge(a_g, g0 + 3)
                act.wait_ge(v_accs, g0 + 1)
                A(gsq[:, i, :], gbuf[:, i, :], ACT.Square).then_inc(a_gsq, 1)

            def tanh_step(e):
                act.wait_ge(v_y, e + 1)
                act.wait_ge(v_u, e)
                settle(act, a_own)
                A(th, yb[:, ds(e % 4, 1), :].rearrange("p a d -> p (a d)"), ACT.Tanh, scale=0.5).then_inc(a_th, 1)

            def results(n):
                act.wait_ge(o_out, 64 * n)
                for s in range(SUB):
                    act.wait_ge(pe_dn, 16 * n + 16 + 2)
                    A(yb[:, s, :], down[s][:, :], ACT.Copy).then_inc(a_yb, 1)

            def ffn_tile(n, prev, last):
                g0 = act.snap(16 * n)
                with act.Fori(0, 2) as q:
                    for i in range(6):
                        gelu_step(g0 + 6 * q + 2 + i, i % 2)
                        if prev and i in (3, 5):
                            tanh_step(4 * n - 4 + 2 * q + i // 4)
                for i in range(2 if last else 4):
                    gelu_step(g0 + NJ - 2 + i, i % 2)
                results(n)

            with act.Fori(0, B) as b:
                with act.Fori(0, TB) as t:
                    n = act.snap(b * TB + t)
                    u = act.snap(b * PU + t * 8)
                    f = act.snap(b * FU + t * 8)
                    for g in range(KD):
                        split_high(u, 32 * b + 4 * t, g, f)
                        if g == 2:
                            normalise(n + 1, 0)
                    for s in range(1, SUB):
                        normalise(n + 1, s)
                    for s in range(SUB):
                        for h in range(2):
                            exp_k(n, f, s, h)
                n0 = act.snap(b * TB)
                q_tile(b, 0, n0, act.snap(b * PU + 32), act.snap(b * FU + 34), b * FU + 32)
                with act.Fori(1, TB) as t:
                    n = act.snap(b * TB + t)
                    f = act.snap(b * FU + 34 + t * 8)
                    q_tile(b, t, n, act.snap(b * PU + 28 + t * 8), f, f)
                for i in range(2):
                    gelu_step(16 * n0 + i, i)
                ffn_tile(n0, False, False)
                with act.Fori(1, TB - 1) as t:
                    ffn_tile(act.snap(b * TB + t), True, False)
                ffn_tile(act.snap(b * TB + TB - 1), True, True)
                with act.Fori(0, 4) as q:
                    tanh_step(16 * b + 12 + q)

        @block.gpsimd
        def _(pool):
            g = nc.gpsimd

            g.memset(mhalf[:, :], -0.5)
            g.memset(ones32, 1.0)
            g.memset(rfb[:, :, :], 0.0)
            g.memset(nrm[:, :, :], 0.0)
            g.memset(ones16[:, :], 1.0).then_inc(g_const, 1)
            pool.wait_ge(v_max, 4)
            g.partition_all_reduce(gm[:, :], mx[:, :], P, ABSMAX).then_inc(g_max, 1)

            def rsqrt_x(m):
                pool.wait_ge(ln_ve, m + 1)
                g.tensor_tensor(rstd[:, :], ve[:, :], mhalf[:, :], ALU.pow).then_inc(ln_rstd, 1)

            def split_x(m, s):
                pool.wait_ge(pe_t, 4 * m + s + 1)
                pool.wait_ge(ln_xn, 4 * m + s + 1)
                settle(pool, g_own)
                g.tensor_scalar(xhl[:, s % 2, 0, :], xat[:, s, :], 1.0, 0.0, ALU.mult, ALU.add).then_inc(ln_hi, 1)
                pool.wait_ge(ln_hi, 4 * m + s + 1)
                g.tensor_tensor(xhl[:, s % 2, 1, :], xat[:, s, :], xhl[:, s % 2, 0, :],
                                ALU.subtract).then_inc(ln_lo, 1)

            def square_high(h4, r, gg):
                pool.wait_ge(pe_ssq, r)
                pool.wait_ge(a_sq, h4 + gg + 1)
                settle(pool, g_own)
                g.tensor_scalar(sqh[:, gg, :], sqL[:, gg % 2, :], 1.0 / SQ_LIFT, 0.0, ALU.mult,
                                ALU.add).then_inc(g_sqh, 1)

            def attention_high(n, gg):
                pool.wait_ge(v_rr, 4 * n + gg + 1)
                pool.wait_ge(v_num, 8 * n + 2 * gg + 2 + 2)
                a = at32[:, gg % 2, :]
                g.tensor_tensor(a, a, dn[:, gg % 2, :], ALU.mult).then_inc(g_mul, 1)
                pool.wait_ge(g_mul, 4 * n + gg + 1 + 2)
                settle(pool, g_own)
                g.tensor_scalar(attT[:, 0, gg, :], a, 1.0, 0.0, ALU.mult, ALU.add).then_inc(g_ah, 1)

            def q_tile(b, t, n):
                h4 = 32 * b + 16 + 4 * t
                for gg in range(KD):
                    square_high(h4, 8 * b + 4 + t, gg)
                for gg in range(KD):
                    attention_high(n, gg)

            def finish(e):
                pool.wait_ge(v_u, e + 1)
                settle(pool, g_own)
                y = yb[:, ds(e % 4, 1), :].rearrange("p a d -> p (a d)")
                g.tensor_tensor(y, y, S[:, ds((e % 16) * D, D)], ALU.mult).then_inc(g_us, 1)
                pool.wait_ge(xr_in, 16 * e + 16)
                pool.wait_ge(g_us, e + 1)
                settle(pool, g_own)
                xr = xres[:, ds(e % 2, 1), :].rearrange("p a d -> p (a d)")
                g.tensor_tensor(y, y, xr, ALU.add).then_inc(g_o, 1)

            def sum_step(g0, i):
                pool.wait_ge(a_g, g0 + 3)
                pool.wait_ge(g_accg, g0 + 2)
                g.tensor_tensor(accg, accg, gbuf[:, i, :], ALU.add).then_inc(g_accg, 1)

            def first_sum(n, g0):
                pool.wait_ge(a_g, g0 + 3)
                pool.wait_ge(v_apl, 2 * n)
                settle(pool, g_own)
                g.tensor_scalar(accg, gbuf[:, 0, :], 1.0, 0.0, ALU.mult, ALU.add).then_inc(g_accg, 1)

            def ffn_root(n):
                pool.wait_ge(v_s5, n + 1)
                g.tensor_tensor(frs[:, :], fv[:, :], mhalf[:, :], ALU.pow).then_inc(g_rs, 1)

            def ffn_tile(n, prev):
                g0 = pool.snap(16 * n)
                first_sum(n, g0)
                sum_step(g0 + 1, 1)
                if prev:
                    ffn_root(n - 1)
                with pool.Fori(0, 2) as q:
                    for i in range(6):
                        sum_step(g0 + 6 * q + 2 + i, i % 2)
                        if prev and i in (3, 5):
                            finish(4 * n - 4 + 2 * q + i // 4)
                for i in range(2):
                    sum_step(g0 + NJ - 2 + i, i)

            rsqrt_x(0)
            for s in range(SUB):
                split_x(0, s)
            with pool.Fori(0, B) as b:
                with pool.Fori(0, TB) as t:
                    n = pool.snap(b * TB + t)
                    rsqrt_x(n + 1)
                    for gg in range(KD):
                        square_high(32 * b + 4 * t, 8 * b + t, gg)
                    split_x(n + 1, 0)
                    split_x(n + 1, 1)
                    split_x(n + 1, 2)
                    split_x(n + 1, 3)
                with pool.Fori(0, TB) as t:
                    q_tile(b, t, pool.snap(b * TB + t))

                ffn_tile(pool.snap(b * TB), False)
                with pool.Fori(1, TB) as t:
                    ffn_tile(pool.snap(b * TB + t), True)
                ffn_root(pool.snap(b * TB + 3))
                with pool.Fori(0, 4) as q:
                    finish(16 * b + 12 + q)

        @block.vector
        def _(dve):
            v = nc.vector
            steps = [0]

            def then(ins):
                steps[0] += 1
                ins.then_inc(v_set, 1)
                dve.wait_ge(v_set, steps[0])

            for s_, k_ in ((p_free, 2), (f_free, 2), (v_sql, 2), (pe_kv, 4), (pe_att, 2), (v_num, 2), (a_dn, 2),
                           (g_mul, 2), (a_g, 2), (v_gl, 2), (g_accg, 2), (v_accs, 2), (a_yb, 4), (pe_t, 2),
                           (pe_dn, 2), (g_o, 2)):
                dve.sem_inc(s_, k_)
            v.memset(mx[:, :], 0.0)
            dve.wait_ge(ld_small, 16 * 11)
            v.tensor_copy(ident16[:, :], ident32[:, :])
            then(v.tensor_copy(heads16[:, :], heads32))
            v.tensor_reduce(mx[:, 2:3], rfT, AX.X, ALU.max, apply_absolute_value=True).then_inc(v_max, 1)
            v.tensor_reduce(mx[:, 3:4], lnwb[:, 0, :], AX.X, ALU.max, apply_absolute_value=True).then_inc(v_max, 1)
            dve.wait_ge(ld_qkv, 16)
            v.tensor_reduce(mx[:, 0:1], stage_qkv.rearrange("p k n -> p (k n)"), AX.X, ALU.max,
                            apply_absolute_value=True).then_inc(v_max, 1)
            dve.wait_ge(ld_wo, 16)
            v.tensor_reduce(mx[:, 1:2], stage_wo.rearrange("p k n -> p (k n)"), AX.X, ALU.max,
                            apply_absolute_value=True).then_inc(v_max, 1)
            dve.wait_ge(g_max, 1)
            then(v.tensor_scalar(pw[:, :].bitcast(I32), gm[:, :].bitcast(I32), 0x7F800000, None, ALU.bitwise_and))
            then(v.tensor_scalar(pw[:, :], pw[:, :], 2.0 ** -100, None, ALU.max))
            then(v.reciprocal(ip[:, :], pw[:, :]))
            v.tensor_scalar(col(S_W), ip[:, 0:1], W_UP, None, ALU.mult)
            v.tensor_scalar(col(S_O), ip[:, 1:2], W_UP, None, ALU.mult)
            v.tensor_scalar(col(S_RF), ip[:, 2:3], W_UP, None, ALU.mult)
            v.scalar_tensor_tensor(col(S_E), pw[:, 0:1], 2.0 ** -16, pw[:, 2:3], ALU.mult, ALU.mult)
            v.tensor_scalar(col(S_NK), ip[:, 2:3], 2.0 ** 19, None, ALU.mult)
            v.tensor_scalar(col(S_NS), ip[:, 2:3], -(2.0 ** 13), None, ALU.mult)
            v.scalar_tensor_tensor(col(S_CO), pw[:, 0:1], 2.0 ** -14, pw[:, 1:2], ALU.mult, ALU.mult)
            v.tensor_scalar(col(S_CR), pw[:, 3:4], 1.0 / G_UP, None, ALU.mult)
            then(v.tensor_scalar(wn[:, :], lnwb[:, 0, :], ip[:, 3:4], G_UP, ALU.mult, ALU.mult))
            v.tensor_scalar(nsel[:, :, :], sel32[:, :, :], col(S_NS), None, ALU.mult)
            v.tensor_scalar(bo_h[:, :], bo_h[:, :], 0.5, None, ALU.mult).then_inc(v_scale, 1)
            then(v.tensor_copy(lnr[:, 0, :], wn[:, :]))
            then(v.tensor_copy(lnr[:, 1, :], lnwb[:, 1, :]))
            for part in range(3):
                for q in range(2):
                    then(v.tensor_copy(lnp[:, :, 3 * q + part], lnr[:, q, :]))
                    if part < 2:
                        then(v.tensor_tensor(lnr[:, q, :], lnr[:, q, :], lnp[:, :, 3 * q + part], ALU.subtract))
            for h in range(4):
                r = slice(h * DH, (h + 1) * DH)
                ins = v.tensor_scalar(rfb[r, 0, h * NF:(h + 1) * NF], rfT[r, :], sc[r, S_RF:S_RF + 1], None, ALU.mult)
            then(ins)
            for h in range(4):
                r = slice(h * DH, (h + 1) * DH)
                v.scalar_tensor_tensor(rfb[r, 1, h * NF:(h + 1) * NF], rfT[r, :], sc[r, S_RF:S_RF + 1],
                                       rfb[r, 0, h * NF:(h + 1) * NF], ALU.mult, ALU.subtract)
            for i, (w, stage, c) in enumerate(((wqkv, stage_qkv, S_W), (wo, stage_wo, S_O))):
                dve.wait_ge(a_whi, i + 1)
                then(v.scalar_tensor_tensor(w[:, 1, :, :].rearrange("p k n -> p (k n)"),
                                            stage.rearrange("p k n -> p (k n)"), col(c),
                                            w[:, 0, :, :].rearrange("p k n -> p (k n)"), ALU.mult, ALU.subtract))
            for q in range(2):
                dve.wait_ge(a_gpart, NJ * (q + 1))
                v.tensor_reduce(gsum[:, q:q + 1], gpart[:, q, :], AX.X, ALU.add).then_inc(v_gsum, 1)
            dve.wait_ge(pe_gsum, 1)
            then(v.tensor_scalar(thr[:, :], small[:, 0:2], 1.0 / (HID * D), GAMMA_EPS, ALU.mult, ALU.add))
            then(v.tensor_scalar(nthr[:, :], thr[:, :], -0.5, None, ALU.mult))
            then(v.tensor_scalar(thr[:, :], thr[:, :], 0.5, None, ALU.mult))
            for q, (stage, neg, w) in enumerate(((stage_fc, neg_fc, wfc), (stage_pj, neg_pj, wpj))):
                v.tensor_scalar(neg, stage, nthr[:, q:q + 1], None, ALU.is_lt).then_inc(v_neg, 1)
                dve.wait_ge(v_neg, 2 * q + 1)
                v.scalar_tensor_tensor(w[:, :, :], stage, thr[:, q:q + 1], neg, ALU.is_gt,
                                       ALU.subtract).then_inc(v_neg, 1)
            dve.wait_ge(pe_ab, 1)
            v.tensor_copy(ab6, feat[1][0:6, :]).then_inc(v_ab, 1)
            for h, dst in enumerate((A_bc, B_bc)):
                dve.wait_ge(pe_abc, h + 1)
                v.tensor_copy(dst[:, :], proj[h][:, :]).then_inc(v_abc, 1)

            def x_stats(m):
                dve.wait_ge(x_in, 16 * m + 16)
                for s in range(SUB):
                    v.bn_stats(bst[:, s, :], xat[:, s, :]).then_inc(ln_st, 1)
                for s in range(SUB):
                    dve.wait_ge(ln_st, 4 * m + s + 1)
                    settle(dve, v_own)
                    v.bn_aggr(mv[:, s, :], bst[:, s, :]).then_inc(ln_mv, 1)
                dve.wait_ge(ln_mv, 4 * m + 4)
                v.tensor_scalar(ve[:, :], mv[:, :, 1], LN_EPS, None, ALU.add).then_inc(ln_ve, 1)

            def x_scales(m):
                dve.wait_ge(ln_rstd, m + 1)
                v.tensor_scalar(xsc[:, :], rstd[:, :], X_UP, None, ALU.mult).then_inc(ln_sc, 1)
                v.scalar_tensor_tensor(xnb[:, :], mv[:, :, 0], -X_UP, rstd[:, :], ALU.mult, ALU.mult).then_inc(ln_sc, 1)

            def xT_out(m, soff, s):
                dve.wait_ge(pe_t, 4 * m + s + 1 + 2)
                dst = xT[:, ds(soff, XS)].rearrange("p (a n) -> p a n", n=TOK)[:, :, s * P:(s + 1) * P]
                v.tensor_scalar(dst, t16, 1.0, None, ALU.mult).then_inc(t_ev, 1)

            x_stats(0)
            x_scales(0)
            for s in range(SUB):
                xT_out(0, 0, s)

            def split_low(u, h4, g):
                dve.wait_ge(a_sq, h4 + g + 1)
                v.scalar_tensor_tensor(qkT[:, 1, g, :], proj[g % 2][:, :], QK_DOWN, qkT[:, 0, g, :], ALU.mult,
                                       ALU.subtract).then_inc(p_free, 1)

            def square_low(h4, g):
                dve.wait_ge(g_sqh, h4 + g + 1)
                v.scalar_tensor_tensor(sql[:, g, :], sqh[:, g, :], -SQ_LIFT, sqL[:, g % 2, :], ALU.mult,
                                       ALU.add).then_inc(v_sql, 1)

            def splits(u, h4, n=None):
                for g in range(KD):
                    split_low(u, h4, g)
                    if g == 1 and n is not None:
                        attention_low(n, 3)
                    if g:
                        square_low(h4, g - 1)
                square_low(h4, KD - 1)

            def sums_out(r):
                dve.wait_ge(pe_ssq, r + 1)
                v.tensor_scalar(ssb[:, :], small[:, 0:SUB * HEADS], 2.0 ** -100, None, ALU.max).then_inc(v_ssb, 1)

            def roots(r):
                done = dve.snap(ROOT_STEPS * r)

                def after(k):
                    dve.wait_ge(v_rt1, done + k)

                dve.wait_ge(v_ssb, r + 1)
                v.tensor_scalar(rt_t[:, :].bitcast(I32), ssb[:, :].bitcast(I32), 1, None,
                                ALU.logical_shift_right).then_inc(v_rt1, 1)
                after(1)
                v.tensor_scalar(rt_y[:, :].bitcast(I32), rt_t[:, :].bitcast(I32), -1, 0x5F3759DF, ALU.mult,
                                ALU.add).then_inc(v_rt1, 1)
                for k in range(3):
                    after(2 + 3 * k)
                    v.tensor_tensor(rt_t[:, :], rt_y[:, :], rt_y[:, :], ALU.mult).then_inc(v_rt1, 1)
                    after(3 + 3 * k)
                    v.scalar_tensor_tensor(rt_t[:, :], rt_t[:, :], -0.5, ssb[:, :], ALU.mult,
                                           ALU.mult).then_inc(v_rt1, 1)
                    after(4 + 3 * k)
                    v.scalar_tensor_tensor(rt_y[:, :], rt_t[:, :], 1.5, rt_y[:, :], ALU.add,
                                           ALU.mult).then_inc(v_rt1, 1)
                after(ROOT_STEPS)
                v.tensor_tensor(rsb[:, :], ssb[:, :], rt_y[:, :], ALU.mult).then_inc(v_root, 1)

            def v_out(n, u, s):
                dve.wait_ge(p_full, u + 4 + s + 1)
                dve.wait_ge(pe_kv, 4 * n + s + 1)
                v.tensor_scalar(vv[:, s, :, 0:2 * DH], proj[s % 2][:, :].rearrange("p (h c) -> p h c", h=PAIRS),
                                QK_DOWN, None, ALU.mult).then_inc(p_free, 1)

            def k_minus_norm(n, f, s, h):
                dve.wait_ge(f_full, f + 2 * s + h + 1)
                dve.wait_ge(pe_kv, 4 * n + s + 3)
                v.tensor_tensor(kp[:, s % 2, h * D:(h + 1) * D].rearrange("p (h f) -> p h f", f=NF),
                                feat[h][:, :].rearrange("p (h f) -> p h f", f=NF),
                                bcast(nk[:, s * HEADS + 8 * h:s * HEADS + 8 * h + 8], NF),
                                ALU.subtract).then_inc(f_free, 1)

            def add_kv(n):
                dve.wait_ge(pe_kv, 4 * n + 4 + 4)
                dve.wait_ge(v_kva, 2 * n)
                for j in range(2):
                    w = kvs[0:VC, j * D:(j + 1) * D]
                    v.tensor_tensor(w, kvbank[j][0:VC, :], w, ALU.add).then_inc(v_kva, 1)

            def norm_rows(n, r):
                dve.wait_ge(v_root, r + 1)
                dve.wait_ge(pe_nt, n)
                rs = rsb[:, :].rearrange("p (s h) -> p s h", s=SUB)
                v.tensor_scalar(nrm[:, :, 0:HEADS], rs, 64.0, None, ALU.mult).then_inc(v_nh, 1)
                dve.wait_ge(v_nh, n + 1)
                v.scalar_tensor_tensor(nrm[:, :, HEADS:2 * HEADS], rs, 64.0, nrm[:, :, 0:HEADS], ALU.mult,
                                       ALU.subtract).then_inc(v_nl, 1)

            def norms_out(n):
                dve.wait_ge(pe_nt, n + 1)
                v.tensor_copy(nrmT[:, :], t16[:, 0:SUB, :].rearrange("p s n -> p (s n)")).then_inc(v_nt, 1)

            def kv_blocks(b, f):
                dve.wait_ge(g_o, 16 * b + 2)
                v.memset(kvb[:, :, :], 0.0).then_inc(v_kvb0, 1)
                dve.wait_ge(v_kvb0, b + 1)
                for j in range(2):
                    dve.wait_ge(f_full, f - 2 + j + 1)
                    src = feat[j][:, 0:4 * 66].rearrange("p (a c) -> p a c", c=66)
                    d = kvb[:, 4 * j:4 * j + 4, :]
                    for h in range(2):
                        r = slice(64 * h, 64 * h + 64)
                        v.tensor_copy(d[r, :, h * DH:(h + 1) * DH], src[r, :, h * DH:(h + 1) * DH])
                        ins = v.tensor_copy(d[r, :, 64 + h * DH:64 + (h + 1) * DH], bcast(src[r, :, 64], DH))
                    ins.then_inc(f_free, 1)

            def out_rows(u, toff, s):
                dve.wait_ge(p_full, u + s + 1)
                v.scalar_tensor_tensor(S[:, ds(toff + s * D, D)], proj[s % 2][:, :], col(S_CO), bo_h[:, :], ALU.mult,
                                       ALU.add).then_inc(p_free, 1)

            def numerators(n, p):
                dve.wait_ge(pe_att, 8 * n + p + 1 + 2)
                h = 64 * (p % 2)
                v.tensor_copy(at32[h:h + 64, (p // 2) % 2, :], attbank[p % 2][0:64, :]).then_inc(v_num, 1)

            def reciprocals(n, g):
                dve.wait_ge(a_dn, 8 * n + 2 * g + 2 + 2)
                v.transpose(dT, dn[:, g % 2, :]).then_inc(v_dt, 1)
                dve.wait_ge(v_dt, 4 * n + g + 1)
                v.reciprocal(rT, dT.rearrange("p (c r) -> p c r", r=32)[:, :, 0]).then_inc(v_rt, 1)
                dve.wait_ge(v_rt, 4 * n + g + 1)
                v.transpose(dn[:, g % 2, :].rearrange("p (c r) -> p c r", r=32), bcast(rT, 32)).then_inc(v_rr, 1)

            def attention_low(n, g):
                dve.wait_ge(g_ah, 4 * n + g + 1)
                v.tensor_tensor(attT[:, 1, g, :], at32[:, g % 2, :], attT[:, 0, g, :], ALU.subtract).then_inc(v_al, 1)

            def q_tile(b, t, n, u, f, first):
                h4 = 32 * b + 16 + 4 * t
                r = 8 * b + 4 + t
                splits(u, h4, None if first else n - 1)
                toff = t * SUB * D - SUB * D
                if first:
                    kv_blocks(b, f)
                else:
                    out_rows(u + 4, toff, 0)
                sums_out(r)
                if not first:
                    out_rows(u + 4, toff, 1)
                roots(r)
                norm_rows(n, r)
                if not first:
                    out_rows(u + 4, toff, 2)
                    out_rows(u + 4, toff, 3)
                norms_out(n)
                for p in range(PAIRS):
                    numerators(n, p)
                    if p % 2:
                        reciprocals(n, p // 2)
                    elif p:
                        attention_low(n, p // 2 - 1)

            def ffn_step(g0, j, i, between=None):
                w = wn[:, ds(j, 1)]
                dve.wait_ge(a_g, g0 + 3)
                dve.wait_ge(pe_dn, g0 + 1)
                v.tensor_scalar(gh[:, i, :], gbuf[:, i, :], w, None, ALU.mult).then_inc(v_gh, 1)
                dve.wait_ge(v_gh, g0 + 1)
                v.scalar_tensor_tensor(gl[:, i, :], gbuf[:, i, :], w, gh[:, i, :], ALU.mult,
                                       ALU.subtract).then_inc(v_gl, 1)
                if between is not None:
                    between()
                    dve.wait_ge(a_gsq, g0 + 1)
                    v.tensor_scalar(accs, gsq[:, i, :], 1.0, None, ALU.mult).then_inc(v_accs, 1)
                else:
                    dve.wait_ge(a_gsq, g0 + 1)
                    dve.wait_ge(v_accs, g0 + 2)
                    v.tensor_tensor(accs, accs, gsq[:, i, :], ALU.add).then_inc(v_accs, 1)

            def split_sums(n):
                dve.wait_ge(pe_st, n)
                dve.wait_ge(g_accg, 16 * n + 16 + 2)
                v.tensor_scalar(accp[:, 0, :], accg, 1.0, None, ALU.mult).then_inc(v_aph, 1)
                dve.wait_ge(v_accs, 16 * n + 16 + 2)
                v.tensor_scalar(accp[:, 2, :], accs, SQSUM_DOWN, None, ALU.mult).then_inc(v_aph, 1)
                dve.wait_ge(v_aph, 2 * n + 1)
                v.tensor_tensor(accp[:, 1, :], accg, accp[:, 0, :], ALU.subtract).then_inc(v_apl, 1)
                dve.wait_ge(v_aph, 2 * n + 2)
                v.scalar_tensor_tensor(accp[:, 3, :], accs, SQSUM_DOWN, accp[:, 2, :], ALU.mult,
                                       ALU.subtract).then_inc(v_apl, 1)

            def ffn_stats(n):
                dve.wait_ge(pe_st, n + 1)
                q = small[:, 0:2 * SUB].rearrange("p (s q) -> p s q", q=2)
                v.tensor_scalar(nm[:, :], q[:, :, 0], -1.0 / HID, None, ALU.mult).then_inc(v_st, 1)
                v.tensor_scalar(e2[:, :], q[:, :, 1], 1.0 / (SQSUM_DOWN * HID), LN_EPS, ALU.mult,
                                ALU.add).then_inc(v_st, 1)
                dve.wait_ge(v_st, 2 * n + 2)
                v.scalar_tensor_tensor(mm[:, :], nm[:, :], -1.0, nm[:, :], ALU.mult, ALU.mult).then_inc(v_s3, 1)
                dve.wait_ge(v_s3, n + 1)
                v.tensor_tensor(mm[:, :], mm[:, :], e2[:, :], ALU.add).then_inc(v_s4, 1)
                dve.wait_ge(v_s4, n + 1)
                v.tensor_scalar(fv[:, :], mm[:, :], LN_EPS, None, ALU.max).then_inc(v_s5, 1)

            def ffn_scale(n):
                dve.wait_ge(g_rs, n + 1)
                v.tensor_scalar(fr[:, :], frs[:, :], col(S_CR), None, ALU.mult).then_inc(v_fr, 1)

            def y_rows(e, q):
                y = yb[:, ds(q, 1), :].rearrange("p a d -> p (a d)")
                dve.wait_ge(a_yb, e + 1 + 4)
                v.scalar_tensor_tensor(y, A_bc[:, :], nm[:, ds(q, 1)], y, ALU.mult, ALU.add).then_inc(v_y1, 1)
                dve.wait_ge(v_y1, e + 1)
                v.scalar_tensor_tensor(y, y, fr[:, ds(q, 1)], B_bc[:, :], ALU.mult, ALU.add).then_inc(v_y, 1)

            def silu_rows(e, q):
                y = yb[:, ds(q, 1), :].rearrange("p a d -> p (a d)")
                dve.wait_ge(a_th, e + 1)
                v.scalar_tensor_tensor(y, th, 1.0, y, ALU.add, ALU.mult).then_inc(v_u, 1)

            def ffn_tile(n, prev):
                g0 = dve.snap(16 * n)

                def sums_before():
                    if prev:
                        split_sums(n - 1)
                    dve.wait_ge(v_apl, 2 * n)

                ffn_step(g0, 0, 0, sums_before)
                if prev:
                    ffn_stats(n - 1)
                ffn_step(g0 + 1, 1, 1)
                if prev:
                    ffn_scale(n - 1)
                with dve.Fori(0, 2) as q:
                    for i in range(6):
                        ffn_step(g0 + 6 * q + 2 + i, 6 * q + 2 + i, i % 2)
                        if prev:
                            r = 2 * q + i // 4
                            if i == 2:
                                dve.wait_ge(v_fr, n)
                            if i in (2, 4):
                                y_rows(4 * n - 4 + r, r)
                            if i in (3, 5):
                                silu_rows(4 * n - 4 + r, r)
                for i in range(2):
                    ffn_step(g0 + NJ - 2 + i, NJ - 2 + i, i)

            with dve.Fori(0, B) as b:
                dve.wait_ge(v_u, 16 * b)
                v.memset(kvs[:, :], 0.0).then_inc(v_kvz, 1)
                v.memset(vv[:, :, :, 2 * DH], 1.0)
                dve.wait_ge(v_kvz, b + 1)
                settle(dve, v_own)
                with dve.Fori(0, TB) as t:
                    n = dve.snap(b * TB + t)
                    u = dve.snap(b * PU + t * 8)
                    f = dve.snap(b * FU + t * 8)
                    r = 8 * b + t
                    h4 = 32 * b + 4 * t
                    soff = dve.snap(((n + 1) % SLOTS) * XS)
                    x_stats(n + 1)
                    for g in range(KD):
                        split_low(u, h4, g)
                        if g == 1:
                            x_scales(n + 1)
                        if g:
                            square_low(h4, g - 1)
                    square_low(h4, KD - 1)
                    v_out(n, u, 0)
                    sums_out(r)
                    v_out(n, u, 1)
                    roots(r)
                    v_out(n, u, 2)
                    dve.wait_ge(v_root, r + 1)
                    v.tensor_scalar(nk[:, :], rsb[:, :], col(S_NK), None, ALU.mult).then_inc(v_nk, 1)
                    v_out(n, u, 3)
                    dve.wait_ge(v_nk, n + 1)
                    for s in range(SUB):
                        for h in range(2):
                            k_minus_norm(n, f, s, h)
                        xT_out(n + 1, soff, s)
                    add_kv(n)
                n0 = dve.snap(b * TB)
                q_tile(b, 0, n0, dve.snap(b * PU + 32), dve.snap(b * FU + 34), True)
                with dve.Fori(1, TB) as t:
                    q_tile(b, t, dve.snap(b * TB + t), dve.snap(b * PU + 28 + t * 8), dve.snap(b * FU + 34 + t * 8),
                           False)
                attention_low(dve.snap(b * TB + TB - 1), 3)
                for s in range(SUB):
                    out_rows(dve.snap(b * PU + 60), 3 * SUB * D, s)
                ffn_tile(n0, False)
                with dve.Fori(1, TB) as t:
                    ffn_tile(dve.snap(b * TB + t), True)
                n3 = dve.snap(b * TB + TB - 1)
                split_sums(n3)
                ffn_stats(n3)
                ffn_scale(n3)
                dve.wait_ge(v_fr, n3 + 1)
                settle(dve, v_own)
                with dve.Fori(0, 4) as q:
                    y_rows(16 * b + 12 + q, q)
                    silu_rows(16 * b + 12 + q, q)


def bcast(ap, n):
    return ap.unsqueeze(len(ap.shape)).broadcast_to([*ap.shape, n])


_INS = ["L0_attn_x", "L0_attn_w_qkv", "L0_attn_w_out", "L0_attn_b_out", "L0_attn_random_features", "L0_ffn_W_fc",
        "L0_ffn_ln_w", "L0_ffn_ln_b", "L0_ffn_W_proj"]


def kernel(**inputs):
    import numpy as _np
    import concourse.bacc as _bacc
    from concourse import mybir as _mybir
    from concourse.bass_utils import run_bass_kernel_spmd as _run

    nc = _bacc.Bacc("TRN2", target_bir_lowering=False, num_devices=1)
    arrays, args = {}, []
    for name in _INS:
        a = _np.asarray(inputs[name])
        if a.ndim == 2:
            a = a.T
        elif name.startswith("L0_ffn_ln"):
            a = a.reshape(NJ, P).T
        arrays[f"in_{name}"] = _np.ascontiguousarray(a)
    arrays.update(setup_constants())
    for name, a in arrays.items():
        args.append(nc.dram_tensor(name, a.shape, _mybir.dt.from_np(a.dtype), kind="ExternalInput").ap())
    args.append(nc.dram_tensor("out_0", (B, SEQ, D), F32, kind="ExternalOutput").ap())
    build_program(nc, *args)
    r = _run(nc, [arrays], core_ids=[0])
    return r.results[0]["out_0"]
```

```python
from contextlib import ExitStack

import numpy as np

import concourse.bass as bass
from concourse import mybir

F32 = mybir.dt.float32
F16 = mybir.dt.float16
BF16 = mybir.dt.bfloat16
I32 = mybir.dt.int32
ALU = mybir.AluOpType
ACT = mybir.ActivationFunctionType
AX = mybir.AxisListType
ABSMAX = bass.bass_isa.ReduceOp.max

P = 128
D = 512
KD = D // P
HEADS = 16
DH = D // HEADS
NF = 64
HID = 2048
NJ = HID // P
B, SEQ = 4, 2048
TOK = 512
SUB = TOK // P
TB = SEQ // TOK
PAIRS = HEADS // 2
SLOTS = 5
XS = 2 * KD * TOK
LN_EPS = 1e-5
VC = 65
GAMMA_EPS = 1e-6
DEN_EPS = 1e-6

X_UP = 2.0 ** 8
W_UP = 2.0 ** 8
QK_DOWN = 2.0 ** -11
SQ_DOWN = 2.0 ** -13
SQ_LIFT = 2.0 ** 12
G_UP = 2.0 ** 5
SQSUM_DOWN = 2.0 ** -7


def setup_constants():
    ident = np.eye(P, dtype=np.float32)
    sel = np.zeros((P, PAIRS * P), np.float32)
    for part in range(2):
        for h in range(HEADS):
            sel[part * HEADS + h, h * NF:(h + 1) * NF] = 1.0
    heads = np.zeros((P, 2 * KD), np.float32)
    for p in range(P):
        heads[p, p // DH] = 1.0
        heads[p, KD + p // DH] = 1.0 / SQ_LIFT
    pick = np.zeros((6, 2 * P), np.float32)
    pick[0:3, 0:P] = 1.0
    pick[3:6, P:] = 1.0
    return {"c_ident": ident, "c_sel": sel, "c_heads": heads, "c_pick": pick}


def build_program(nc, x, w_qkv, w_out, b_out, rf, w_fc, ln_w, ln_b, w_proj, c_ident, c_sel, c_heads, c_pick, out):
    ds = bass.ds
    x_v = x.rearrange("b (t s p) d -> (b t) p s d", s=SUB, p=P)
    out_v = out.rearrange("b (t s p) d -> (b t) p s d", s=SUB, p=P)

    with ExitStack() as ctx:
        def sb(name, shape, dt):
            return ctx.enter_context(nc.sbuf_tensor(name, shape, dt))

        def sem(name):
            return ctx.enter_context(nc.semaphore(name))

        xT = sb("xT", [P, SLOTS * XS], F16)
        wqkv = sb("wqkv", [P, 2, KD, 3 * D], F16)
        wo = sb("wo", [P, 2, KD, D], F16)
        wfc = sb("wfc", [P, KD, HID], BF16)
        wpj = sb("wpj", [P, NJ, D], BF16)
        S = sb("S", [P, TB * SUB * D], F32)
        A_bc = sb("A_bc", [P, D], F32)
        B_bc = sb("B_bc", [P, D], F32)
        bo_h = sb("bo_h", [P, D], F32)
        rfb = sb("rfb", [P, 2, 4 * NF], F16)
        nsel = sb("nsel", [P, PAIRS, P], BF16)
        heads16 = sb("heads16", [P, 2 * KD], F16)
        ident16 = sb("ident16", [P, P], F16)
        ident32 = sb("ident32", [P, P], F32)
        ones16 = sb("ones16", [P, 2], F16)
        wn = sb("wn", [P, NJ], F32)
        sc = sb("sc", [P, 16], F32)
        S_W, S_O, S_RF, S_E, S_NK, S_NS, S_CO, S_CR = range(8)
        col = lambda i: sc[:, i:i + 1]

        ARENA = 37376
        arena = sb("arena", [P, ARENA // 4], F32)

        def at(off, n, dt=F32):
            size = 4 if dt in (F32, I32) else 2
            v = arena[:, off // 4:(off + n * size) // 4]
            return v if dt == F32 else v.bitcast(dt)

        R = 0
        kp = at(R, 2 * 2 * D * 1).rearrange("p (a n) -> p a n", a=2)
        vv = at(R + 8192, SUB * PAIRS * VC).rearrange("p (s h c) -> p s h c", s=SUB, c=VC)
        qp = at(R, 2 * TOK).rearrange("p (a n) -> p a n", a=2)
        dn = at(R + 4096, 2 * TOK).rearrange("p (a n) -> p a n", a=2)
        dT = at(R + 8192, TOK)
        at32 = at(R + 10240, 2 * TOK).rearrange("p (a n) -> p a n", a=2)
        rT = at(R + 14336, SUB * 4)
        gh = at(R + 8192, 2 * TOK, F16).rearrange("p (a n) -> p a n", a=2)
        gl = at(R + 10240, 2 * TOK, F16).rearrange("p (a n) -> p a n", a=2)
        KVQ = 16640
        qkT = at(KVQ, 2 * KD * TOK, F16).rearrange("p (a g n) -> p a g n", a=2, g=KD)
        sqL = at(KVQ + 8192, 2 * TOK).rearrange("p (a n) -> p a n", a=2)
        sqh = at(KVQ + 12288, KD * TOK, F16).rearrange("p (g n) -> p g n", g=KD)
        sql = at(KVQ + 16384, KD * TOK, F16).rearrange("p (g n) -> p g n", g=KD)
        gbuf = at(KVQ, 2 * TOK).rearrange("p (a n) -> p a n", a=2)
        accg = at(KVQ + 4096, TOK)
        accs = at(KVQ + 6144, TOK)
        gsq = sqL
        accp = sqh
        stage_qkv = at(0, KD * 3 * D).rearrange("p (k n) -> p k n", k=KD)
        stage_wo = at(24576, KD * D).rearrange("p (k n) -> p k n", k=KD)
        neg_pj = at(0, NJ * D, BF16).rearrange("p (j n) -> p j n", j=NJ)
        stage_fc = S[:, :].rearrange("p (k n) -> p k n", k=KD)
        stage_pj = xT[:, XS:].bitcast(F32).rearrange("p (j n) -> p j n", j=NJ)
        neg_fc = wpj[:, :, :].rearrange("p j n -> p (j n)").rearrange("p (k n) -> p k n", k=KD)

        xln = S[:, 0:SUB * D].rearrange("p (s n) -> p s n", s=SUB)
        xat = sb("xat", [P, SUB, D], F32)
        attT = xat[:, :, :].bitcast(F16).rearrange("p (a b) n -> p a (b n)", a=2).rearrange(
            "p a (g n) -> p a g n", g=KD)
        yb = xat
        xhl = sb("xhl", [P, 2, 2, D], F16)
        kvs = sb("kvs", [P, PAIRS * P], F32)
        th = kvs[:, 0:D]
        kvb = sb("kvb", [P, PAIRS, P], F32)
        xres = kvb[:, :, :].rearrange("p a b -> p (a b)").rearrange("p (a n) -> p a n", a=2)
        nrm = sb("nrm", [P, SUB, P], F16)
        nrmT = sb("nrmT", [P, TOK], F16)
        ssb = sb("ssb", [P, SUB * HEADS], F32)
        rsb = sb("rsb", [P, SUB * HEADS], F32)
        nk = sb("nk", [P, SUB * HEADS], F32)
        rt_y = sb("rt_y", [P, SUB * HEADS], F32)
        rt_t = sb("rt_t", [P, SUB * HEADS], F32)
        mhalf = sb("mhalf", [P, SUB], F32)
        bst = sb("bst", [P, SUB, 6], F32)
        mv = sb("mv", [P, SUB, 2], F32)
        ve = sb("ve", [P, SUB], F32)
        rstd = sb("rstd", [P, SUB], F32)
        xsc = sb("xsc", [P, SUB], F32)
        xnb = sb("xnb", [P, SUB], F32)
        nm = sb("nm", [P, SUB], F32)
        e2 = sb("e2", [P, SUB], F32)
        mm = sb("mm", [P, SUB], F32)
        fv = sb("fv", [P, SUB], F32)
        frs = sb("frs", [P, SUB], F32)
        fr = sb("fr", [P, SUB], F32)
        mx = sb("mx", [P, 4], F32)
        gm = sb("gm", [P, 4], F32)
        pw = sb("pw", [P, 4], F32)
        ip = sb("ip", [P, 4], F32)
        gpart = xhl[:, 1, 0, 0:4 * NJ].bitcast(F32).rearrange("p (a n) -> p a n", a=2)
        gsum = sb("gsum", [P, 2], F32)
        thr = sb("thr", [P, 2], F32)
        nthr = sb("nthr", [P, 2], F32)
        ones32 = xhl[:, 0, 0, 0:2 * P].bitcast(F32)
        lnwb = yb[:, 0, 0:2 * NJ].rearrange("p (a j) -> p a j", a=2)
        lnr = yb[:, 0, 64:64 + 4 * NJ].rearrange("p (a j) -> p a j", a=4)
        lnp = yb[:, 0, 128:128 + 4 * NJ].bitcast(BF16)[:, 0:6 * NJ].rearrange("p (j c) -> p j c", c=6)
        rfT = yb[:, 0, 256:256 + NF]
        heads32 = yb[:, 0, 384:392]
        junk = yb[:, 1:3, :]
        ab6 = yb[0:6, 3, :]
        pick = xhl[0:6, 1, 1, :].bitcast(F32).rearrange("p (a n) -> p a n", a=2)
        sel32 = kvb

        ps = [ctx.enter_context(nc.psum_tensor(f"bank{i}", [P, 512], F32)) for i in range(8)]
        kvbank = ps[0:2]
        attbank = ps[0:2]
        small = ps[2]
        proj = ps[3:5]
        feat = ps[5:7]
        tbank = ps[7]
        down = [ps[0], ps[1], ps[3], ps[4]]
        t16 = tbank[:, :].bitcast(F16).rearrange("p (a n) -> p a n", n=P)

        ld_qkv, ld_wo, ld_fc, ld_pj = sem("ld_qkv"), sem("ld_wo"), sem("ld_fc"), sem("ld_pj")
        ld_small = sem("ld_small")
        v_set = sem("v_set")
        g_const = sem("g_const")
        v_max, g_max, v_scale = sem("v_max"), sem("g_max"), sem("v_scale")
        a_gpart, v_gsum, pe_gsum, v_thr = sem("a_gpart"), sem("v_gsum"), sem("pe_gsum"), sem("v_thr")
        a_whi, v_neg = sem("a_whi"), sem("v_neg")
        pe_ab, v_ab, pe_abc, v_abc = sem("pe_ab"), sem("v_ab"), sem("pe_abc"), sem("v_abc")
        x_in, ln_st, ln_mv, ln_ve, ln_rstd = sem("x_in"), sem("ln_st"), sem("ln_mv"), sem("ln_ve"), sem("ln_rstd")
        ln_sc, ln_xn, ln_hi, ln_lo = sem("ln_sc"), sem("ln_xn"), sem("ln_hi"), sem("ln_lo")
        pe_t, t_ev = sem("pe_t"), sem("t_ev")
        p_full, p_free = sem("p_full"), sem("p_free")
        a_hi, a_sq, g_sqh, v_sql = sem("a_hi"), sem("a_sq"), sem("g_sqh"), sem("v_sql")
        pe_ssq, v_ssb, v_rt1, v_root, v_nk = sem("pe_ssq"), sem("v_ssb"), sem("v_rt1"), sem("v_root"), sem("v_nk")
        f_full, f_free, a_kp = sem("f_full"), sem("f_free"), sem("a_kp")
        pe_kv, v_kvz, v_kva = sem("pe_kv"), sem("v_kvz"), sem("v_kva")
        v_kvb0 = sem("v_kvb0")
        v_nh, v_nl, pe_nt, v_nt = sem("v_nh"), sem("v_nl"), sem("pe_nt"), sem("v_nt")
        pe_att, a_dn, v_num = sem("pe_att"), sem("a_dn"), sem("v_num")
        v_dt, v_rt, v_rr, g_mul, g_ah, v_al = (sem("v_dt"), sem("v_rt"), sem("v_rr"), sem("g_mul"), sem("g_ah"),
                                               sem("v_al"))
        pe_fc, a_g, g_free, a_gsq = sem("pe_fc"), sem("a_g"), sem("g_free"), sem("a_gsq")
        v_gh, v_gl, v_accs, g_accg = sem("v_gh"), sem("v_gl"), sem("v_accs"), sem("g_accg")
        pe_dn, a_yb, v_aph, v_apl, pe_st = sem("pe_dn"), sem("a_yb"), sem("v_aph"), sem("v_apl"), sem("pe_st")
        v_st, v_s3, v_s4, v_s5, g_rs, v_fr = (sem("v_st"), sem("v_s3"), sem("v_s4"), sem("v_s5"), sem("g_rs"),
                                              sem("v_fr"))
        v_y1, v_y, a_th, v_u, g_us, g_o = sem("v_y1"), sem("v_y"), sem("a_th"), sem("v_u"), sem("g_us"), sem("g_o")
        xr_in, o_out = sem("xr_in"), sem("o_out")
        sp_own, pe_own, a_own, g_own, v_own = sem("sp_own"), sem("pe_own"), sem("a_own"), sem("g_own"), sem("v_own")
        block = ctx.enter_context(nc.Block())

        def snap(engine, value):
            return value if isinstance(value, int) else engine.snap(value)

        def settle(engine, own):
            engine.sem_inc(own, 1)

        PU, FU = 64, 66

        ROOT_STEPS = 11

        @block.sync
        def _(sp):
            sp.dma_start(stage_qkv, w_qkv.rearrange("(k p) n -> p k n", p=P)).then_inc(ld_qkv, 16)
            sp.dma_start(stage_wo, w_out.rearrange("(k p) n -> p k n", p=P)).then_inc(ld_wo, 16)
            sp.dma_start(ident32[:, :], c_ident).then_inc(ld_small, 16)
            sp.dma_start(heads32, c_heads).then_inc(ld_small, 16)
            sp.dma_start(sel32[:, :, :], c_sel.rearrange("p (a b) -> p a b", a=PAIRS)).then_inc(ld_small, 16)
            for h in range(4):
                sp.dma_start(rfT[h * DH:(h + 1) * DH, :], rf).then_inc(ld_small, 16)
            sp.dma_start(lnwb[:, 0, :], ln_w).then_inc(ld_small, 16)
            sp.dma_start(lnwb[:, 1, :], ln_b).then_inc(ld_small, 16)
            sp.dma_start(bo_h[:, :], b_out.rearrange("(a d) -> a d", a=1).partition_broadcast(P)).then_inc(ld_small, 16)
            sp.dma_start(pick, c_pick.rearrange("q (a p) -> q a p", a=2)).then_inc(ld_small, 16)
            sp.dma_start(stage_fc, w_fc.rearrange("(k p) n -> p k n", p=P)).then_inc(ld_fc, 16)
            sp.dma_start(stage_pj, w_proj.rearrange("(j p) n -> p j n", p=P)).then_inc(ld_pj, 16)
            sp.wait_ge(v_neg, 2)
            sp.dma_start(xln, x_v[0]).then_inc(x_in, 16)

            def load_x(m):
                src = snap(sp, m % (B * TB))
                sp.wait_ge(ln_lo, 4 * m)
                sp.dma_start(xln, x_v[ds(src, 1)].rearrange("a p s d -> p (a s) d")).then_inc(x_in, 16)

            def ffn_io(n):
                for s in range(SUB):
                    sp.wait_ge(g_o, 4 * n + s + 1)
                    settle(sp, sp_own)
                    sp.wait_ge(xr_in, 64 * n + 16 * s)
                    sp.dma_start(xres[:, s % 2, :], x_v[ds(n, 1), :, s, :].rearrange(
                        "a p d -> p (a d)")).then_inc(xr_in, 16)
                    if s:
                        sp.wait_ge(g_o, 4 * n + s + 2)
                        sp.dma_start(out_v[ds(n, 1), :, s - 1, :].rearrange("a p d -> p (a d)"),
                                     yb[:, s - 1, :]).then_inc(o_out, 16)
                sp.wait_ge(g_o, 4 * n + 4 + 2)
                sp.dma_start(out_v[ds(n, 1), :, SUB - 1, :].rearrange("a p d -> p (a d)"),
                             yb[:, SUB - 1, :]).then_inc(o_out, 16)

            def row(b, last):
                with sp.Fori(1, TB) as t:
                    load_x(snap(sp, b * TB + t + 1))
                sp.wait_ge(pe_att, 32 * b + 32 + 2)
                settle(sp, sp_own)
                n0 = snap(sp, b * TB)
                ffn_io(n0)
                if not last:
                    load_x(snap(sp, n0 + TB + 1))
                with sp.Fori(1, TB) as t:
                    ffn_io(snap(sp, b * TB + t))

            load_x(1)
            with sp.Fori(0, B - 1) as b:
                row(b, False)
            row(B - 1, True)
            sp.wait_ge(o_out, 64 * B * TB)

        @block.tensor
        def _(pe):
            def mm(o, lhsT, rhs, start, stop, **kw):
                return nc.tensor.matmul(o, lhsT, rhs, start=start, stop=stop, skip_group_check=True, **kw)

            pe.wait_ge(g_const, 1)
            pe.wait_ge(v_gsum, 2)
            mm(small[:, 0:2], ones32, gsum[:, :], True, True).then_inc(pe_gsum, 1)
            pe.wait_ge(v_neg, 4)
            for j in range(NJ):
                i = mm(feat[1][0:6, :], lnp[:, j, :], wpj[:, j, :], j == 0, j == NJ - 1)
            i.then_inc(pe_ab, 1)
            pe.wait_ge(v_ab, 1)
            for h in range(2):
                mm(proj[h][:, :], pick[:, h, :], ab6, True, True).then_inc(pe_abc, 1)

            def transpose_x(m, s):
                pe.wait_ge(ln_lo, 4 * m + s + 1)
                pe.wait_ge(t_ev, 4 * m + s)
                for a in range(2):
                    for k in range(KD):
                        i = nc.tensor.transpose(t16[:, a * KD + k, :], xhl[:, s % 2, a, k * P:(k + 1) * P],
                                                ident16[:, :])
                i.then_inc(pe_t, 1)

            for s in range(SUB):
                transpose_x(0, s)

            def xmov(off, a, k):
                return xT[:, ds(off + (a * KD + k) * TOK, TOK)]

            def project_T(u, off, first, groups=range(KD), banks=None):
                for g in groups:
                    if banks is not None and g < 2:
                        pe.wait_ge(a_yb, banks + g + 1)
                    pe.wait_ge(p_free, u + g + 1)
                    o = proj[g % 2][:, :]
                    for i, (wa, xa) in enumerate(((0, 0), (0, 1), (1, 0))):
                        for k in range(KD):
                            c0 = first + g * P
                            ins = mm(o, wqkv[:, wa, k, c0:c0 + P], xmov(off, xa, k), i == 0 and k == 0,
                                     i == 2 and k == KD - 1)
                    ins.then_inc(p_full, 1)

            def project_v(u, off, s):
                pe.wait_ge(p_free, u + 4 + s + 1)
                o = proj[s % 2][:, :]
                for i, (wa, xa) in enumerate(((0, 0), (1, 0), (0, 1))):
                    for k in range(KD):
                        ins = mm(o, xT[:, ds(off + (xa * KD + k) * TOK + s * P, P)], wqkv[:, wa, k, 2 * D:3 * D],
                                 i == 0 and k == 0, i == 2 and k == KD - 1)
                ins.then_inc(p_full, 1)

            def square_sums(h4, r):
                pe.wait_ge(v_sql, h4 + 4 + 2)
                pe.wait_ge(v_ssb, r)
                for s in range(SUB):
                    for g in range(KD):
                        o = small[:, s * HEADS + g * 4:s * HEADS + g * 4 + 4]
                        mm(o, sqh[:, g, s * P:(s + 1) * P], heads16[:, 0:4], True, False)
                        ins = mm(o, sql[:, g, s * P:(s + 1) * P], heads16[:, 4:8], False, True)
                ins.then_inc(pe_ssq, 1)

            def k_features(f, s, h):
                pe.wait_ge(f_free, f + 2 * s + h + 1)
                for g2 in range(2):
                    g = 2 * h + g2
                    o = feat[h][:, g2 * 4 * NF:(g2 + 1) * 4 * NF]
                    mm(o, qkT[:, 0, g, s * P:(s + 1) * P], rfb[:, 0, :], True, False)
                    mm(o, qkT[:, 1, g, s * P:(s + 1) * P], rfb[:, 0, :], False, False)
                    ins = mm(o, qkT[:, 0, g, s * P:(s + 1) * P], rfb[:, 1, :], False, True)
                ins.then_inc(f_full, 1)

            def kv_sums(n, u, s):
                pe.wait_ge(a_kp, 8 * n + 2 * s + 2)
                pe.wait_ge(p_free, u + 4 + s + 3)
                if s == 0:
                    pe.wait_ge(v_kva, 2 * n)
                for p in range(PAIRS):
                    ins = mm(kvbank[p // 4][0:VC, (p % 4) * P:(p % 4 + 1) * P], vv[:, s, p, :],
                             kp[:, s % 2, p * P:(p + 1) * P], s == 0 and p % 4 == 0, s == SUB - 1)
                ins.then_inc(pe_kv, 1)

            def out_project(u, n, s):
                pe.wait_ge(v_al, 4 * n + 4)
                pe.wait_ge(p_free, u + s + 1)
                for i, (wa, xa) in enumerate(((0, 0), (1, 0), (0, 1))):
                    for g in range(KD):
                        ins = mm(proj[s % 2][:, :], attT[:, xa, g, s * P:(s + 1) * P], wo[:, wa, g, :],
                                 i == 0 and g == 0, i == 2 and g == KD - 1)
                ins.then_inc(p_full, 1)

            def norms_T(n, b):
                pe.wait_ge(v_nl, n + 1)
                pe.wait_ge(t_ev, 16 * b + 20)
                pe.wait_ge(v_nt, n)
                for s in range(SUB):
                    ins = nc.tensor.transpose(t16[:, s, :], nrm[:, s, :], ident16[:, :])
                ins.then_inc(pe_nt, 1)

            def q_feature(f, p):
                pe.wait_ge(f_free, f + p + 1)
                o = feat[p % 2][:, :]
                c0 = (p % 2) * P
                mm(o, rfb[:, 0, c0:c0 + P], qkT[:, 0, p // 2, :], True, False)
                mm(o, rfb[:, 0, c0:c0 + P], qkT[:, 1, p // 2, :], False, False)
                mm(o, rfb[:, 1, c0:c0 + P], qkT[:, 0, p // 2, :], False, False)

            def minus_norm(p):
                mm(feat[p % 2][:, :], nsel[:, p, :], nrmT[:, :], False, True).then_inc(f_full, 1)

            def attend(n, f, p):
                pe.wait_ge(f_free, f + p + 1 + 2)
                pe.wait_ge(v_num, 8 * n + p + 1)
                pe.wait_ge(a_dn, 8 * n + p + 1)
                mm(attbank[p % 2][:, :], kvb[:, p, :], qp[:, p % 2, :], True, True).then_inc(pe_att, 1)

            def q_tile(b, t, n, u, f, off, noff, first):
                if first:
                    project_T(u, off, 0)
                    pe.wait_ge(v_kva, 8 * b + 8)
                    for j in range(2):
                        pe.wait_ge(f_free, f - 2 + j + 1)
                        for p in range(4):
                            c0 = (4 * j + p) * P
                            ins = nc.tensor.transpose(feat[j][:, p * 66:p * 66 + VC], kvs[0:VC, c0:c0 + P],
                                                      ident32[0:VC, 0:VC])
                        ins.then_inc(f_full, 1)
                else:
                    project_T(u, off, 0, (2, 3))
                    out_project(u + 4, n - 1, 0)
                square_sums(32 * b + 4 * t + 16, 8 * b + t + 4)
                if not first:
                    for s in range(1, SUB):
                        out_project(u + 4, n - 1, s)
                if first:
                    pe.wait_ge(f_free, f + 2)
                    q_feature(f, 0)
                    project_T(u + 4, noff, 0, (0,))
                    norms_T(n, b)
                else:
                    norms_T(n, b)
                    q_feature(f, 0)
                pe.wait_ge(v_nt, n + 1)
                minus_norm(0)
                q_feature(f, 1)
                minus_norm(1)
                un = u + 4 if first else u + 8
                for p in range(PAIRS):
                    if p == PAIRS - 2 and noff is not None and not first:
                        project_T(un, noff, 0, (0,))
                    if p == PAIRS - 1:
                        if noff is not None:
                            project_T(un, noff, 0, (1,))
                    attend(n, f, p)
                    if p + 2 < PAIRS:
                        q_feature(f, p + 2)
                        minus_norm(p + 2)

            def up(g0, off, j, i):
                pe.wait_ge(a_g, g0 + 1)
                for k in range(KD):
                    for a in range(2):
                        ins = mm(feat[i][:, :], wfc[:, k, ds(j * P, P)], xmov(off, a, k), k == 0 and a == 0,
                                 k == KD - 1 and a == 1)
                ins.then_inc(pe_fc, 1)

            def down_step(g0, n, j, i, first=False, last=False):
                pe.wait_ge(v_gl, g0 + 1 + 2)
                for s in range(SUB):
                    if first:
                        pe.wait_ge(a_yb, 4 * n - 4 + s + 1 + 4)
                    mm(down[s][:, :], gh[:, i, s * P:(s + 1) * P], wpj[:, ds(j, 1), :], first, False)
                    ins = mm(down[s][:, :], gl[:, i, s * P:(s + 1) * P], wpj[:, ds(j, 1), :], False, last)
                ins.then_inc(pe_dn, 1)

            def ffn_sums(n):
                pe.wait_ge(v_apl, 2 * n + 2)
                pe.wait_ge(v_st, 2 * n)
                for s in range(SUB):
                    for q in range(2):
                        o = small[:, 2 * s + q:2 * s + q + 1]
                        mm(o, accp[:, 2 * q, s * P:(s + 1) * P], ones16[:, 0:1], True, False)
                        ins = mm(o, accp[:, 2 * q + 1, s * P:(s + 1) * P], ones16[:, 0:1], False, True)
                ins.then_inc(pe_st, 1)

            def ffn_tile(n, off, noff, first, last):
                g0 = snap(pe, 16 * n)
                for i in range(2):
                    if not first:
                        up(g0 + i + 2, off, i + 2, i)
                    down_step(g0 + i, n, i, i, first=i == 0)
                    if i == 0 and not first:
                        ffn_sums(n - 1)
                with pe.Fori(1, NJ // 2 - 1) as jj:
                    j = 2 * jj
                    for i in range(2):
                        up(g0 + j + i + 2, off, j + i + 2, i)
                        down_step(g0 + j + i, n, j + i, i)
                for i in range(2):
                    if not last:
                        up(g0 + NJ + i, noff, i, i)
                    down_step(g0 + NJ - 2 + i, n, NJ - 2 + i, i, last=i == 1)
            def kv_tile(b, t, n, after_ffn=False):
                u = snap(pe, b * PU + t * 8)
                f = snap(pe, b * FU + t * 8)
                off = snap(pe, (n % SLOTS) * XS)
                pe.wait_ge(t_ev, 4 * n + 4)
                if after_ffn:
                    project_T(u, off, D, (0,), banks=4 * n)
                    ffn_sums(n - 1)
                    project_T(u, off, D, (1, 2, 3), banks=4 * n)
                    pe.wait_ge(a_yb, 4 * n + 4)
                    pe.wait_ge(v_st, 2 * n)
                else:
                    project_T(u, off, D)
                for s in range(2):
                    project_v(u, off, s)
                square_sums(32 * b + 4 * t, 8 * b + t)
                for s in (2, 3):
                    project_v(u, off, s)
                for s in range(SUB):
                    for h in range(2):
                        k_features(f, s, h)
                    transpose_x(n + 1, s)
                    if s:
                        kv_sums(n, u, s - 1)
                kv_sums(n, u, SUB - 1)

            def row(b, last):
                with pe.Fori(1, TB) as t:
                    kv_tile(b, t, snap(pe, b * TB + t))
                n0 = snap(pe, b * TB)
                q_tile(b, 0, n0, snap(pe, b * PU + 32), snap(pe, b * FU + 34), snap(pe, (n0 % SLOTS) * XS),
                       snap(pe, ((n0 + 1) % SLOTS) * XS), True)
                with pe.Fori(1, TB - 1) as t:
                    n = snap(pe, b * TB + t)
                    q_tile(b, t, n, snap(pe, b * PU + 28 + t * 8), snap(pe, b * FU + 34 + t * 8),
                           snap(pe, (n % SLOTS) * XS), snap(pe, ((n + 1) % SLOTS) * XS), False)
                n3 = snap(pe, b * TB + TB - 1)
                t = TB - 1
                q_tile(b, t, n3, snap(pe, b * PU + 28 + t * 8), snap(pe, b * FU + 34 + t * 8),
                       snap(pe, (n3 % SLOTS) * XS), None, False)
                pe.wait_ge(f_free, FU * b + FU + 2)
                off0 = snap(pe, (n0 % SLOTS) * XS)
                for i in range(4):
                    up(16 * n0 + i, off0, i, i % 2)
                for s in range(SUB):
                    out_project(snap(pe, b * PU + 60), n3, s)
                pe.wait_ge(p_free, PU * b + PU + 2)
                pe.wait_ge(v_num, 32 * b + 32 + 2)
                pe.wait_ge(a_dn, 32 * b + 32 + 2)
                ffn_tile(n0, off0, snap(pe, ((n0 + 1) % SLOTS) * XS), True, False)
                with pe.Fori(1, TB - 1) as t:
                    n = snap(pe, b * TB + t)
                    ffn_tile(n, snap(pe, (n % SLOTS) * XS), snap(pe, ((n + 1) % SLOTS) * XS), False, False)
                ffn_tile_last = snap(pe, (n3 % SLOTS) * XS)
                ffn_tile(n3, ffn_tile_last, None, False, True)
                if last:
                    ffn_sums(n3)
                else:
                    kv_tile(snap(pe, b + 1), 0, snap(pe, n0 + TB), after_ffn=True)

            kv_tile(0, 0, 0)
            with pe.Fori(0, B - 1) as b:
                row(b, False)
            row(B - 1, True)

        @block.scalar
        def _(act):
            def A(o, i, f, **kw):
                return nc.scalar.activation(o, i, f, **kw)

            act.wait_ge(v_scale, 1)
            A(wqkv[:, 0, :, :], stage_qkv, ACT.Copy, scale=col(S_W)).then_inc(a_whi, 1)
            A(wo[:, 0, :, :], stage_wo, ACT.Copy, scale=col(S_O)).then_inc(a_whi, 1)
            for q, (stage, l) in enumerate(((stage_fc, ld_fc), (stage_pj, ld_pj))):
                act.wait_ge(l, 16)
                flat = stage.rearrange("p a n -> p (a n)")
                for c in range(NJ):
                    if NJ * q + c >= 2:
                        act.wait_ge(a_gpart, NJ * q + c - 1)
                    A(junk[:, c % 2, :], flat[:, c * D:(c + 1) * D], ACT.Abs,
                      accum_out=gpart[:, q, c:c + 1]).then_inc(a_gpart, 1)

            def normalise(m, s):
                act.wait_ge(ln_sc, 2 * m + 2)
                A(xln[:, s, :], xln[:, s, :], ACT.Identity, scale=xsc[:, s:s + 1],
                  bias=xnb[:, s:s + 1]).then_inc(ln_xn, 1)

            for s in range(SUB):
                normalise(0, s)

            def split_high(u, h4, g, fwait=None):
                if fwait is not None and g == 0:
                    act.wait_ge(f_full, fwait)
                act.wait_ge(p_full, u + g + 1)
                A(qkT[:, 0, g, :], proj[g % 2][:, :], ACT.Copy, scale=QK_DOWN).then_inc(a_hi, 1)
                act.wait_ge(v_sql, h4 + g + 1)
                A(sqL[:, g % 2, :], proj[g % 2][:, :], ACT.Square, scale=SQ_DOWN).then_inc(a_sq, 1)

            def exp_k(n, f, s, h):
                act.wait_ge(f_free, f + 2 * s + h + 3)
                v = kp[:, s % 2, h * D:(h + 1) * D]
                A(v, v, ACT.Exp, scale=col(S_E)).then_inc(a_kp, 1)

            def exp_q(n, f, p):
                act.wait_ge(f_full, f + p + 1)
                act.wait_ge(pe_att, 8 * n + p + 1)
                A(qp[:, p % 2, :], feat[p % 2][:, :], ACT.Exp, scale=col(S_E)).then_inc(f_free, 1)

            def denominators(n, p):
                act.wait_ge(pe_att, 8 * n + p + 1 + 2)
                if p % 2 == 0:
                    act.wait_ge(g_mul, 4 * n + p // 2 + 1)
                h = 64 * (p % 2)
                A(dn[h:h + 64, (p // 2) % 2, :], attbank[p % 2][64:128, :], ACT.Copy,
                  bias=DEN_EPS).then_inc(a_dn, 1)

            def q_tile(b, t, n, u, f, first, last):
                h4 = 32 * b + 16 + 4 * t
                for g in range(0 if first else 2, KD):
                    split_high(u, h4, g, f - 2 if first else None)
                un = snap(act, u + (4 if first else 8))
                exp_q(n, f, 0)
                for p in range(PAIRS):
                    if p + 1 < PAIRS:
                        exp_q(n, f, p + 1)
                    if p >= PAIRS - 2 and not last:
                        split_high(un, h4 + 4, p - (PAIRS - 2))
                    denominators(n, p)

            def gelu_step(g0, i):
                act.wait_ge(pe_fc, g0 + 1)
                act.wait_ge(v_gl, g0 + 1)
                act.wait_ge(g_accg, g0 + 1)
                A(gbuf[:, i, :], feat[i][:, :], ACT.Gelu, scale=1.0 / X_UP).then_inc(a_g, 1)
                act.wait_ge(a_g, g0 + 3)
                act.wait_ge(v_accs, g0 + 1)
                A(gsq[:, i, :], gbuf[:, i, :], ACT.Square).then_inc(a_gsq, 1)

            def tanh_step(e):
                act.wait_ge(v_y, e + 1)
                act.wait_ge(v_u, e)
                settle(act, a_own)
                A(th, yb[:, ds(e % 4, 1), :].rearrange("p a d -> p (a d)"), ACT.Tanh, scale=0.5).then_inc(a_th, 1)

            def results(n, last):
                act.wait_ge(o_out, 64 * n)
                for s in ((2, 3, 0, 1) if last else range(SUB)):
                    act.wait_ge(pe_dn, 16 * n + 16 + 2)
                    A(yb[:, s, :], down[s][:, :], ACT.Copy).then_inc(a_yb, 1)

            def ffn_tile(n, prev, last):
                g0 = snap(act, 16 * n)
                with act.Fori(0, 2) as q:
                    for i in range(6):
                        gelu_step(g0 + 6 * q + 2 + i, i % 2)
                        if prev and i in (3, 5):
                            tanh_step(4 * n - 4 + 2 * q + i // 4)
                for i in range(2 if last else 4):
                    gelu_step(g0 + NJ - 2 + i, i % 2)
                results(n, last)

            def kv_tile(b, t, n, after_ffn=False):
                u = snap(act, b * PU + t * 8)
                f = snap(act, b * FU + t * 8)
                if after_ffn:
                    act.wait_ge(v_gl, 16 * n + 2)
                    act.wait_ge(g_accg, 16 * n + 2)
                    act.wait_ge(v_accs, 16 * n + 2)
                    act.wait_ge(a_gsq, 16 * n)
                for g in range(KD):
                    split_high(u, 32 * b + 4 * t, g, f)
                    if after_ffn and g:
                        tanh_step(4 * n - 4 + g - 1)
                    if not after_ffn and g == 2:
                        normalise(n + 1, 0)
                if after_ffn:
                    tanh_step(4 * n - 1)
                    normalise(n + 1, 0)
                for s in range(1, SUB):
                    normalise(n + 1, s)
                for s in range(SUB):
                    for h in range(2):
                        exp_k(n, f, s, h)

            def row(b, last):
                with act.Fori(1, TB) as t:
                    kv_tile(b, t, snap(act, b * TB + t))
                n0 = snap(act, b * TB)
                n3 = snap(act, b * TB + TB - 1)
                q_tile(b, 0, n0, snap(act, b * PU + 32), snap(act, b * FU + 34), True, False)
                with act.Fori(1, TB - 1) as t:
                    q_tile(b, t, snap(act, b * TB + t), snap(act, b * PU + 28 + t * 8), snap(act, b * FU + 34 + t * 8),
                           False, False)
                t = TB - 1
                q_tile(b, t, n3, snap(act, b * PU + 28 + t * 8), snap(act, b * FU + 34 + t * 8), False, True)
                for i in range(2):
                    gelu_step(16 * n0 + i, i)
                ffn_tile(n0, False, False)
                with act.Fori(1, TB - 1) as t:
                    ffn_tile(snap(act, b * TB + t), True, False)
                ffn_tile(n3, True, True)
                if last:
                    for q in range(SUB):
                        tanh_step(16 * b + 12 + q)
                else:
                    kv_tile(snap(act, b + 1), 0, snap(act, n0 + TB), after_ffn=True)

            kv_tile(0, 0, 0)
            with act.Fori(0, B - 1) as b:
                row(b, False)
            row(B - 1, True)

        @block.gpsimd
        def _(pool):
            g = nc.gpsimd

            g.memset(mhalf[:, :], -0.5)
            g.memset(ones32, 1.0)
            g.memset(rfb[:, :, :], 0.0)
            g.memset(nrm[:, :, :], 0.0)
            g.memset(ones16[:, :], 1.0).then_inc(g_const, 1)
            pool.wait_ge(v_max, 4)
            g.partition_all_reduce(gm[:, :], mx[:, :], P, ABSMAX).then_inc(g_max, 1)

            def rsqrt_x(m):
                pool.wait_ge(ln_ve, m + 1)
                g.tensor_tensor(rstd[:, :], ve[:, :], mhalf[:, :], ALU.pow).then_inc(ln_rstd, 1)

            def split_x(m, s):
                pool.wait_ge(pe_t, 4 * m + s + 1)
                pool.wait_ge(ln_xn, 4 * m + s + 1)
                settle(pool, g_own)
                g.tensor_scalar(xhl[:, s % 2, 0, :], xln[:, s, :], 1.0, 0.0, ALU.mult, ALU.add).then_inc(ln_hi, 1)
                pool.wait_ge(ln_hi, 4 * m + s + 1)
                g.tensor_tensor(xhl[:, s % 2, 1, :], xln[:, s, :], xhl[:, s % 2, 0, :],
                                ALU.subtract).then_inc(ln_lo, 1)

            def square_high(h4, r, gg):
                pool.wait_ge(pe_ssq, r)
                pool.wait_ge(a_sq, h4 + gg + 1)
                settle(pool, g_own)
                g.tensor_scalar(sqh[:, gg, :], sqL[:, gg % 2, :], 1.0 / SQ_LIFT, 0.0, ALU.mult,
                                ALU.add).then_inc(g_sqh, 1)

            def attention_high(n, gg):
                pool.wait_ge(v_rr, 4 * n + gg + 1)
                pool.wait_ge(v_num, 8 * n + 2 * gg + 2 + 2)
                a = at32[:, gg % 2, :]
                g.tensor_tensor(a, a, dn[:, gg % 2, :], ALU.mult).then_inc(g_mul, 1)
                pool.wait_ge(g_mul, 4 * n + gg + 1 + 2)
                settle(pool, g_own)
                g.tensor_scalar(attT[:, 0, gg, :], a, 1.0, 0.0, ALU.mult, ALU.add).then_inc(g_ah, 1)

            def q_tile(b, t, n, first, last):
                h4 = 32 * b + 16 + 4 * t
                r = 8 * b + 4 + t
                for gg in range(0 if first else 2, KD):
                    square_high(h4, r, gg)
                if first:
                    pool.wait_ge(o_out, 256 * b)
                    settle(pool, g_own)
                for gg in range(KD):
                    if gg == KD - 1 and not last:
                        for j in range(2):
                            square_high(h4 + 4, r + 1, j)
                    attention_high(n, gg)

            def finish(e):
                pool.wait_ge(v_u, e + 1)
                settle(pool, g_own)
                y = yb[:, ds(e % 4, 1), :].rearrange("p a d -> p (a d)")
                g.tensor_tensor(y, y, S[:, ds((e % 16) * D, D)], ALU.mult).then_inc(g_us, 1)
                pool.wait_ge(xr_in, 16 * e + 16)
                pool.wait_ge(g_us, e + 1)
                settle(pool, g_own)
                xr = xres[:, ds(e % 2, 1), :].rearrange("p a d -> p (a d)")
                g.tensor_tensor(y, y, xr, ALU.add).then_inc(g_o, 1)

            def sum_step(g0, i):
                pool.wait_ge(a_g, g0 + 3)
                pool.wait_ge(g_accg, g0 + 2)
                g.tensor_tensor(accg, accg, gbuf[:, i, :], ALU.add).then_inc(g_accg, 1)

            def first_sum(n, g0):
                pool.wait_ge(a_g, g0 + 3)
                pool.wait_ge(v_apl, 2 * n)
                settle(pool, g_own)
                g.tensor_scalar(accg, gbuf[:, 0, :], 1.0, 0.0, ALU.mult, ALU.add).then_inc(g_accg, 1)

            def ffn_root(n):
                pool.wait_ge(v_s5, n + 1)
                g.tensor_tensor(frs[:, :], fv[:, :], mhalf[:, :], ALU.pow).then_inc(g_rs, 1)

            def ffn_tile(n, prev):
                g0 = snap(pool, 16 * n)
                first_sum(n, g0)
                sum_step(g0 + 1, 1)
                if prev:
                    ffn_root(n - 1)
                with pool.Fori(0, 2) as q:
                    for i in range(6):
                        sum_step(g0 + 6 * q + 2 + i, i % 2)
                        if prev and i in (3, 5):
                            finish(4 * n - 4 + 2 * q + i // 4)
                for i in range(2):
                    sum_step(g0 + NJ - 2 + i, i)

            rsqrt_x(0)
            for s in range(SUB):
                split_x(0, s)
            def kv_tile(b, t, n, after_ffn=False):
                h4, r = 32 * b + 4 * t, 8 * b + t
                rsqrt_x(n + 1)
                if after_ffn:
                    ffn_root(n - 1)
                    pool.wait_ge(pe_st, n)
                    settle(pool, g_own)
                for gg in range(KD):
                    square_high(h4, r, gg)
                    if after_ffn and gg:
                        finish(4 * n - 4 + gg - 1)
                if after_ffn:
                    finish(4 * n - 1)
                for s in range(SUB):
                    split_x(n + 1, s)

            def row(b, last):
                n0 = snap(pool, b * TB)
                n3 = snap(pool, b * TB + TB - 1)
                with pool.Fori(1, TB) as t:
                    kv_tile(b, t, snap(pool, b * TB + t))
                q_tile(b, 0, n0, True, False)
                with pool.Fori(1, TB - 1) as t:
                    q_tile(b, t, snap(pool, b * TB + t), False, False)
                q_tile(b, TB - 1, n3, False, True)
                ffn_tile(n0, False)
                with pool.Fori(1, TB) as t:
                    ffn_tile(snap(pool, b * TB + t), True)
                if last:
                    ffn_root(n3)
                    for q in range(SUB):
                        finish(16 * b + 12 + q)
                else:
                    kv_tile(snap(pool, b + 1), 0, snap(pool, n0 + TB), after_ffn=True)

            kv_tile(0, 0, 0)
            with pool.Fori(0, B - 1) as b:
                row(b, False)
            row(B - 1, True)

        @block.vector
        def _(dve):
            v = nc.vector
            steps = [0]

            def then(ins):
                steps[0] += 1
                ins.then_inc(v_set, 1)
                dve.wait_ge(v_set, steps[0])

            for s_, k_ in ((p_free, 2), (f_free, 2), (v_sql, 2), (pe_kv, 4), (pe_att, 2), (v_num, 2), (a_dn, 2),
                           (g_mul, 2), (a_g, 2), (v_gl, 2), (g_accg, 2), (v_accs, 2), (a_yb, 4), (pe_t, 2),
                           (pe_dn, 2), (g_o, 2)):
                dve.sem_inc(s_, k_)
            v.memset(mx[:, :], 0.0)
            dve.wait_ge(ld_small, 16 * 11)
            v.tensor_copy(ident16[:, :], ident32[:, :])
            then(v.tensor_copy(heads16[:, :], heads32))
            v.tensor_reduce(mx[:, 2:3], rfT, AX.X, ALU.max, apply_absolute_value=True).then_inc(v_max, 1)
            v.tensor_reduce(mx[:, 3:4], lnwb[:, 0, :], AX.X, ALU.max, apply_absolute_value=True).then_inc(v_max, 1)
            dve.wait_ge(ld_qkv, 16)
            v.tensor_reduce(mx[:, 0:1], stage_qkv.rearrange("p k n -> p (k n)"), AX.X, ALU.max,
                            apply_absolute_value=True).then_inc(v_max, 1)
            dve.wait_ge(ld_wo, 16)
            v.tensor_reduce(mx[:, 1:2], stage_wo.rearrange("p k n -> p (k n)"), AX.X, ALU.max,
                            apply_absolute_value=True).then_inc(v_max, 1)
            dve.wait_ge(g_max, 1)
            then(v.tensor_scalar(pw[:, :].bitcast(I32), gm[:, :].bitcast(I32), 0x7F800000, None, ALU.bitwise_and))
            then(v.tensor_scalar(pw[:, :], pw[:, :], 2.0 ** -100, None, ALU.max))
            then(v.reciprocal(ip[:, :], pw[:, :]))
            v.tensor_scalar(col(S_W), ip[:, 0:1], W_UP, None, ALU.mult)
            v.tensor_scalar(col(S_O), ip[:, 1:2], W_UP, None, ALU.mult)
            v.tensor_scalar(col(S_RF), ip[:, 2:3], W_UP, None, ALU.mult)
            v.scalar_tensor_tensor(col(S_E), pw[:, 0:1], 2.0 ** -16, pw[:, 2:3], ALU.mult, ALU.mult)
            v.tensor_scalar(col(S_NK), ip[:, 2:3], 2.0 ** 19, None, ALU.mult)
            v.tensor_scalar(col(S_NS), ip[:, 2:3], -(2.0 ** 13), None, ALU.mult)
            v.scalar_tensor_tensor(col(S_CO), pw[:, 0:1], 2.0 ** -14, pw[:, 1:2], ALU.mult, ALU.mult)
            v.tensor_scalar(col(S_CR), pw[:, 3:4], 1.0 / G_UP, None, ALU.mult)
            then(v.tensor_scalar(wn[:, :], lnwb[:, 0, :], ip[:, 3:4], G_UP, ALU.mult, ALU.mult))
            v.tensor_scalar(nsel[:, :, :], sel32[:, :, :], col(S_NS), None, ALU.mult)
            v.tensor_scalar(bo_h[:, :], bo_h[:, :], 0.5, None, ALU.mult).then_inc(v_scale, 1)
            then(v.tensor_copy(lnr[:, 0, :], wn[:, :]))
            then(v.tensor_copy(lnr[:, 1, :], lnwb[:, 1, :]))
            for part in range(3):
                for q in range(2):
                    then(v.tensor_copy(lnp[:, :, 3 * q + part], lnr[:, q, :]))
                    if part < 2:
                        then(v.tensor_tensor(lnr[:, q, :], lnr[:, q, :], lnp[:, :, 3 * q + part], ALU.subtract))
            for h in range(4):
                r = slice(h * DH, (h + 1) * DH)
                ins = v.tensor_scalar(rfb[r, 0, h * NF:(h + 1) * NF], rfT[r, :], sc[r, S_RF:S_RF + 1], None, ALU.mult)
            then(ins)
            for h in range(4):
                r = slice(h * DH, (h + 1) * DH)
                v.scalar_tensor_tensor(rfb[r, 1, h * NF:(h + 1) * NF], rfT[r, :], sc[r, S_RF:S_RF + 1],
                                       rfb[r, 0, h * NF:(h + 1) * NF], ALU.mult, ALU.subtract)
            for i, (w, stage, c) in enumerate(((wqkv, stage_qkv, S_W), (wo, stage_wo, S_O))):
                dve.wait_ge(a_whi, i + 1)
                then(v.scalar_tensor_tensor(w[:, 1, :, :].rearrange("p k n -> p (k n)"),
                                            stage.rearrange("p k n -> p (k n)"), col(c),
                                            w[:, 0, :, :].rearrange("p k n -> p (k n)"), ALU.mult, ALU.subtract))
            for q in range(2):
                dve.wait_ge(a_gpart, NJ * (q + 1))
                v.tensor_reduce(gsum[:, q:q + 1], gpart[:, q, :], AX.X, ALU.add).then_inc(v_gsum, 1)
            dve.wait_ge(pe_gsum, 1)
            then(v.tensor_scalar(thr[:, :], small[:, 0:2], 1.0 / (HID * D), GAMMA_EPS, ALU.mult, ALU.add))
            then(v.tensor_scalar(nthr[:, :], thr[:, :], -0.5, None, ALU.mult))
            then(v.tensor_scalar(thr[:, :], thr[:, :], 0.5, None, ALU.mult))
            for q, (stage, neg, w) in enumerate(((stage_fc, neg_fc, wfc), (stage_pj, neg_pj, wpj))):
                v.tensor_scalar(neg, stage, nthr[:, q:q + 1], None, ALU.is_lt).then_inc(v_neg, 1)
                dve.wait_ge(v_neg, 2 * q + 1)
                v.scalar_tensor_tensor(w[:, :, :], stage, thr[:, q:q + 1], neg, ALU.is_gt,
                                       ALU.subtract).then_inc(v_neg, 1)
            dve.wait_ge(pe_ab, 1)
            v.tensor_copy(ab6, feat[1][0:6, :]).then_inc(v_ab, 1)
            for h, dst in enumerate((A_bc, B_bc)):
                dve.wait_ge(pe_abc, h + 1)
                v.tensor_copy(dst[:, :], proj[h][:, :]).then_inc(v_abc, 1)

            def x_stats(m):
                dve.wait_ge(x_in, 16 * m + 16)
                for s in range(SUB):
                    v.bn_stats(bst[:, s, :], xln[:, s, :]).then_inc(ln_st, 1)
                for s in range(SUB):
                    dve.wait_ge(ln_st, 4 * m + s + 1)
                    settle(dve, v_own)
                    v.bn_aggr(mv[:, s, :], bst[:, s, :]).then_inc(ln_mv, 1)
                dve.wait_ge(ln_mv, 4 * m + 4)
                v.tensor_scalar(ve[:, :], mv[:, :, 1], LN_EPS, None, ALU.add).then_inc(ln_ve, 1)

            def x_scales(m):
                dve.wait_ge(ln_rstd, m + 1)
                v.tensor_scalar(xsc[:, :], rstd[:, :], X_UP, None, ALU.mult).then_inc(ln_sc, 1)
                v.scalar_tensor_tensor(xnb[:, :], mv[:, :, 0], -X_UP, rstd[:, :], ALU.mult, ALU.mult).then_inc(ln_sc, 1)

            def xT_out(m, soff, s):
                dve.wait_ge(pe_t, 4 * m + s + 1 + 2)
                dst = xT[:, ds(soff, XS)].rearrange("p (a n) -> p a n", n=TOK)[:, :, s * P:(s + 1) * P]
                v.tensor_scalar(dst, t16, 1.0, None, ALU.mult).then_inc(t_ev, 1)

            x_stats(0)
            x_scales(0)
            for s in range(SUB):
                xT_out(0, 0, s)

            def split_low(u, h4, g):
                dve.wait_ge(a_sq, h4 + g + 1)
                v.scalar_tensor_tensor(qkT[:, 1, g, :], proj[g % 2][:, :], QK_DOWN, qkT[:, 0, g, :], ALU.mult,
                                       ALU.subtract).then_inc(p_free, 1)

            def square_low(h4, g):
                dve.wait_ge(g_sqh, h4 + g + 1)
                v.scalar_tensor_tensor(sql[:, g, :], sqh[:, g, :], -SQ_LIFT, sqL[:, g % 2, :], ALU.mult,
                                       ALU.add).then_inc(v_sql, 1)

            def sums_out(r):
                dve.wait_ge(pe_ssq, r + 1)
                v.tensor_scalar(ssb[:, :], small[:, 0:SUB * HEADS], 2.0 ** -100, None, ALU.max).then_inc(v_ssb, 1)

            def roots(r):
                done = snap(dve, ROOT_STEPS * r)

                def after(k):
                    dve.wait_ge(v_rt1, done + k)

                dve.wait_ge(v_ssb, r + 1)
                v.tensor_scalar(rt_t[:, :].bitcast(I32), ssb[:, :].bitcast(I32), 1, None,
                                ALU.logical_shift_right).then_inc(v_rt1, 1)
                after(1)
                v.tensor_scalar(rt_y[:, :].bitcast(I32), rt_t[:, :].bitcast(I32), -1, 0x5F3759DF, ALU.mult,
                                ALU.add).then_inc(v_rt1, 1)
                for k in range(3):
                    after(2 + 3 * k)
                    v.tensor_tensor(rt_t[:, :], rt_y[:, :], rt_y[:, :], ALU.mult).then_inc(v_rt1, 1)
                    after(3 + 3 * k)
                    v.scalar_tensor_tensor(rt_t[:, :], rt_t[:, :], -0.5, ssb[:, :], ALU.mult,
                                           ALU.mult).then_inc(v_rt1, 1)
                    after(4 + 3 * k)
                    v.scalar_tensor_tensor(rt_y[:, :], rt_t[:, :], 1.5, rt_y[:, :], ALU.add,
                                           ALU.mult).then_inc(v_rt1, 1)
                after(ROOT_STEPS)
                v.tensor_tensor(rsb[:, :], ssb[:, :], rt_y[:, :], ALU.mult).then_inc(v_root, 1)

            def v_out(n, u, s):
                dve.wait_ge(p_full, u + 4 + s + 1)
                dve.wait_ge(pe_kv, 4 * n + s + 1)
                v.tensor_scalar(vv[:, s, :, 0:2 * DH], proj[s % 2][:, :].rearrange("p (h c) -> p h c", h=PAIRS),
                                QK_DOWN, None, ALU.mult).then_inc(p_free, 1)

            def k_minus_norm(n, f, s, h):
                dve.wait_ge(f_full, f + 2 * s + h + 1)
                dve.wait_ge(pe_kv, 4 * n + s + 3)
                v.tensor_tensor(kp[:, s % 2, h * D:(h + 1) * D].rearrange("p (h f) -> p h f", f=NF),
                                feat[h][:, :].rearrange("p (h f) -> p h f", f=NF),
                                bcast(nk[:, s * HEADS + 8 * h:s * HEADS + 8 * h + 8], NF),
                                ALU.subtract).then_inc(f_free, 1)

            def add_kv(n, first):
                dve.wait_ge(pe_kv, 4 * n + 4 + 4)
                dve.wait_ge(v_kva, 2 * n)
                for j in range(2):
                    w = kvs[0:VC, j * D:(j + 1) * D]
                    if first:
                        v.tensor_copy(w, kvbank[j][0:VC, :]).then_inc(v_kva, 1)
                    else:
                        v.tensor_tensor(w, kvbank[j][0:VC, :], w, ALU.add).then_inc(v_kva, 1)

            def norm_rows(n, r):
                dve.wait_ge(v_root, r + 1)
                dve.wait_ge(pe_nt, n)
                rs = rsb[:, :].rearrange("p (s h) -> p s h", s=SUB)
                v.tensor_scalar(nrm[:, :, 0:HEADS], rs, 64.0, None, ALU.mult).then_inc(v_nh, 1)
                dve.wait_ge(v_nh, n + 1)
                v.scalar_tensor_tensor(nrm[:, :, HEADS:2 * HEADS], rs, 64.0, nrm[:, :, 0:HEADS], ALU.mult,
                                       ALU.subtract).then_inc(v_nl, 1)

            def norms_out(n):
                dve.wait_ge(pe_nt, n + 1)
                v.tensor_copy(nrmT[:, :], t16[:, 0:SUB, :].rearrange("p s n -> p (s n)")).then_inc(v_nt, 1)

            def kv_blocks(b, f):
                dve.wait_ge(g_o, 16 * b + 2)
                v.memset(kvb[:, :, :], 0.0).then_inc(v_kvb0, 1)
                dve.wait_ge(v_kvb0, b + 1)
                for j in range(2):
                    dve.wait_ge(f_full, f - 2 + j + 1)
                    src = feat[j][:, 0:4 * 66].rearrange("p (a c) -> p a c", c=66)
                    d = kvb[:, 4 * j:4 * j + 4, :]
                    for h in range(2):
                        r = slice(64 * h, 64 * h + 64)
                        v.tensor_copy(d[r, :, h * DH:(h + 1) * DH], src[r, :, h * DH:(h + 1) * DH])
                        ins = v.tensor_copy(d[r, :, 64 + h * DH:64 + (h + 1) * DH], bcast(src[r, :, 64], DH))
                    ins.then_inc(f_free, 1)

            def out_rows(u, toff, s):
                dve.wait_ge(p_full, u + s + 1)
                v.scalar_tensor_tensor(S[:, ds(toff + s * D, D)], proj[s % 2][:, :], col(S_CO), bo_h[:, :], ALU.mult,
                                       ALU.add).then_inc(p_free, 1)

            def numerators(n, p):
                dve.wait_ge(pe_att, 8 * n + p + 1 + 2)
                h = 64 * (p % 2)
                v.tensor_copy(at32[h:h + 64, (p // 2) % 2, :], attbank[p % 2][0:64, :]).then_inc(v_num, 1)

            def reciprocals(n, g):
                dve.wait_ge(a_dn, 8 * n + 2 * g + 2 + 2)
                v.transpose(dT, dn[:, g % 2, :]).then_inc(v_dt, 1)
                dve.wait_ge(v_dt, 4 * n + g + 1)
                v.reciprocal(rT, dT.rearrange("p (c r) -> p c r", r=32)[:, :, 0]).then_inc(v_rt, 1)
                dve.wait_ge(v_rt, 4 * n + g + 1)
                v.transpose(dn[:, g % 2, :].rearrange("p (c r) -> p c r", r=32), bcast(rT, 32)).then_inc(v_rr, 1)

            def attention_low(n, g):
                dve.wait_ge(g_ah, 4 * n + g + 1)
                v.tensor_tensor(attT[:, 1, g, :], at32[:, g % 2, :], attT[:, 0, g, :], ALU.subtract).then_inc(v_al, 1)

            def q_tile(b, t, n, u, f, first, last):
                h4 = 32 * b + 16 + 4 * t
                r = 8 * b + 4 + t
                for g in range(0 if first else 2, KD):
                    split_low(u, h4, g)
                    if g:
                        square_low(h4, g - 1)
                    if g == 2 and not first:
                        attention_low(n - 1, 3)
                square_low(h4, KD - 1)
                toff = t * SUB * D - SUB * D
                if first:
                    kv_blocks(b, f)
                else:
                    out_rows(u + 4, toff, 0)
                sums_out(r)
                if not first:
                    out_rows(u + 4, toff, 1)
                roots(r)
                norm_rows(n, r)
                if not first:
                    out_rows(u + 4, toff, 2)
                    out_rows(u + 4, toff, 3)
                norms_out(n)
                un = snap(dve, u + (4 if first else 8))
                for p in range(PAIRS):
                    numerators(n, p)
                    if p == PAIRS - 2 and not last:
                        split_low(un, h4 + 4, 0)
                    if p % 2:
                        reciprocals(n, p // 2)
                    if p % 2 == 0 and 0 < p < PAIRS - 2:
                        attention_low(n, p // 2 - 1)
                attention_low(n, 2)
                if not last:
                    split_low(un, h4 + 4, 1)
                    square_low(h4 + 4, 0)

            def ffn_step(g0, j, i, between=None):
                w = wn[:, ds(j, 1)]
                dve.wait_ge(a_g, g0 + 3)
                dve.wait_ge(pe_dn, g0 + 1)
                v.tensor_scalar(gh[:, i, :], gbuf[:, i, :], w, None, ALU.mult).then_inc(v_gh, 1)
                dve.wait_ge(v_gh, g0 + 1)
                v.scalar_tensor_tensor(gl[:, i, :], gbuf[:, i, :], w, gh[:, i, :], ALU.mult,
                                       ALU.subtract).then_inc(v_gl, 1)
                if between is not None:
                    between()
                    dve.wait_ge(a_gsq, g0 + 1)
                    v.tensor_scalar(accs, gsq[:, i, :], 1.0, None, ALU.mult).then_inc(v_accs, 1)
                else:
                    dve.wait_ge(a_gsq, g0 + 1)
                    dve.wait_ge(v_accs, g0 + 2)
                    v.tensor_tensor(accs, accs, gsq[:, i, :], ALU.add).then_inc(v_accs, 1)

            def split_sums(n):
                dve.wait_ge(pe_st, n)
                dve.wait_ge(g_accg, 16 * n + 16 + 2)
                v.tensor_scalar(accp[:, 0, :], accg, 1.0, None, ALU.mult).then_inc(v_aph, 1)
                dve.wait_ge(v_accs, 16 * n + 16 + 2)
                v.tensor_scalar(accp[:, 2, :], accs, SQSUM_DOWN, None, ALU.mult).then_inc(v_aph, 1)
                dve.wait_ge(v_aph, 2 * n + 1)
                v.tensor_tensor(accp[:, 1, :], accg, accp[:, 0, :], ALU.subtract).then_inc(v_apl, 1)
                dve.wait_ge(v_aph, 2 * n + 2)
                v.scalar_tensor_tensor(accp[:, 3, :], accs, SQSUM_DOWN, accp[:, 2, :], ALU.mult,
                                       ALU.subtract).then_inc(v_apl, 1)

            def ffn_stats(n):
                dve.wait_ge(pe_st, n + 1)
                q = small[:, 0:2 * SUB].rearrange("p (s q) -> p s q", q=2)
                v.tensor_scalar(nm[:, :], q[:, :, 0], -1.0 / HID, None, ALU.mult).then_inc(v_st, 1)
                v.tensor_scalar(e2[:, :], q[:, :, 1], 1.0 / (SQSUM_DOWN * HID), LN_EPS, ALU.mult,
                                ALU.add).then_inc(v_st, 1)
                dve.wait_ge(v_st, 2 * n + 2)
                v.scalar_tensor_tensor(mm[:, :], nm[:, :], -1.0, nm[:, :], ALU.mult, ALU.mult).then_inc(v_s3, 1)
                dve.wait_ge(v_s3, n + 1)
                v.tensor_tensor(mm[:, :], mm[:, :], e2[:, :], ALU.add).then_inc(v_s4, 1)
                dve.wait_ge(v_s4, n + 1)
                v.tensor_scalar(fv[:, :], mm[:, :], LN_EPS, None, ALU.max).then_inc(v_s5, 1)

            def ffn_scale(n):
                dve.wait_ge(g_rs, n + 1)
                v.tensor_scalar(fr[:, :], frs[:, :], col(S_CR), None, ALU.mult).then_inc(v_fr, 1)

            def y_rows(e, q, n=None):
                y = yb[:, ds(q, 1), :].rearrange("p a d -> p (a d)")
                dve.wait_ge(a_yb, (e + 1 if n is None else 4 * n) + 4)
                v.scalar_tensor_tensor(y, A_bc[:, :], nm[:, ds(q, 1)], y, ALU.mult, ALU.add).then_inc(v_y1, 1)
                dve.wait_ge(v_y1, e + 1)
                v.scalar_tensor_tensor(y, y, fr[:, ds(q, 1)], B_bc[:, :], ALU.mult, ALU.add).then_inc(v_y, 1)

            def silu_rows(e, q):
                y = yb[:, ds(q, 1), :].rearrange("p a d -> p (a d)")
                dve.wait_ge(a_th, e + 1)
                v.scalar_tensor_tensor(y, th, 1.0, y, ALU.add, ALU.mult).then_inc(v_u, 1)

            def ffn_tile(n, prev, stats=False):
                g0 = snap(dve, 16 * n)

                def sums_before():
                    if prev:
                        split_sums(n - 1)
                    dve.wait_ge(v_apl, 2 * n)

                ffn_step(g0, 0, 0, sums_before)
                if prev:
                    ffn_stats(n - 1)
                ffn_step(g0 + 1, 1, 1)
                if prev:
                    ffn_scale(n - 1)
                with dve.Fori(0, 2) as q:
                    for i in range(6):
                        ffn_step(g0 + 6 * q + 2 + i, 6 * q + 2 + i, i % 2)
                        if prev:
                            r = 2 * q + i // 4
                            if i == 2:
                                dve.wait_ge(v_fr, n)
                            if i in (2, 4):
                                y_rows(4 * n - 4 + r, r)
                            if i in (3, 5):
                                silu_rows(4 * n - 4 + r, r)
                if stats:
                    x_stats(n + 2)
                for i in range(2):
                    ffn_step(g0 + NJ - 2 + i, NJ - 2 + i, i)

            def kv_tile(b, t, n, after_ffn=False):
                u = snap(dve, b * PU + t * 8)
                f = snap(dve, b * FU + t * 8)
                r = 8 * b + t
                h4 = 32 * b + 4 * t
                soff = snap(dve, ((n + 1) % SLOTS) * XS)
                e = 4 * n - 4
                if after_ffn:
                    split_sums(n - 1)
                    dve.wait_ge(v_apl, 2 * n)
                    dve.wait_ge(pe_dn, 16 * n + 2)
                    settle(dve, v_own)
                if isinstance(t, int):
                    v.memset(vv[:, :, :, 2 * DH], 1.0)
                if after_ffn:
                    x_scales(n + 1)
                else:
                    x_stats(n + 1)
                for g in range(KD):
                    if after_ffn and g > 1:
                        square_low(h4, g - 2)
                    split_low(u, h4, g)
                    if after_ffn:
                        if g == 0:
                            ffn_stats(n - 1)
                        if g == 1:
                            ffn_scale(n - 1)
                            dve.wait_ge(v_fr, n)
                            settle(dve, v_own)
                            y_rows(e, 0, n)
                        if g > 1:
                            silu_rows(e + g - 2, g - 2)
                            y_rows(e + g - 1, g - 1, n)
                    else:
                        if g == 1:
                            x_scales(n + 1)
                        if g:
                            square_low(h4, g - 1)
                if after_ffn:
                    square_low(h4, KD - 2)
                square_low(h4, KD - 1)
                if after_ffn:
                    silu_rows(e + 2, 2)
                    y_rows(e + 3, 3, n)
                v_out(n, u, 0)
                if after_ffn:
                    silu_rows(e + 3, 3)
                v_out(n, u, 1)
                sums_out(r)
                roots(r)
                v_out(n, u, 2)
                dve.wait_ge(v_root, r + 1)
                v.tensor_scalar(nk[:, :], rsb[:, :], col(S_NK), None, ALU.mult).then_inc(v_nk, 1)
                v_out(n, u, 3)
                dve.wait_ge(v_nk, n + 1)
                for s in range(SUB):
                    for h in range(2):
                        k_minus_norm(n, f, s, h)
                    xT_out(n + 1, soff, s)
                add_kv(n, isinstance(t, int))

            def row(b, last):
                n0 = snap(dve, b * TB)
                n3 = snap(dve, b * TB + TB - 1)
                with dve.Fori(1, TB) as t:
                    kv_tile(b, t, snap(dve, b * TB + t))
                q_tile(b, 0, n0, snap(dve, b * PU + 32), snap(dve, b * FU + 34), True, False)
                with dve.Fori(1, TB - 1) as t:
                    q_tile(b, t, snap(dve, b * TB + t), snap(dve, b * PU + 28 + t * 8), snap(dve, b * FU + 34 + t * 8),
                           False, False)
                t = TB - 1
                q_tile(b, t, n3, snap(dve, b * PU + 28 + t * 8), snap(dve, b * FU + 34 + t * 8), False, True)
                attention_low(n3, 3)
                for s in range(SUB):
                    out_rows(snap(dve, b * PU + 60), 3 * SUB * D, s)
                ffn_tile(n0, False)
                with dve.Fori(1, TB - 1) as t:
                    ffn_tile(snap(dve, b * TB + t), True)
                ffn_tile(n3, True, stats=not last)
                if last:
                    split_sums(n3)
                    ffn_stats(n3)
                    ffn_scale(n3)
                    dve.wait_ge(v_fr, n3 + 1)
                    for q in range(SUB):
                        y_rows(16 * b + 12 + q, q, n3 + 1)
                        silu_rows(16 * b + 12 + q, q)
                else:
                    kv_tile(snap(dve, b + 1), 0, snap(dve, n0 + TB), after_ffn=True)

            kv_tile(0, 0, 0)
            with dve.Fori(0, B - 1) as b:
                row(b, False)
            row(B - 1, True)


def bcast(ap, n):
    return ap.unsqueeze(len(ap.shape)).broadcast_to([*ap.shape, n])


_INS = ["L0_attn_x", "L0_attn_w_qkv", "L0_attn_w_out", "L0_attn_b_out", "L0_attn_random_features", "L0_ffn_W_fc",
        "L0_ffn_ln_w", "L0_ffn_ln_b", "L0_ffn_W_proj"]


def kernel(**inputs):
    import numpy as _np
    import concourse.bacc as _bacc
    from concourse import mybir as _mybir
    from concourse.bass_utils import run_bass_kernel_spmd as _run

    nc = _bacc.Bacc("TRN2", target_bir_lowering=False, num_devices=1)
    arrays, args = {}, []
    for name in _INS:
        a = _np.asarray(inputs[name])
        if a.ndim == 2:
            a = a.T
        elif name.startswith("L0_ffn_ln"):
            a = a.reshape(NJ, P).T
        arrays[f"in_{name}"] = _np.ascontiguousarray(a)
    arrays.update(setup_constants())
    for name, a in arrays.items():
        args.append(nc.dram_tensor(name, a.shape, _mybir.dt.from_np(a.dtype), kind="ExternalInput").ap())
    args.append(nc.dram_tensor("out_0", (B, SEQ, D), F32, kind="ExternalOutput").ap())
    build_program(nc, *args)
    r = _run(nc, [arrays], core_ids=[0])
    return r.results[0]["out_0"]
```

```python
from contextlib import ExitStack

import numpy as np

import concourse.bass as bass
from concourse import mybir

F32 = mybir.dt.float32
F16 = mybir.dt.float16
BF16 = mybir.dt.bfloat16
I32 = mybir.dt.int32
ALU = mybir.AluOpType
ACT = mybir.ActivationFunctionType
AX = mybir.AxisListType
ABSMAX = bass.bass_isa.ReduceOp.max

P = 128
D = 512
KD = D // P
HEADS = 16
DH = D // HEADS
NF = 64
HID = 2048
NJ = HID // P
B, SEQ = 4, 2048
TOK = 512
SUB = TOK // P
TB = SEQ // TOK
PAIRS = HEADS // 2
SLOTS = 5
XS = 2 * KD * TOK
LN_EPS = 1e-5
VC = 65
GAMMA_EPS = 1e-6
DEN_EPS = 1e-6

X_UP = 2.0 ** 8
W_UP = 2.0 ** 8
QK_DOWN = 2.0 ** -11
SQ_DOWN = 2.0 ** -13
SQ_LIFT = 2.0 ** 12
G_UP = 2.0 ** 5
SQSUM_DOWN = 2.0 ** -7


def setup_constants():
    ident = np.eye(P, dtype=np.float32)
    sel = np.zeros((P, PAIRS * P), np.float32)
    for part in range(2):
        for h in range(HEADS):
            sel[part * HEADS + h, h * NF:(h + 1) * NF] = 1.0
    heads = np.zeros((P, 2 * KD), np.float32)
    for p in range(P):
        heads[p, p // DH] = 1.0
        heads[p, KD + p // DH] = 1.0 / SQ_LIFT
    pick = np.zeros((6, 2 * P), np.float32)
    pick[0:3, 0:P] = 1.0
    pick[3:6, P:] = 1.0
    return {"c_ident": ident, "c_sel": sel, "c_heads": heads, "c_pick": pick}


def build_program(nc, x, w_qkv, w_out, b_out, rf, w_fc, ln_w, ln_b, w_proj, c_ident, c_sel, c_heads, c_pick, out):
    ds = bass.ds
    x_v = x.rearrange("b (t s p) d -> (b t) p s d", s=SUB, p=P)
    out_v = out.rearrange("b (t s p) d -> (b t) p s d", s=SUB, p=P)

    with ExitStack() as ctx:
        def sb(name, shape, dt):
            return ctx.enter_context(nc.sbuf_tensor(name, shape, dt))

        def sem(name):
            return ctx.enter_context(nc.semaphore(name))

        xT = sb("xT", [P, SLOTS * XS], F16)
        wqkv = sb("wqkv", [P, 2, KD, 3 * D], F16)
        wo = sb("wo", [P, 2, KD, D], F16)
        wfc = sb("wfc", [P, KD, HID], BF16)
        wpj = sb("wpj", [P, NJ, D], BF16)
        S = sb("S", [P, TB * SUB * D], F32)
        A_bc = sb("A_bc", [P, D], F32)
        B_bc = sb("B_bc", [P, D], F32)
        bo_h = sb("bo_h", [P, D], F32)
        rfb = sb("rfb", [P, 2, 4 * NF], F16)
        nsel = sb("nsel", [P, PAIRS, P], BF16)
        heads16 = sb("heads16", [P, 2 * KD], F16)
        ident16 = sb("ident16", [P, P], F16)
        ident32 = sb("ident32", [P, P], F32)
        ones16 = sb("ones16", [P, 2], F16)
        wn = sb("wn", [P, NJ], F32)
        sc = sb("sc", [P, 16], F32)
        S_W, S_O, S_RF, S_E, S_NK, S_NS, S_CO, S_CR = range(8)
        col = lambda i: sc[:, i:i + 1]

        ARENA = 37376
        arena = sb("arena", [P, ARENA // 4], F32)

        def at(off, n, dt=F32):
            size = 4 if dt in (F32, I32) else 2
            v = arena[:, off // 4:(off + n * size) // 4]
            return v if dt == F32 else v.bitcast(dt)

        R = 0
        kp = at(R, 2 * 2 * D * 1).rearrange("p (a n) -> p a n", a=2)
        vv = at(R + 8192, SUB * PAIRS * VC).rearrange("p (s h c) -> p s h c", s=SUB, c=VC)
        qp = at(R, 2 * TOK).rearrange("p (a n) -> p a n", a=2)
        dn = at(R + 4096, 2 * TOK).rearrange("p (a n) -> p a n", a=2)
        dT = at(R + 8192, TOK)
        at32 = at(R + 10240, 2 * TOK).rearrange("p (a n) -> p a n", a=2)
        rT = at(R + 14336, SUB * 4)
        gh = at(R + 8192, 2 * TOK, F16).rearrange("p (a n) -> p a n", a=2)
        gl = at(R + 10240, 2 * TOK, F16).rearrange("p (a n) -> p a n", a=2)
        KVQ = 16640
        qkT = at(KVQ, 2 * KD * TOK, F16).rearrange("p (a g n) -> p a g n", a=2, g=KD)
        sqL = at(KVQ + 8192, 2 * TOK).rearrange("p (a n) -> p a n", a=2)
        sqh = at(KVQ + 12288, KD * TOK, F16).rearrange("p (g n) -> p g n", g=KD)
        sql = at(KVQ + 16384, KD * TOK, F16).rearrange("p (g n) -> p g n", g=KD)
        gbuf = at(KVQ, 2 * TOK).rearrange("p (a n) -> p a n", a=2)
        accg = at(KVQ + 4096, TOK)
        accs = at(KVQ + 6144, TOK)
        gsq = sqL
        accp = sqh
        xln = S[:, 0:SUB * D].rearrange("p (s n) -> p s n", s=SUB)
        xat = sb("xat", [P, SUB, D], F32)
        attT = xat[:, :, :].bitcast(F16).rearrange("p (a b) n -> p a (b n)", a=2).rearrange(
            "p a (g n) -> p a g n", g=KD)
        yb = xat
        xhl = sb("xhl", [P, 2, 2, D], F16)
        kvs = sb("kvs", [P, PAIRS * P], F32)
        th = kvs[:, 0:D]
        kvb = sb("kvb", [P, PAIRS, P], F32)
        xres = kvb[:, :, :].rearrange("p a b -> p (a b)").rearrange("p (a n) -> p a n", a=2)
        nrm = sb("nrm", [P, SUB, P], F16)
        nrmT = sb("nrmT", [P, TOK], F16)
        ssb = sb("ssb", [P, SUB * HEADS], F32)
        rsb = sb("rsb", [P, SUB * HEADS], F32)
        nk = sb("nk", [P, SUB * HEADS], F32)
        rt_y = sb("rt_y", [P, SUB * HEADS], F32)
        rt_t = sb("rt_t", [P, SUB * HEADS], F32)
        mhalf = sb("mhalf", [P, SUB], F32)
        bst = sb("bst", [P, SUB, 6], F32)
        mv = sb("mv", [P, SUB, 2], F32)
        ve = sb("ve", [P, SUB], F32)
        rstd = sb("rstd", [P, SUB], F32)
        xsc = sb("xsc", [P, SUB], F32)
        xnb = sb("xnb", [P, SUB], F32)
        nm = sb("nm", [P, SUB], F32)
        e2 = sb("e2", [P, SUB], F32)
        mm = sb("mm", [P, SUB], F32)
        fv = sb("fv", [P, SUB], F32)
        frs = sb("frs", [P, SUB], F32)
        fr = sb("fr", [P, SUB], F32)
        region = [S[:, (c + 1) * SUB * D:(c + 2) * SUB * D] for c in range(3)] + [
            xat[:, :, :].rearrange("p s n -> p (s n)")]
        mx = sb("mx", [P, 4], F32)
        mq = sb("mq", [P, 3], F32)
        gm = sb("gm", [P, 4], F32)
        pw = sb("pw", [P, 4], F32)
        ip = sb("ip", [P, 4], F32)
        gsum = sb("gsum", [P, 2], F32)
        thr = sb("thr", [P, 2], F32)
        nthr = sb("nthr", [P, 2], F32)
        ones32 = sb("ones32", [P, P], F32)
        flat = kvb[:, :, :].rearrange("p a b -> p (a b)")
        ab6 = flat[0:6, 0:D]
        pick = flat[0:6, D:D + 2 * P].rearrange("p (a n) -> p a n", a=2)
        lnwb = flat[:, 768:768 + 2 * NJ].rearrange("p (a j) -> p a j", a=2)
        lnr = flat[:, 800:800 + 2 * NJ].rearrange("p (a j) -> p a j", a=2)
        lnp = flat[:, 832:832 + 3 * NJ].bitcast(BF16).rearrange("p (j c) -> p j c", c=6)
        heads32 = flat[:, 880:880 + 2 * KD]
        gpart = flat[:, 896:896 + 2 * NJ].rearrange("p (a n) -> p a n", a=2)
        sel32 = at(KVQ + 16384, PAIRS * P).rearrange("p (a b) -> p a b", a=PAIRS)
        rfT = at(R, NF)
        ternary = (wfc[:, :, :].rearrange("p k n -> p (k n)"), wpj[:, :, :].rearrange("p j n -> p (j n)"))
        RG = SUB * D

        ps = [ctx.enter_context(nc.psum_tensor(f"bank{i}", [P, 512], F32)) for i in range(8)]
        kvbank = ps[0:2]
        attbank = ps[0:2]
        small = ps[2]
        proj = ps[3:5]
        feat = ps[5:7]
        tbank = ps[7]
        down = [ps[0], ps[1], ps[3], ps[4]]
        t16 = tbank[:, :].bitcast(F16).rearrange("p (a n) -> p a n", n=P)

        ld = [sem(f"ld_region{c}") for c in range(4)]
        ld_small, ld_rest = sem("ld_small"), sem("ld_rest")
        v_set = sem("v_set")
        g_const = sem("g_const")
        v_max, g_max, v_scale = sem("v_max"), sem("g_max"), sem("v_scale")
        a_gpart, v_gsum, pe_gsum, v_thr = sem("a_gpart"), sem("v_gsum"), sem("pe_gsum"), sem("v_thr")
        a_whi, v_wlo, v_neg, v_tern = sem("a_whi"), sem("v_wlo"), sem("v_neg"), sem("v_tern")
        pe_ab, v_ab, pe_abc, v_abc = sem("pe_ab"), sem("v_ab"), sem("pe_abc"), sem("v_abc")
        x_in, ln_st, ln_mv, ln_ve, ln_rstd = sem("x_in"), sem("ln_st"), sem("ln_mv"), sem("ln_ve"), sem("ln_rstd")
        ln_sc, ln_xn, ln_hi, ln_lo = sem("ln_sc"), sem("ln_xn"), sem("ln_hi"), sem("ln_lo")
        pe_t, t_ev = sem("pe_t"), sem("t_ev")
        p_full, p_free = sem("p_full"), sem("p_free")
        a_hi, a_sq, g_sqh, v_sql = sem("a_hi"), sem("a_sq"), sem("g_sqh"), sem("v_sql")
        pe_ssq, v_ssb, v_rt1, v_root, v_nk = sem("pe_ssq"), sem("v_ssb"), sem("v_rt1"), sem("v_root"), sem("v_nk")
        f_full, f_free, a_kp = sem("f_full"), sem("f_free"), sem("a_kp")
        pe_kv, v_kva = sem("pe_kv"), sem("v_kva")
        v_kvb0 = sem("v_kvb0")
        v_nh, v_nl, pe_nt, v_nt = sem("v_nh"), sem("v_nl"), sem("pe_nt"), sem("v_nt")
        pe_att, a_dn, v_num = sem("pe_att"), sem("a_dn"), sem("v_num")
        v_dt, v_rt, v_rr, g_mul, g_ah, v_al = (sem("v_dt"), sem("v_rt"), sem("v_rr"), sem("g_mul"), sem("g_ah"),
                                               sem("v_al"))
        pe_fc, a_g, a_gsq = sem("pe_fc"), sem("a_g"), sem("a_gsq")
        v_gh, v_gl, v_accs, g_accg = sem("v_gh"), sem("v_gl"), sem("v_accs"), sem("g_accg")
        pe_dn, a_yb, v_aph, v_apl, pe_st = sem("pe_dn"), sem("a_yb"), sem("v_aph"), sem("v_apl"), sem("pe_st")
        v_st, v_s3, v_s4, v_s5, g_rs, v_fr = (sem("v_st"), sem("v_s3"), sem("v_s4"), sem("v_s5"), sem("g_rs"),
                                              sem("v_fr"))
        v_y1, v_y, a_th, v_u, g_us, g_o = sem("v_y1"), sem("v_y"), sem("a_th"), sem("v_u"), sem("g_us"), sem("g_o")
        v_us = sem("v_us")
        xr_in, o_out = sem("xr_in"), sem("o_out")
        sp_own, a_own, g_own, v_own = sem("sp_own"), sem("a_own"), sem("g_own"), sem("v_own")
        block = ctx.enter_context(nc.Block())

        def snap(engine, value):
            return value if isinstance(value, int) else engine.snap(value)

        def settle(engine, own):
            engine.sem_inc(own, 1)

        PU, FU = 64, 66

        ROOT_STEPS = 11

        @block.sync
        def _(sp):
            sp.dma_start(xln, x_v[0]).then_inc(x_in, 16)
            for dst, src in ((ident32[:, :], c_ident), (heads32, c_heads), (lnwb[:, 0, :], ln_w),
                             (lnwb[:, 1, :], ln_b)):
                sp.dma_start(dst, src).then_inc(ld_small, 16)
            for h in range(4):
                sp.dma_start(rfT[h * DH:(h + 1) * DH, :], rf).then_inc(ld_small, 16)
            for c in (1, 2, 0):
                sp.dma_start(region[c].rearrange("p (k n) -> p k n", k=KD), w_qkv[:, c * D:(c + 1) * D].rearrange(
                    "(k p) n -> p k n", p=P)).then_inc(ld[c], 16)
            sp.dma_start(region[3].rearrange("p (k n) -> p k n", k=KD),
                         w_out.rearrange("(k p) n -> p k n", p=P)).then_inc(ld[3], 16)
            sp.dma_start(sel32, c_sel.rearrange("p (a b) -> p a b", a=PAIRS)).then_inc(ld_rest, 16)
            sp.dma_start(bo_h[:, :], b_out.rearrange("(a d) -> a d", a=1).partition_broadcast(P)).then_inc(ld_rest, 16)
            sp.dma_start(pick, c_pick.rearrange("q (a p) -> q a p", a=2)).then_inc(ld_rest, 16)

            def load_x(m):
                src = snap(sp, m % (B * TB))
                sp.wait_ge(ln_lo, 4 * m)
                sp.dma_start(xln, x_v[ds(src, 1)].rearrange("a p s d -> p (a s) d")).then_inc(x_in, 16)

            def ffn_io(n, load_next=None):
                for s in range(SUB):
                    sp.wait_ge(g_o, 4 * n + s + 1)
                    settle(sp, sp_own)
                    sp.wait_ge(xr_in, 64 * n + 16 * s + 1)
                    sp.dma_start(xres[:, s % 2, :], x_v[ds(n, 1), :, s, :].rearrange(
                        "a p d -> p (a d)")).then_inc(xr_in, 16)
                    if load_next is not None and s == SUB - 1:
                        load_x(load_next)
                    if s:
                        sp.wait_ge(g_o, 4 * n + s + 2)
                        sp.dma_start(out_v[ds(n, 1), :, s - 1, :].rearrange("a p d -> p (a d)"),
                                     yb[:, s - 1, :]).then_inc(o_out, 16)
                sp.wait_ge(g_o, 4 * n + 4 + 2)
                sp.dma_start(out_v[ds(n, 1), :, SUB - 1, :].rearrange("a p d -> p (a d)"),
                             yb[:, SUB - 1, :]).then_inc(o_out, 16)

            def row(b, last):
                sp.wait_ge(pe_att, 32 * b + 32 + 2)
                settle(sp, sp_own)
                n0 = snap(sp, b * TB)
                ffn_io(n0)
                if not last:
                    load_x(snap(sp, n0 + TB + 1))
                with sp.Fori(1, TB - 1) as t:
                    ffn_io(snap(sp, b * TB + t))
                ffn_io(snap(sp, n0 + TB - 1), None if last else snap(sp, n0 + TB + 2))
                if not last:
                    with sp.Fori(2, TB) as t:
                        load_x(snap(sp, n0 + TB + t + 1))

            for t in range(TB):
                load_x(t + 1)
                if t == 0:
                    for i, c in enumerate((1, 2, 0, 3)):
                        sp.wait_ge(v_wlo, i + 1)
                        sp.dma_start(region[c], w_fc[c * P:(c + 1) * P, :]).then_inc(ld[c], 16)
                if t == 2:
                    for c in range(4):
                        sp.wait_ge(v_tern, c + 1)
                        sp.dma_start(region[c].rearrange("p (j n) -> p j n", j=4), w_proj[4 * c * P:4 * (c + 1) * P, :]
                                     .rearrange("(j p) n -> p j n", p=P)).then_inc(ld[c], 16)
            sp.wait_ge(v_abc, 2)
            with sp.Fori(0, B - 1) as b:
                row(b, False)
            row(B - 1, True)
            sp.wait_ge(o_out, 64 * B * TB + 1)

        @block.tensor
        def _(pe):
            def mm(o, lhsT, rhs, start, stop, **kw):
                return nc.tensor.matmul(o, lhsT, rhs, start=start, stop=stop, skip_group_check=True, **kw)

            def weight_mean(q):
                pe.wait_ge(g_const, 1)
                pe.wait_ge(v_gsum, q + 1)
                mm(small[:, 80 + q:81 + q], ones32[:, :], gsum[:, q:q + 1], True, True).then_inc(pe_gsum, 1)

            def layer_norm_rows():
                pe.wait_ge(v_tern, 8)
                pe.wait_ge(v_ssb, TB)
                for j in range(NJ):
                    i = mm(small[0:6, :], lnp[:, j, :], wpj[:, j, :], j == 0, j == NJ - 1)
                i.then_inc(pe_ab, 1)
                for h in range(2):
                    pe.wait_ge(v_ab if h == 0 else v_abc, 1)
                    mm(small[:, :], pick[:, h, :], ab6, True, True).then_inc(pe_abc, 1)
                pe.wait_ge(v_abc, 2)

            def transpose_x(m, s):
                pe.wait_ge(ln_lo, 4 * m + s + 1)
                pe.wait_ge(t_ev, 4 * m + s)
                for a in range(2):
                    for k in range(KD):
                        i = nc.tensor.transpose(t16[:, a * KD + k, :], xhl[:, s % 2, a, k * P:(k + 1) * P],
                                                ident16[:, :])
                i.then_inc(pe_t, 1)

            for s in range(SUB):
                transpose_x(0, s)

            def xmov(off, a, k):
                return xT[:, ds(off + (a * KD + k) * TOK, TOK)]

            def project_T(u, off, first, groups=range(KD), banks=None):
                for g in groups:
                    if banks is not None and g < 2:
                        pe.wait_ge(a_yb, banks + g + 1)
                    pe.wait_ge(p_free, u + g + 1)
                    o = proj[g % 2][:, :]
                    for i, (wa, xa) in enumerate(((0, 0), (0, 1), (1, 0))):
                        for k in range(KD):
                            c0 = first + g * P
                            ins = mm(o, wqkv[:, wa, k, c0:c0 + P], xmov(off, xa, k), i == 0 and k == 0,
                                     i == 2 and k == KD - 1)
                    ins.then_inc(p_full, 1)

            def project_v(u, off, s):
                pe.wait_ge(p_free, u + 4 + s + 1)
                o = proj[s % 2][:, :]
                for i, (wa, xa) in enumerate(((0, 0), (1, 0), (0, 1))):
                    for k in range(KD):
                        ins = mm(o, xT[:, ds(off + (xa * KD + k) * TOK + s * P, P)], wqkv[:, wa, k, 2 * D:3 * D],
                                 i == 0 and k == 0, i == 2 and k == KD - 1)
                ins.then_inc(p_full, 1)

            def square_sums(h4, r):
                pe.wait_ge(v_sql, h4 + 4 + 2)
                pe.wait_ge(v_ssb, r)
                for s in range(SUB):
                    for g in range(KD):
                        o = small[:, s * HEADS + g * 4:s * HEADS + g * 4 + 4]
                        mm(o, sqh[:, g, s * P:(s + 1) * P], heads16[:, 0:4], True, False)
                        ins = mm(o, sql[:, g, s * P:(s + 1) * P], heads16[:, 4:8], False, True)
                ins.then_inc(pe_ssq, 1)

            def k_features(f, s, h):
                pe.wait_ge(f_free, f + 2 * s + h + 1)
                for g2 in range(2):
                    g = 2 * h + g2
                    o = feat[h][:, g2 * 4 * NF:(g2 + 1) * 4 * NF]
                    mm(o, qkT[:, 0, g, s * P:(s + 1) * P], rfb[:, 0, :], True, False)
                    mm(o, qkT[:, 1, g, s * P:(s + 1) * P], rfb[:, 0, :], False, False)
                    ins = mm(o, qkT[:, 0, g, s * P:(s + 1) * P], rfb[:, 1, :], False, True)
                ins.then_inc(f_full, 1)

            def kv_sums(n, u, s):
                pe.wait_ge(a_kp, 8 * n + 2 * s + 2)
                pe.wait_ge(p_free, u + 4 + s + 3)
                if s == 0:
                    pe.wait_ge(v_kva, 2 * n)
                for p in range(PAIRS):
                    ins = mm(kvbank[p // 4][0:VC, (p % 4) * P:(p % 4 + 1) * P], vv[:, s, p, :],
                             kp[:, s % 2, p * P:(p + 1) * P], s == 0 and p % 4 == 0, s == SUB - 1)
                ins.then_inc(pe_kv, 1)

            def out_project(u, n, s):
                pe.wait_ge(v_al, 4 * n + 4)
                pe.wait_ge(p_free, u + s + 1)
                for i, (wa, xa) in enumerate(((0, 0), (1, 0), (0, 1))):
                    for g in range(KD):
                        ins = mm(proj[s % 2][:, :], attT[:, xa, g, s * P:(s + 1) * P], wo[:, wa, g, :],
                                 i == 0 and g == 0, i == 2 and g == KD - 1)
                ins.then_inc(p_full, 1)

            def norms_T(n, b):
                pe.wait_ge(v_nl, n + 1)
                pe.wait_ge(t_ev, 16 * b + 20)
                pe.wait_ge(v_nt, n + 1)
                for s in range(SUB):
                    ins = nc.tensor.transpose(t16[:, s, :], nrm[:, s, :], ident16[:, :])
                ins.then_inc(pe_nt, 1)

            def q_feature(f, p):
                pe.wait_ge(f_free, f + p + 1)
                o = feat[p % 2][:, :]
                c0 = (p % 2) * P
                mm(o, rfb[:, 0, c0:c0 + P], qkT[:, 0, p // 2, :], True, False)
                mm(o, rfb[:, 0, c0:c0 + P], qkT[:, 1, p // 2, :], False, False)
                mm(o, rfb[:, 1, c0:c0 + P], qkT[:, 0, p // 2, :], False, False)

            def minus_norm(p):
                mm(feat[p % 2][:, :], nsel[:, p, :], nrmT[:, :], False, True).then_inc(f_full, 1)

            def attend(n, f, p):
                pe.wait_ge(f_free, f + p + 1 + 2)
                pe.wait_ge(v_num, 8 * n + p + 1)
                pe.wait_ge(a_dn, 8 * n + p + 1)
                mm(attbank[p % 2][:, :], kvb[:, p, :], qp[:, p % 2, :], True, True).then_inc(pe_att, 1)

            def q_tile(b, t, n, u, f, off, noff, first):
                if first:
                    for j in range(2):
                        project_T(u, off, 0, (j,))
                        pe.wait_ge(v_kva, 8 * b + 8)
                        pe.wait_ge(f_free, f - 2 + j + 1)
                        for p in range(4):
                            c0 = (4 * j + p) * P
                            ins = nc.tensor.transpose(feat[j][:, p * 66:p * 66 + VC], kvs[0:VC, c0:c0 + P],
                                                      ident32[0:VC, 0:VC])
                        ins.then_inc(f_full, 1)
                    project_T(u, off, 0, (2, 3))
                    project_T(u + 4, noff, 0, (0,))
                else:
                    project_T(u, off, 0, (1, 2, 3))
                    for s in (0, 1):
                        out_project(u + 4, n - 1, s)
                square_sums(32 * b + 4 * t + 16, 8 * b + t + 4)
                if first:
                    pe.wait_ge(f_free, f + 2)
                    q_feature(f, 0)
                    q_feature(f, 1)
                    norms_T(n, b)
                    pe.wait_ge(v_nt, n + 1 + 1)
                    minus_norm(0)
                    minus_norm(1)
                else:
                    for s in (2, 3):
                        out_project(u + 4, n - 1, s)
                    norms_T(n, b)
                    q_feature(f, 0)
                    pe.wait_ge(v_nt, n + 1 + 1)
                    minus_norm(0)
                    q_feature(f, 1)
                    minus_norm(1)
                for p in range(PAIRS):
                    if p == PAIRS - 1 and not first:
                        if noff is not None:
                            project_T(u + 8, noff, 0, (0,))
                        else:
                            pe.wait_ge(f_free, f + PAIRS - 1 + 2)
                            up(snap(pe, 16 * b * TB), snap(pe, ((b * TB) % SLOTS) * XS), 0, 0)
                    attend(n, f, p)
                    if p + 2 < PAIRS:
                        q_feature(f, p + 2)
                        minus_norm(p + 2)

            def up(g0, off, j, i):
                pe.wait_ge(a_g, g0 + 1)
                for k in range(KD):
                    for a in range(2):
                        ins = mm(feat[i][:, :], wfc[:, k, ds(j * P, P)], xmov(off, a, k), k == 0 and a == 0,
                                 k == KD - 1 and a == 1)
                ins.then_inc(pe_fc, 1)

            def down_step(g0, n, j, i, first=False, last=False, p_done=None):
                pe.wait_ge(v_gl, g0 + 1 + 2)
                for s in range(SUB):
                    if first:
                        pe.wait_ge(a_yb, 4 * n - 4 + s + 1 + 4)
                    if p_done is not None and s == 2:
                        pe.wait_ge(p_free, p_done)
                    mm(down[s][:, :], gh[:, i, s * P:(s + 1) * P], wpj[:, ds(j, 1), :], first, False)
                    ins = mm(down[s][:, :], gl[:, i, s * P:(s + 1) * P], wpj[:, ds(j, 1), :], False, last)
                ins.then_inc(pe_dn, 1)

            def ffn_sums(n):
                pe.wait_ge(v_apl, 2 * n + 2 + 1)
                pe.wait_ge(v_st, 2 * n + 1)
                for s in range(SUB):
                    for q in range(2):
                        o = small[:, 2 * s + q:2 * s + q + 1]
                        mm(o, accp[:, 2 * q, s * P:(s + 1) * P], ones16[:, 0:1], True, False)
                        ins = mm(o, accp[:, 2 * q + 1, s * P:(s + 1) * P], ones16[:, 0:1], False, True)
                ins.then_inc(pe_st, 1)

            def ffn_tile(n, off, noff, first, last, p_done=None):
                g0 = snap(pe, 16 * n)
                for i in range(2):
                    if not first:
                        up(g0 + i + 2, off, i + 2, i)
                    down_step(g0 + i, n, i, i, first=i == 0, p_done=p_done if i == 0 else None)
                    if i == 0 and not first:
                        ffn_sums(n - 1)
                with pe.Fori(1, NJ // 2 - 1) as jj:
                    j = 2 * jj
                    for i in range(2):
                        up(g0 + j + i + 2, off, j + i + 2, i)
                        down_step(g0 + j + i, n, j + i, i)
                for i in range(2):
                    if not last:
                        up(g0 + NJ + i, noff, i, i)
                    down_step(g0 + NJ - 2 + i, n, NJ - 2 + i, i, last=i == 1)
            def kv_tile(b, t, n, after_ffn=False, setup=None):
                u = snap(pe, b * PU + t * 8)
                f = snap(pe, b * FU + t * 8)
                off = snap(pe, (n % SLOTS) * XS)
                pe.wait_ge(t_ev, 4 * n + 4)
                if setup == 0:
                    pe.wait_ge(v_wlo, 1)
                if after_ffn:
                    project_T(u, off, D, (0,), banks=4 * n)
                    ffn_sums(n - 1)
                    project_T(u, off, D, (1, 2, 3), banks=4 * n)
                    pe.wait_ge(a_yb, 4 * n + 4)
                    pe.wait_ge(v_st, 2 * n + 1)
                else:
                    project_T(u, off, D)
                if setup == 0:
                    pe.wait_ge(v_wlo, 2)
                for s in range(2):
                    project_v(u, off, s)
                square_sums(32 * b + 4 * t, 8 * b + t)
                for s in (2, 3):
                    project_v(u, off, s)
                for s in range(SUB):
                    for h in range(2):
                        k_features(f, s, h)
                    transpose_x(n + 1, s)
                    if setup in (0, 2) and s == SUB - 1:
                        weight_mean(setup // 2)
                    if s:
                        kv_sums(n, u, s - 1)
                kv_sums(n, u, SUB - 1)

            def row(b, last):
                n0 = snap(pe, b * TB)
                q_tile(b, 0, n0, snap(pe, b * PU + 32), snap(pe, b * FU + 34), snap(pe, (n0 % SLOTS) * XS),
                       snap(pe, ((n0 + 1) % SLOTS) * XS), True)
                with pe.Fori(1, TB - 1) as t:
                    n = snap(pe, b * TB + t)
                    q_tile(b, t, n, snap(pe, b * PU + 28 + t * 8), snap(pe, b * FU + 34 + t * 8),
                           snap(pe, (n % SLOTS) * XS), snap(pe, ((n + 1) % SLOTS) * XS), False)
                n3 = snap(pe, b * TB + TB - 1)
                t = TB - 1
                q_tile(b, t, n3, snap(pe, b * PU + 28 + t * 8), snap(pe, b * FU + 34 + t * 8),
                       snap(pe, (n3 % SLOTS) * XS), None, False)
                pe.wait_ge(f_free, FU * b + FU + 2)
                off0 = snap(pe, (n0 % SLOTS) * XS)
                for i in range(1, 4):
                    up(16 * n0 + i, off0, i, i % 2)
                for s in range(SUB):
                    out_project(snap(pe, b * PU + 60), n3, s)
                pe.wait_ge(v_num, 32 * b + 32 + 2)
                pe.wait_ge(a_dn, 32 * b + 32 + 2)
                ffn_tile(n0, off0, snap(pe, ((n0 + 1) % SLOTS) * XS), True, False,
                         p_done=PU * b + PU + 2)
                with pe.Fori(1, TB - 1) as t:
                    n = snap(pe, b * TB + t)
                    ffn_tile(n, snap(pe, (n % SLOTS) * XS), snap(pe, ((n + 1) % SLOTS) * XS), False, False)
                ffn_tile_last = snap(pe, (n3 % SLOTS) * XS)
                ffn_tile(n3, ffn_tile_last, None, False, True)
                if last:
                    ffn_sums(n3)
                else:
                    kv_tile(snap(pe, b + 1), 0, snap(pe, n0 + TB), after_ffn=True)
                    with pe.Fori(1, TB) as t:
                        kv_tile(snap(pe, b + 1), t, snap(pe, n0 + TB + t))

            for t in range(TB):
                kv_tile(0, t, t, setup=t)
            layer_norm_rows()
            with pe.Fori(0, B - 1) as b:
                row(b, False)
            row(B - 1, True)

        @block.scalar
        def _(act):
            def A(o, i, f, **kw):
                return nc.scalar.activation(o, i, f, **kw)

            def normalise(m, s):
                act.wait_ge(ln_sc, 2 * m + 2)
                A(xln[:, s, :], xln[:, s, :], ACT.Identity, scale=xsc[:, s:s + 1],
                  bias=xnb[:, s:s + 1]).then_inc(ln_xn, 1)

            def weight_sums(q, c):
                act.wait_ge(ld[c], 16 * (2 + q))
                for i in range(4):
                    j = 4 * c + i
                    A(ternary[q][:, j * D:(j + 1) * D], region[c][:, i * D:(i + 1) * D], ACT.Abs,
                      accum_out=gpart[:, q, j:j + 1]).then_inc(a_gpart, 1)

            for s in range(SUB):
                normalise(0, s)
            act.wait_ge(v_scale, 1)
            for c in (1, 2, 0, 3):
                w, k = (wqkv[:, 0, :, c * D:(c + 1) * D], S_W) if c < 3 else (wo[:, 0, :, :], S_O)
                A(w, region[c].rearrange("p (k n) -> p k n", k=KD), ACT.Copy, scale=col(k)).then_inc(a_whi, 1)

            def split_high(u, h4, g, fwait=None):
                if fwait is not None and g == 0:
                    act.wait_ge(f_full, fwait)
                act.wait_ge(p_full, u + g + 1)
                A(qkT[:, 0, g, :], proj[g % 2][:, :], ACT.Copy, scale=QK_DOWN).then_inc(a_hi, 1)
                act.wait_ge(v_sql, h4 + g + 1)
                A(sqL[:, g % 2, :], proj[g % 2][:, :], ACT.Square, scale=SQ_DOWN).then_inc(a_sq, 1)

            def exp_k(n, f, s, h):
                act.wait_ge(f_free, f + 2 * s + h + 3)
                v = kp[:, s % 2, h * D:(h + 1) * D]
                A(v, v, ACT.Exp, scale=col(S_E)).then_inc(a_kp, 1)

            def exp_q(n, f, p):
                act.wait_ge(f_full, f + p + 1)
                act.wait_ge(pe_att, 8 * n + p + 1)
                A(qp[:, p % 2, :], feat[p % 2][:, :], ACT.Exp, scale=col(S_E)).then_inc(f_free, 1)

            def denominators(n, p):
                act.wait_ge(pe_att, 8 * n + p + 1 + 2)
                if p % 2 == 0:
                    act.wait_ge(g_mul, 4 * n + p // 2 + 1)
                h = 64 * (p % 2)
                A(dn[h:h + 64, (p // 2) % 2, :], attbank[p % 2][64:128, :], ACT.Copy,
                  bias=DEN_EPS).then_inc(a_dn, 1)

            def q_tile(b, t, n, u, f, first, last):
                h4 = 32 * b + 16 + 4 * t
                for g in range(0 if first else 1, KD):
                    split_high(u, h4, g, f - 2 if first else None)
                un = snap(act, u + (4 if first else 8))
                exp_q(n, f, 0)
                for p in range(PAIRS):
                    if p + 1 < PAIRS:
                        exp_q(n, f, p + 1)
                    if p == PAIRS - 1 and not last:
                        split_high(un, h4 + 4, 0)
                    denominators(n, p)

            def gelu_step(g0, i):
                act.wait_ge(pe_fc, g0 + 1)
                act.wait_ge(v_gl, g0 + 1)
                act.wait_ge(g_accg, g0 + 1)
                A(gbuf[:, i, :], feat[i][:, :], ACT.Gelu, scale=1.0 / X_UP).then_inc(a_g, 1)
                act.wait_ge(a_g, g0 + 3)
                act.wait_ge(v_accs, g0 + 1)
                A(gsq[:, i, :], gbuf[:, i, :], ACT.Square).then_inc(a_gsq, 1)

            def tanh_step(e):
                act.wait_ge(v_y, e + 1)
                act.wait_ge(v_u, e + 1)
                settle(act, a_own)
                A(th, yb[:, ds(e % 4, 1), :].rearrange("p a d -> p (a d)"), ACT.Tanh, scale=0.5).then_inc(a_th, 1)

            def results(n, last):
                act.wait_ge(o_out, 64 * n + 1)
                for s in ((2, 3, 0, 1) if last else range(SUB)):
                    act.wait_ge(pe_dn, 16 * n + 16 + 2)
                    A(yb[:, s, :], down[s][:, :], ACT.Copy).then_inc(a_yb, 1)

            def ffn_tile(n, prev, last):
                g0 = snap(act, 16 * n)
                with act.Fori(0, 2) as q:
                    for i in range(6):
                        gelu_step(g0 + 6 * q + 2 + i, i % 2)
                        if prev and i in (3, 5):
                            tanh_step(4 * n - 4 + 2 * q + i // 4)
                for i in range(2 if last else 4):
                    gelu_step(g0 + NJ - 2 + i, i % 2)
                results(n, last)

            def kv_tile(b, t, n, after_ffn=False, setup=None):
                u = snap(act, b * PU + t * 8)
                f = snap(act, b * FU + t * 8)
                if after_ffn:
                    act.wait_ge(v_gl, 16 * n + 2)
                    act.wait_ge(g_accg, 16 * n + 2)
                    act.wait_ge(v_accs, 16 * n + 2)
                    act.wait_ge(a_gsq, 16 * n)
                for g in range(KD):
                    split_high(u, 32 * b + 4 * t, g, f)
                    if not after_ffn and g == 2:
                        normalise(n + 1, 0)
                if after_ffn:
                    normalise(n + 1, 0)
                for s in range(1, SUB):
                    normalise(n + 1, s)
                if after_ffn:
                    tanh_step(4 * n - 4)
                    tanh_step(4 * n - 3)
                if setup in (0, 2):
                    weight_sums(setup // 2, 1)
                    weight_sums(setup // 2, 2)
                for s in range(SUB):
                    for h in range(2):
                        exp_k(n, f, s, h)
                    if after_ffn and s < 2:
                        tanh_step(4 * n - 2 + s)
                    if setup in (0, 2) and s < 2:
                        weight_sums(setup // 2, 3 * s)

            def row(b, last):
                n0 = snap(act, b * TB)
                n3 = snap(act, b * TB + TB - 1)
                q_tile(b, 0, n0, snap(act, b * PU + 32), snap(act, b * FU + 34), True, False)
                with act.Fori(1, TB - 1) as t:
                    q_tile(b, t, snap(act, b * TB + t), snap(act, b * PU + 28 + t * 8), snap(act, b * FU + 34 + t * 8),
                           False, False)
                t = TB - 1
                q_tile(b, t, n3, snap(act, b * PU + 28 + t * 8), snap(act, b * FU + 34 + t * 8), False, True)
                for i in range(2):
                    gelu_step(16 * n0 + i, i)
                ffn_tile(n0, False, False)
                with act.Fori(1, TB - 1) as t:
                    ffn_tile(snap(act, b * TB + t), True, False)
                ffn_tile(n3, True, True)
                if last:
                    for q in range(SUB):
                        tanh_step(16 * b + 12 + q)
                else:
                    kv_tile(snap(act, b + 1), 0, snap(act, n0 + TB), after_ffn=True)
                    with act.Fori(1, TB) as t:
                        kv_tile(snap(act, b + 1), t, snap(act, n0 + TB + t))

            for t in range(TB):
                kv_tile(0, t, t, setup=t)
            with act.Fori(0, B - 1) as b:
                row(b, False)
            row(B - 1, True)

        @block.gpsimd
        def _(pool):
            g = nc.gpsimd

            g.memset(mhalf[:, :], -0.5)
            g.memset(ones32[:, :], 1.0)
            g.memset(rfb[:, :, :], 0.0)
            g.memset(nrm[:, :, :], 0.0)
            g.memset(ones16[:, :], 1.0).then_inc(g_const, 1)

            def rsqrt_x(m):
                pool.wait_ge(ln_ve, m + 1)
                g.tensor_tensor(rstd[:, :], ve[:, :], mhalf[:, :], ALU.pow).then_inc(ln_rstd, 1)

            def split_x(m, s):
                pool.wait_ge(pe_t, 4 * m + s + 1)
                pool.wait_ge(ln_xn, 4 * m + s + 1)
                settle(pool, g_own)
                g.tensor_scalar(xhl[:, s % 2, 0, :], xln[:, s, :], 1.0, 0.0, ALU.mult, ALU.add).then_inc(ln_hi, 1)
                pool.wait_ge(ln_hi, 4 * m + s + 1)
                g.tensor_tensor(xhl[:, s % 2, 1, :], xln[:, s, :], xhl[:, s % 2, 0, :],
                                ALU.subtract).then_inc(ln_lo, 1)

            def square_high(h4, r, gg):
                pool.wait_ge(pe_ssq, r)
                pool.wait_ge(a_sq, h4 + gg + 1)
                settle(pool, g_own)
                g.tensor_scalar(sqh[:, gg, :], sqL[:, gg % 2, :], 1.0 / SQ_LIFT, 0.0, ALU.mult,
                                ALU.add).then_inc(g_sqh, 1)

            def attention_high(n, gg):
                pool.wait_ge(v_rr, 4 * n + gg + 1)
                pool.wait_ge(v_num, 8 * n + 2 * gg + 2 + 2)
                a = at32[:, gg % 2, :]
                g.tensor_tensor(a, a, dn[:, gg % 2, :], ALU.mult).then_inc(g_mul, 1)
                pool.wait_ge(g_mul, 4 * n + gg + 1 + 2)
                settle(pool, g_own)
                g.tensor_scalar(attT[:, 0, gg, :], a, 1.0, 0.0, ALU.mult, ALU.add).then_inc(g_ah, 1)

            def q_tile(b, t, n, first, last):
                h4 = 32 * b + 16 + 4 * t
                r = 8 * b + 4 + t
                for gg in range(0 if first else 1, KD):
                    square_high(h4, r, gg)
                if first:
                    pool.wait_ge(o_out, 256 * b + 1)
                    settle(pool, g_own)
                for gg in range(KD):
                    if gg == KD - 1 and not last:
                        square_high(h4 + 4, r + 1, 0)
                    attention_high(n, gg)

            def finish(e):
                pool.wait_ge(v_u, e + 1 + 1)
                settle(pool, g_own)
                y = yb[:, ds(e % 4, 1), :].rearrange("p a d -> p (a d)")
                g.tensor_tensor(y, y, S[:, ds((e % 16) * D, D)], ALU.mult).then_inc(g_us, 1)
                pool.wait_ge(xr_in, 16 * e + 16 + 1)
                pool.wait_ge(g_us, e + 1)
                settle(pool, g_own)
                xr = xres[:, ds(e % 2, 1), :].rearrange("p a d -> p (a d)")
                g.tensor_tensor(y, y, xr, ALU.add).then_inc(g_o, 1)

            def sum_step(g0, i):
                pool.wait_ge(a_g, g0 + 3)
                pool.wait_ge(g_accg, g0 + 2)
                g.tensor_tensor(accg, accg, gbuf[:, i, :], ALU.add).then_inc(g_accg, 1)

            def first_sum(n, g0):
                pool.wait_ge(a_g, g0 + 3)
                pool.wait_ge(v_apl, 2 * n + 1)
                settle(pool, g_own)
                g.tensor_scalar(accg, gbuf[:, 0, :], 1.0, 0.0, ALU.mult, ALU.add).then_inc(g_accg, 1)

            def ffn_root(n):
                pool.wait_ge(v_s5, n + 1)
                g.tensor_tensor(frs[:, :], fv[:, :], mhalf[:, :], ALU.pow).then_inc(g_rs, 1)

            def ffn_tile(n, prev):
                g0 = snap(pool, 16 * n)
                first_sum(n, g0)
                sum_step(g0 + 1, 1)
                if prev:
                    ffn_root(n - 1)
                with pool.Fori(0, 2) as q:
                    for i in range(6):
                        sum_step(g0 + 6 * q + 2 + i, i % 2)
                        if prev and i in (3, 5):
                            finish(4 * n - 4 + 2 * q + i // 4)
                for i in range(2):
                    sum_step(g0 + NJ - 2 + i, i)

            pool.wait_ge(g_const, 1)
            rsqrt_x(0)
            for s in range(SUB):
                if s == SUB - 1:
                    pool.wait_ge(v_max, 6)
                    g.partition_all_reduce(gm[:, :], mx[:, :], P, ABSMAX).then_inc(g_max, 1)
                split_x(0, s)

            def kv_tile(b, t, n, after_ffn=False, setup=None):
                h4, r = 32 * b + 4 * t, 8 * b + t
                rsqrt_x(n + 1)
                if after_ffn:
                    ffn_root(n - 1)
                    pool.wait_ge(pe_st, n + 1)
                    settle(pool, g_own)
                for gg in range(KD):
                    square_high(h4, r, gg)
                for s in range(SUB):
                    split_x(n + 1, s)
                    if after_ffn and s:
                        finish(4 * n - 4 + s - 1)
                if after_ffn:
                    finish(4 * n - 1)

            def row(b, last):
                n0 = snap(pool, b * TB)
                n3 = snap(pool, b * TB + TB - 1)
                q_tile(b, 0, n0, True, False)
                with pool.Fori(1, TB - 1) as t:
                    q_tile(b, t, snap(pool, b * TB + t), False, False)
                q_tile(b, TB - 1, n3, False, True)
                ffn_tile(n0, False)
                with pool.Fori(1, TB) as t:
                    ffn_tile(snap(pool, b * TB + t), True)
                if last:
                    ffn_root(n3)
                    for q in range(SUB - 1):
                        finish(16 * b + 12 + q)
                    e = 16 * b + 15
                    pool.wait_ge(v_us, 1)
                    pool.wait_ge(xr_in, 16 * e + 16 + 1)
                    g.tensor_tensor(yb[:, SUB - 1, :], yb[:, SUB - 1, :], xres[:, e % 2, :], ALU.add).then_inc(g_o, 1)
                else:
                    kv_tile(snap(pool, b + 1), 0, snap(pool, n0 + TB), after_ffn=True)
                    with pool.Fori(1, TB) as t:
                        kv_tile(snap(pool, b + 1), t, snap(pool, n0 + TB + t))

            for t in range(TB):
                kv_tile(0, t, t, setup=t)
            pool.wait_ge(v_tern, 8)
            with pool.Fori(0, B - 1) as b:
                row(b, False)
            row(B - 1, True)

        @block.vector
        def _(dve):
            v = nc.vector
            steps = [0]

            def then(ins):
                steps[0] += 1
                ins.then_inc(v_set, 1)
                dve.wait_ge(v_set, steps[0])

            def low_weights(i):
                c = (1, 2, 0, 3)[i]
                dve.wait_ge(a_whi, i + 1)
                w, k = (wqkv[:, :, :, c * D:(c + 1) * D], S_W) if c < 3 else (wo[:, :, :, :], S_O)
                v.scalar_tensor_tensor(w[:, 1, :, :], region[c].rearrange("p (k n) -> p k n", k=KD), col(k),
                                       w[:, 0, :, :], ALU.mult, ALU.subtract).then_inc(v_wlo, 1)

            def ln_parts():
                then(v.tensor_copy(lnr[:, 0, :], wn[:, :]))
                then(v.tensor_copy(lnr[:, 1, :], lnwb[:, 1, :]))
                for part in range(3):
                    for q in range(2):
                        then(v.tensor_copy(lnp[:, :, 3 * q + part], lnr[:, q, :]))
                        if part < 2:
                            then(v.tensor_tensor(lnr[:, q, :], lnr[:, q, :], lnp[:, :, 3 * q + part], ALU.subtract))

            def threshold(q):
                dve.wait_ge(pe_gsum, q + 1)
                t, nt = thr[:, q:q + 1], nthr[:, q:q + 1]
                then(v.tensor_scalar(t, small[:, 80 + q:81 + q], 1.0 / (HID * D), GAMMA_EPS, ALU.mult, ALU.add))
                then(v.tensor_scalar(t, t, 0.5, None, ALU.mult))
                v.tensor_scalar(nt, t, -1.0, None, ALU.mult).then_inc(v_thr, 1)

            def make_negative(q, c):
                dve.wait_ge(v_thr, q + 1)
                v.tensor_scalar(ternary[q][:, c * RG:(c + 1) * RG], region[c], nthr[:, q:q + 1], None,
                                ALU.is_lt).then_inc(v_neg, 1)

            def make_ternary(q, c):
                dve.wait_ge(v_neg, 4 * q + c + 1)
                w = ternary[q][:, c * RG:(c + 1) * RG]
                v.scalar_tensor_tensor(w, region[c], thr[:, q:q + 1], w, ALU.is_gt, ALU.subtract).then_inc(v_tern, 1)

            def layer_norm_rows():
                dve.wait_ge(pe_ab, 1)
                v.tensor_copy(ab6, small[0:6, :]).then_inc(v_ab, 1)
                for h, dst in enumerate((A_bc, B_bc)):
                    dve.wait_ge(pe_abc, h + 1)
                    v.tensor_copy(dst[:, :], small[:, :]).then_inc(v_abc, 1)

            def x_stats(m):
                dve.wait_ge(x_in, 16 * m + 16)
                for s in range(SUB):
                    v.bn_stats(bst[:, s, :], xln[:, s, :]).then_inc(ln_st, 1)
                for s in range(SUB):
                    dve.wait_ge(ln_st, 4 * m + s + 1)
                    settle(dve, v_own)
                    v.bn_aggr(mv[:, s, :], bst[:, s, :]).then_inc(ln_mv, 1)
                dve.wait_ge(ln_mv, 4 * m + 4)
                v.tensor_scalar(ve[:, :], mv[:, :, 1], LN_EPS, None, ALU.add).then_inc(ln_ve, 1)

            def x_scales(m):
                dve.wait_ge(ln_rstd, m + 1)
                v.tensor_scalar(xsc[:, :], rstd[:, :], X_UP, None, ALU.mult).then_inc(ln_sc, 1)
                v.scalar_tensor_tensor(xnb[:, :], mv[:, :, 0], -X_UP, rstd[:, :], ALU.mult, ALU.mult).then_inc(ln_sc, 1)

            def xT_out(m, soff, s):
                dve.wait_ge(pe_t, 4 * m + s + 1 + 2)
                dst = xT[:, ds(soff, XS)].rearrange("p (a n) -> p a n", n=TOK)[:, :, s * P:(s + 1) * P]
                v.tensor_scalar(dst, t16, 1.0, None, ALU.mult).then_inc(t_ev, 1)

            for ring, size in ((p_free, 2), (f_free, 2), (v_sql, 2), (pe_kv, 4), (pe_att, 2), (v_num, 2), (a_dn, 2),
                           (g_mul, 2), (a_g, 2), (v_gl, 2), (g_accg, 2), (v_accs, 2), (a_yb, 4), (pe_t, 2),
                           (pe_dn, 2), (g_o, 2)):
                dve.sem_inc(ring, size)
            for event in (o_out, v_u, v_apl, pe_st, v_st, pe_nt, v_nt, xr_in):
                dve.sem_inc(event, 1)
            x_stats(0)
            dve.wait_ge(ld_small, 16 * 8)
            v.tensor_copy(ident16[:, :], ident32[:, :])
            then(v.tensor_copy(heads16[:, :], heads32))
            x_scales(0)
            v.tensor_reduce(mx[:, 2:3], rfT, AX.X, ALU.max, apply_absolute_value=True).then_inc(v_max, 1)
            v.tensor_reduce(mx[:, 3:4], lnwb[:, 0, :], AX.X, ALU.max, apply_absolute_value=True).then_inc(v_max, 1)
            for i, c in enumerate((1, 2, 0, 3)):
                dve.wait_ge(ld[c], 16)
                dst = mq[:, i:i + 1] if c < 3 else mx[:, 1:2]
                ins = v.tensor_reduce(dst, region[c], AX.X, ALU.max, apply_absolute_value=True)
                if i == 0:
                    ins.then_inc(v_max, 1)
                elif i < 3:
                    then(ins)
                    xT_out(0, 0, i - 1)
                else:
                    ins.then_inc(v_max, 1)
            dve.wait_ge(v_max, 4)
            v.tensor_reduce(mx[:, 0:1], mq[:, :], AX.X, ALU.max).then_inc(v_max, 2)
            xT_out(0, 0, 2)
            dve.wait_ge(g_max, 1)
            then(v.tensor_scalar(pw[:, :].bitcast(I32), gm[:, :].bitcast(I32), 0x7F800000, None, ALU.bitwise_and))
            then(v.tensor_scalar(pw[:, :], pw[:, :], 2.0 ** -100, None, ALU.max))
            then(v.reciprocal(ip[:, :], pw[:, :]))
            v.tensor_scalar(col(S_W), ip[:, 0:1], W_UP, None, ALU.mult)
            v.tensor_scalar(col(S_O), ip[:, 1:2], W_UP, None, ALU.mult)
            v.tensor_scalar(col(S_RF), ip[:, 2:3], W_UP, None, ALU.mult)
            v.scalar_tensor_tensor(col(S_E), pw[:, 0:1], 2.0 ** -16, pw[:, 2:3], ALU.mult, ALU.mult)
            v.tensor_scalar(col(S_NK), ip[:, 2:3], 2.0 ** 19, None, ALU.mult)
            v.tensor_scalar(col(S_NS), ip[:, 2:3], -(2.0 ** 13), None, ALU.mult)
            v.scalar_tensor_tensor(col(S_CO), pw[:, 0:1], 2.0 ** -14, pw[:, 1:2], ALU.mult, ALU.mult)
            v.tensor_scalar(col(S_CR), pw[:, 3:4], 1.0 / G_UP, None, ALU.mult)
            v.tensor_scalar(wn[:, :], lnwb[:, 0, :], ip[:, 3:4], G_UP, ALU.mult, ALU.mult).then_inc(v_scale, 1)
            xT_out(0, 0, 3)
            dve.wait_ge(v_scale, 1)
            for h in range(4):
                r = slice(h * DH, (h + 1) * DH)
                ins = v.tensor_scalar(rfb[r, 0, h * NF:(h + 1) * NF], rfT[r, :], sc[r, S_RF:S_RF + 1], None, ALU.mult)
            then(ins)
            for h in range(4):
                r = slice(h * DH, (h + 1) * DH)
                v.scalar_tensor_tensor(rfb[r, 1, h * NF:(h + 1) * NF], rfT[r, :], sc[r, S_RF:S_RF + 1],
                                       rfb[r, 0, h * NF:(h + 1) * NF], ALU.mult, ALU.subtract)
            def split_low(u, h4, g):
                dve.wait_ge(a_sq, h4 + g + 1)
                v.scalar_tensor_tensor(qkT[:, 1, g, :], proj[g % 2][:, :], QK_DOWN, qkT[:, 0, g, :], ALU.mult,
                                       ALU.subtract).then_inc(p_free, 1)

            def square_low(h4, g):
                dve.wait_ge(g_sqh, h4 + g + 1)
                v.scalar_tensor_tensor(sql[:, g, :], sqh[:, g, :], -SQ_LIFT, sqL[:, g % 2, :], ALU.mult,
                                       ALU.add).then_inc(v_sql, 1)

            def sums_out(r):
                dve.wait_ge(pe_ssq, r + 1)
                v.tensor_scalar(ssb[:, :], small[:, 0:SUB * HEADS], 2.0 ** -100, None, ALU.max).then_inc(v_ssb, 1)

            def roots(r):
                done = snap(dve, ROOT_STEPS * r)

                def after(k):
                    dve.wait_ge(v_rt1, done + k)

                dve.wait_ge(v_ssb, r + 1)
                v.tensor_scalar(rt_t[:, :].bitcast(I32), ssb[:, :].bitcast(I32), 1, None,
                                ALU.logical_shift_right).then_inc(v_rt1, 1)
                after(1)
                v.tensor_scalar(rt_y[:, :].bitcast(I32), rt_t[:, :].bitcast(I32), -1, 0x5F3759DF, ALU.mult,
                                ALU.add).then_inc(v_rt1, 1)
                for k in range(3):
                    after(2 + 3 * k)
                    v.tensor_tensor(rt_t[:, :], rt_y[:, :], rt_y[:, :], ALU.mult).then_inc(v_rt1, 1)
                    after(3 + 3 * k)
                    v.scalar_tensor_tensor(rt_t[:, :], rt_t[:, :], -0.5, ssb[:, :], ALU.mult,
                                           ALU.mult).then_inc(v_rt1, 1)
                    after(4 + 3 * k)
                    v.scalar_tensor_tensor(rt_y[:, :], rt_t[:, :], 1.5, rt_y[:, :], ALU.add,
                                           ALU.mult).then_inc(v_rt1, 1)
                after(ROOT_STEPS)
                v.tensor_tensor(rsb[:, :], ssb[:, :], rt_y[:, :], ALU.mult).then_inc(v_root, 1)

            def v_out(n, u, s):
                dve.wait_ge(p_full, u + 4 + s + 1)
                dve.wait_ge(pe_kv, 4 * n + s + 1)
                v.tensor_scalar(vv[:, s, :, 0:2 * DH], proj[s % 2][:, :].rearrange("p (h c) -> p h c", h=PAIRS),
                                QK_DOWN, None, ALU.mult).then_inc(p_free, 1)

            def k_minus_norm(n, f, s, h):
                dve.wait_ge(f_full, f + 2 * s + h + 1)
                dve.wait_ge(pe_kv, 4 * n + s + 3)
                v.tensor_tensor(kp[:, s % 2, h * D:(h + 1) * D].rearrange("p (h f) -> p h f", f=NF),
                                feat[h][:, :].rearrange("p (h f) -> p h f", f=NF),
                                bcast(nk[:, s * HEADS + 8 * h:s * HEADS + 8 * h + 8], NF),
                                ALU.subtract).then_inc(f_free, 1)

            def add_kv(n, first):
                dve.wait_ge(pe_kv, 4 * n + 4 + 4)
                dve.wait_ge(v_kva, 2 * n)
                if first:
                    dve.wait_ge(v_u, 4 * n + 1)
                for j in range(2):
                    w = kvs[0:VC, j * D:(j + 1) * D]
                    if first:
                        v.tensor_copy(w, kvbank[j][0:VC, :]).then_inc(v_kva, 1)
                    else:
                        v.tensor_tensor(w, kvbank[j][0:VC, :], w, ALU.add).then_inc(v_kva, 1)

            def norm_rows(n, r):
                dve.wait_ge(v_root, r + 1)
                dve.wait_ge(pe_nt, n + 1)
                rs = rsb[:, :].rearrange("p (s h) -> p s h", s=SUB)
                v.tensor_scalar(nrm[:, :, 0:HEADS], rs, 64.0, None, ALU.mult).then_inc(v_nh, 1)
                dve.wait_ge(v_nh, n + 1)
                v.scalar_tensor_tensor(nrm[:, :, HEADS:2 * HEADS], rs, 64.0, nrm[:, :, 0:HEADS], ALU.mult,
                                       ALU.subtract).then_inc(v_nl, 1)

            def norms_out(n):
                dve.wait_ge(pe_nt, n + 1 + 1)
                v.tensor_copy(nrmT[:, :], t16[:, 0:SUB, :].rearrange("p s n -> p (s n)")).then_inc(v_nt, 1)

            def clear_blocks(b):
                dve.wait_ge(g_o, 16 * b + 2)
                v.memset(kvb[:, :, :], 0.0).then_inc(v_kvb0, 1)

            def kv_blocks(b, f, j):
                dve.wait_ge(v_kvb0, b + 1)
                dve.wait_ge(f_full, f - 2 + j + 1)
                src = feat[j][:, 0:4 * 66].rearrange("p (a c) -> p a c", c=66)
                d = kvb[:, 4 * j:4 * j + 4, :]
                for h in range(2):
                    r = slice(64 * h, 64 * h + 64)
                    v.tensor_copy(d[r, :, h * DH:(h + 1) * DH], src[r, :, h * DH:(h + 1) * DH])
                    ins = v.tensor_copy(d[r, :, 64 + h * DH:64 + (h + 1) * DH], bcast(src[r, :, 64], DH))
                ins.then_inc(f_free, 1)

            def out_rows(u, toff, s):
                dve.wait_ge(p_full, u + s + 1)
                v.scalar_tensor_tensor(S[:, ds(toff + s * D, D)], proj[s % 2][:, :], col(S_CO), bo_h[:, :], ALU.mult,
                                       ALU.add).then_inc(p_free, 1)

            def numerators(n, p):
                dve.wait_ge(pe_att, 8 * n + p + 1 + 2)
                h = 64 * (p % 2)
                v.tensor_copy(at32[h:h + 64, (p // 2) % 2, :], attbank[p % 2][0:64, :]).then_inc(v_num, 1)

            def reciprocals(n, g):
                dve.wait_ge(a_dn, 8 * n + 2 * g + 2 + 2)
                v.transpose(dT, dn[:, g % 2, :]).then_inc(v_dt, 1)
                dve.wait_ge(v_dt, 4 * n + g + 1)
                v.reciprocal(rT, dT.rearrange("p (c r) -> p c r", r=32)[:, :, 0]).then_inc(v_rt, 1)
                dve.wait_ge(v_rt, 4 * n + g + 1)
                v.transpose(dn[:, g % 2, :].rearrange("p (c r) -> p c r", r=32), bcast(rT, 32)).then_inc(v_rr, 1)

            def attention_low(n, g):
                dve.wait_ge(g_ah, 4 * n + g + 1)
                v.tensor_tensor(attT[:, 1, g, :], at32[:, g % 2, :], attT[:, 0, g, :], ALU.subtract).then_inc(v_al, 1)

            def q_tile(b, t, n, u, f, first, last):
                h4 = 32 * b + 16 + 4 * t
                r = 8 * b + 4 + t
                if first:
                    clear_blocks(b)
                for g in range(0 if first else 1, KD):
                    split_low(u, h4, g)
                    if first and g < 2:
                        kv_blocks(b, f, g)
                    if g:
                        square_low(h4, g - 1)
                    if g == 1 and not first:
                        attention_low(n - 1, 3)
                square_low(h4, KD - 1)
                toff = t * SUB * D - SUB * D
                if not first:
                    out_rows(u + 4, toff, 0)
                if not first:
                    out_rows(u + 4, toff, 1)
                sums_out(r)
                roots(r)
                norm_rows(n, r)
                if not first:
                    out_rows(u + 4, toff, 2)
                norms_out(n)
                if not first:
                    out_rows(u + 4, toff, 3)
                un = snap(dve, u + (4 if first else 8))
                for p in range(PAIRS):
                    numerators(n, p)
                    if p == PAIRS - 1 and not last:
                        split_low(un, h4 + 4, 0)
                    if p % 2:
                        reciprocals(n, p // 2)
                    if p % 2 == 0 and 0 < p < PAIRS - 2:
                        attention_low(n, p // 2 - 1)
                attention_low(n, 2)

            def ffn_step(g0, j, i, between=None):
                w = wn[:, ds(j, 1)]
                dve.wait_ge(a_g, g0 + 3)
                dve.wait_ge(pe_dn, g0 + 1)
                v.tensor_scalar(gh[:, i, :], gbuf[:, i, :], w, None, ALU.mult).then_inc(v_gh, 1)
                dve.wait_ge(v_gh, g0 + 1)
                v.scalar_tensor_tensor(gl[:, i, :], gbuf[:, i, :], w, gh[:, i, :], ALU.mult,
                                       ALU.subtract).then_inc(v_gl, 1)
                if between is not None:
                    between()
                    dve.wait_ge(a_gsq, g0 + 1)
                    v.tensor_scalar(accs, gsq[:, i, :], 1.0, None, ALU.mult).then_inc(v_accs, 1)
                else:
                    dve.wait_ge(a_gsq, g0 + 1)
                    dve.wait_ge(v_accs, g0 + 2)
                    v.tensor_tensor(accs, accs, gsq[:, i, :], ALU.add).then_inc(v_accs, 1)

            def split_sums(n):
                dve.wait_ge(pe_st, n + 1)
                dve.wait_ge(g_accg, 16 * n + 16 + 2)
                v.tensor_scalar(accp[:, 0, :], accg, 1.0, None, ALU.mult).then_inc(v_aph, 1)
                dve.wait_ge(v_accs, 16 * n + 16 + 2)
                v.tensor_scalar(accp[:, 2, :], accs, SQSUM_DOWN, None, ALU.mult).then_inc(v_aph, 1)
                dve.wait_ge(v_aph, 2 * n + 1)
                v.tensor_tensor(accp[:, 1, :], accg, accp[:, 0, :], ALU.subtract).then_inc(v_apl, 1)
                dve.wait_ge(v_aph, 2 * n + 2)
                v.scalar_tensor_tensor(accp[:, 3, :], accs, SQSUM_DOWN, accp[:, 2, :], ALU.mult,
                                       ALU.subtract).then_inc(v_apl, 1)

            def ffn_stats(n):
                dve.wait_ge(pe_st, n + 1 + 1)
                q = small[:, 0:2 * SUB].rearrange("p (s q) -> p s q", q=2)
                v.tensor_scalar(nm[:, :], q[:, :, 0], -1.0 / HID, None, ALU.mult).then_inc(v_st, 1)
                v.tensor_scalar(e2[:, :], q[:, :, 1], 1.0 / (SQSUM_DOWN * HID), LN_EPS, ALU.mult,
                                ALU.add).then_inc(v_st, 1)
                dve.wait_ge(v_st, 2 * n + 2 + 1)
                v.scalar_tensor_tensor(mm[:, :], nm[:, :], -1.0, nm[:, :], ALU.mult, ALU.mult).then_inc(v_s3, 1)
                dve.wait_ge(v_s3, n + 1)
                v.tensor_tensor(mm[:, :], mm[:, :], e2[:, :], ALU.add).then_inc(v_s4, 1)
                dve.wait_ge(v_s4, n + 1)
                v.tensor_scalar(fv[:, :], mm[:, :], LN_EPS, None, ALU.max).then_inc(v_s5, 1)

            def ffn_scale(n):
                dve.wait_ge(g_rs, n + 1)
                v.tensor_scalar(fr[:, :], frs[:, :], col(S_CR), None, ALU.mult).then_inc(v_fr, 1)

            def y_rows(e, q, n=None):
                y = yb[:, ds(q, 1), :].rearrange("p a d -> p (a d)")
                dve.wait_ge(a_yb, (e + 1 if n is None else 4 * n) + 4)
                v.scalar_tensor_tensor(y, A_bc[:, :], nm[:, ds(q, 1)], y, ALU.mult, ALU.add).then_inc(v_y1, 1)
                dve.wait_ge(v_y1, e + 1)
                v.scalar_tensor_tensor(y, y, fr[:, ds(q, 1)], B_bc[:, :], ALU.mult, ALU.add).then_inc(v_y, 1)

            def silu_rows(e, q):
                y = yb[:, ds(q, 1), :].rearrange("p a d -> p (a d)")
                dve.wait_ge(a_th, e + 1)
                v.scalar_tensor_tensor(y, th, 1.0, y, ALU.add, ALU.mult).then_inc(v_u, 1)

            def ffn_tile(n, prev, stats=False, before=None):
                g0 = snap(dve, 16 * n)

                def sums_before():
                    if prev:
                        split_sums(n - 1)
                    dve.wait_ge(v_apl, 2 * n + 1)

                if before is not None:
                    before(0)
                ffn_step(g0, 0, 0, sums_before)
                if before is not None:
                    before(1)
                ffn_step(g0 + 1, 1, 1)
                if before is not None:
                    before(2)
                    before(3)
                if prev:
                    ffn_stats(n - 1)
                    ffn_scale(n - 1)
                with dve.Fori(0, 2) as q:
                    for i in range(6):
                        ffn_step(g0 + 6 * q + 2 + i, 6 * q + 2 + i, i % 2)
                        if prev:
                            r = 2 * q + i // 4
                            if i == 2:
                                dve.wait_ge(v_fr, n)
                            if i in (2, 4):
                                y_rows(4 * n - 4 + r, r)
                            if i in (3, 5):
                                silu_rows(4 * n - 4 + r, r)
                if stats:
                    x_stats(n + 2)
                for i in range(2):
                    ffn_step(g0 + NJ - 2 + i, NJ - 2 + i, i)

            def kv_tile(b, t, n, after_ffn=False, setup=None):
                u = snap(dve, b * PU + t * 8)
                f = snap(dve, b * FU + t * 8)
                r = 8 * b + t
                h4 = 32 * b + 4 * t
                soff = snap(dve, ((n + 1) % SLOTS) * XS)
                e = 4 * n - 4
                if after_ffn:
                    split_sums(n - 1)
                    dve.wait_ge(v_apl, 2 * n + 1)
                    dve.wait_ge(pe_dn, 16 * n + 2)
                    settle(dve, v_own)
                if isinstance(t, int) and t == 0:
                    v.memset(vv[:, :, :, 2 * DH], 1.0)
                if after_ffn:
                    x_scales(n + 1)
                else:
                    x_stats(n + 1)
                for g in range(KD):
                    if after_ffn and g > 1:
                        square_low(h4, g - 2)
                    split_low(u, h4, g)
                    if after_ffn:
                        if g == 0:
                            ffn_stats(n - 1)
                        if g == 1:
                            ffn_scale(n - 1)
                    else:
                        if g == 1:
                            x_scales(n + 1)
                        if g:
                            square_low(h4, g - 1)
                if after_ffn:
                    square_low(h4, KD - 2)
                square_low(h4, KD - 1)
                if setup == 0:
                    low_weights(2)
                    low_weights(3)
                v_out(n, u, 0)
                v_out(n, u, 1)
                if after_ffn:
                    dve.wait_ge(v_fr, n)
                    y_rows(e, 0, n)
                sums_out(r)
                if setup in (1, 3):
                    make_negative(setup // 2, 0)
                roots(r)
                v_out(n, u, 2)
                if after_ffn:
                    silu_rows(e, 0)
                if setup in (1, 3):
                    make_negative(setup // 2, 1)
                dve.wait_ge(v_root, r + 1)
                v.tensor_scalar(nk[:, :], rsb[:, :], col(S_NK), None, ALU.mult).then_inc(v_nk, 1)
                v_out(n, u, 3)
                if after_ffn:
                    y_rows(e + 1, 1, n)
                if setup in (1, 3):
                    make_negative(setup // 2, 2)
                dve.wait_ge(v_nk, n + 1)
                for s in range(SUB):
                    for h in range(2):
                        k_minus_norm(n, f, s, h)
                    xT_out(n + 1, soff, s)
                    if after_ffn and s < 3:
                        silu_rows(e + s + 1, s + 1)
                    if after_ffn and s < 2:
                        y_rows(e + s + 2, s + 2, n)
                    if setup in (0, 2) and s == 2:
                        q = setup // 2
                        dve.wait_ge(a_gpart, NJ * (q + 1))
                        v.tensor_reduce(gsum[:, q:q + 1], gpart[:, q, :], AX.X, ALU.add).then_inc(v_gsum, 1)
                    if setup in (1, 3):
                        if s == 0:
                            make_negative(setup // 2, 3)
                        make_ternary(setup // 2, s)
                if setup == 0:
                    ln_parts()
                if setup in (0, 2):
                    threshold(setup // 2)
                add_kv(n, isinstance(t, int) and t == 0)

            def row(b, last):
                n0 = snap(dve, b * TB)
                n3 = snap(dve, b * TB + TB - 1)
                q_tile(b, 0, n0, snap(dve, b * PU + 32), snap(dve, b * FU + 34), True, False)
                with dve.Fori(1, TB - 1) as t:
                    q_tile(b, t, snap(dve, b * TB + t), snap(dve, b * PU + 28 + t * 8), snap(dve, b * FU + 34 + t * 8),
                           False, False)
                t = TB - 1
                q_tile(b, t, n3, snap(dve, b * PU + 28 + t * 8), snap(dve, b * FU + 34 + t * 8), False, True)
                attention_low(n3, 3)
                ffn_tile(n0, False, before=lambda s: out_rows(snap(dve, b * PU + 60), 3 * SUB * D, s))
                with dve.Fori(1, TB - 1) as t:
                    ffn_tile(snap(dve, b * TB + t), True)
                ffn_tile(n3, True, stats=not last)
                if last:
                    split_sums(n3)
                    ffn_stats(n3)
                    ffn_scale(n3)
                    dve.wait_ge(v_fr, n3 + 1)
                    y_rows(16 * b + 12, 0, n3 + 1)
                    for q in range(SUB):
                        if q + 1 < SUB:
                            y_rows(16 * b + 12 + q + 1, q + 1, n3 + 1)
                        silu_rows(16 * b + 12 + q, q)
                    y = yb[:, SUB - 1, :]
                    dve.wait_ge(v_u, 16 * b + 16 + 1)
                    v.tensor_tensor(y, y, S[:, (TB * SUB - 1) * D:], ALU.mult).then_inc(v_us, 1)
                else:
                    kv_tile(snap(dve, b + 1), 0, snap(dve, n0 + TB), after_ffn=True)
                    with dve.Fori(1, TB) as t:
                        kv_tile(snap(dve, b + 1), t, snap(dve, n0 + TB + t))

            low_weights(0)
            low_weights(1)
            dve.wait_ge(ld_rest, 48)
            v.tensor_scalar(nsel[:, :, :], sel32[:, :, :], col(S_NS), None, ALU.mult)
            then(v.tensor_scalar(bo_h[:, :], bo_h[:, :], 0.5, None, ALU.mult))
            for t in range(TB):
                kv_tile(0, t, t, setup=t)
            layer_norm_rows()
            with dve.Fori(0, B - 1) as b:
                row(b, False)
            row(B - 1, True)


def bcast(ap, n):
    return ap.unsqueeze(len(ap.shape)).broadcast_to([*ap.shape, n])


_INS = ["L0_attn_x", "L0_attn_w_qkv", "L0_attn_w_out", "L0_attn_b_out", "L0_attn_random_features", "L0_ffn_W_fc",
        "L0_ffn_ln_w", "L0_ffn_ln_b", "L0_ffn_W_proj"]


def kernel(**inputs):
    import numpy as _np
    import concourse.bacc as _bacc
    from concourse import mybir as _mybir
    from concourse.bass_utils import run_bass_kernel_spmd as _run

    nc = _bacc.Bacc("TRN2", target_bir_lowering=False, num_devices=1)
    arrays, args = {}, []
    for name in _INS:
        a = _np.asarray(inputs[name])
        if a.ndim == 2:
            a = a.T
        elif name.startswith("L0_ffn_ln"):
            a = a.reshape(NJ, P).T
        arrays[f"in_{name}"] = _np.ascontiguousarray(a)
    arrays.update(setup_constants())
    for name, a in arrays.items():
        args.append(nc.dram_tensor(name, a.shape, _mybir.dt.from_np(a.dtype), kind="ExternalInput").ap())
    args.append(nc.dram_tensor("out_0", (B, SEQ, D), F32, kind="ExternalOutput").ap())
    build_program(nc, *args)
    r = _run(nc, [arrays], core_ids=[0])
    return r.results[0]["out_0"]
```
